# Optimizing a Trainium2 kernel written in Bass

```python
import numpy as np
import jax
import jax.numpy as jnp

def _softmax(x, axis=-1):
    return jax.nn.softmax(x, axis=axis)

def _gelu(x):
    return jax.nn.gelu(x, approximate=True)

def _silu(x):
    return jax.nn.silu(x)

def _sigmoid(x):
    return jax.nn.sigmoid(x)

def _layernorm(x, axis=-1, eps=1e-05):
    m = jnp.mean(x, axis=axis, keepdims=True)
    v = jnp.var(x, axis=axis, keepdims=True)
    return (x - m) / jnp.sqrt(v + eps)

def _scatter_add(tgt, idx, src, axis=0):
    return tgt.at[idx].add(src)

def _segment_sum(src, seg, n):
    return jax.ops.segment_sum(src, seg, n)
kernel_name = 'mk_adaln_d2_jaxref_r8_aff12f'

def setup_inputs(seed: int=0):
    np.random.seed(seed)
    _w = jnp.asarray

    def _L0_attn_setup():
        import jax, jax.numpy as jnp
        import numpy as np
        HIDDEN = 512
        N_HEADS = 32
        KV_HEADS = 8
        HEAD_DIM = 128
        LOW_RANK = 64
        TOP_K_ROPE = 32
        ROPE_THETA = 10000.0
        B, S = (2, 256)
        GROUPS = N_HEADS // KV_HEADS
        _half = HEAD_DIM // 2
        _m = np.ones(_half, dtype=bool)
        _m[:TOP_K_ROPE] = False
        _m = np.concatenate([_m, _m])
        NOPE_MASK = np.tile(_m, KV_HEADS)
        ROPE_IDX = jnp.asarray(np.where(~NOPE_MASK)[0])
        NOPE_IDX = jnp.asarray(np.where(NOPE_MASK)[0])
        R_DIM = int((~NOPE_MASK).sum())
        C_DIM = LOW_RANK * KV_HEADS

        def _rope_tables(seq_len, dtype):
            inv_freq = 1.0 / ROPE_THETA ** (np.arange(0, HEAD_DIM, 2, dtype=np.float32) / HEAD_DIM)
            pos = np.arange(seq_len, dtype=np.float32)
            freqs = np.outer(pos, inv_freq)
            emb = np.concatenate([freqs, freqs], axis=-1)
            return (jnp.asarray(np.cos(emb), dtype), jnp.asarray(np.sin(emb), dtype))

        def _rotate_half(x):
            x1, x2 = (x[..., :HEAD_DIM // 2], x[..., HEAD_DIM // 2:])
            return jnp.concatenate([-x2, x1], axis=-1)
        key = jax.random.key(seed)
        ks = jax.random.split(key, 7)
        s = 0.02
        return {'hidden_states': jax.random.normal(ks[0], (B, S, HIDDEN), jnp.float32), 'Wq': jax.random.normal(ks[1], (N_HEADS * HEAD_DIM, HIDDEN), jnp.float32) * s, 'Wkr': jax.random.normal(ks[2], (R_DIM, HIDDEN), jnp.float32) * s, 'Wdk': jax.random.normal(ks[3], (C_DIM, HIDDEN), jnp.float32) * s, 'Wupk': jax.random.normal(ks[4], (KV_HEADS * HEAD_DIM - R_DIM, C_DIM), jnp.float32) * s, 'Wupv': jax.random.normal(ks[5], (KV_HEADS * HEAD_DIM, C_DIM), jnp.float32) * s, 'Wo': jax.random.normal(ks[6], (HIDDEN, N_HEADS * HEAD_DIM), jnp.float32) * s}
    _L0_attn_in = _L0_attn_setup()

    def _L0_ffn_setup():
        import jax, jax.numpy as jnp
        import numpy as np
        LORA_SCALE = 16.0 / jnp.sqrt(16.0)
        TOP_K = 2
        key = jax.random.key(seed)
        k1, k2, k3, k4 = jax.random.split(key, 4)
        B_, S, D, O, E, R = (4, 256, 512, 512, 4, 16)
        x = jax.random.normal(k1, (B_, S, D), dtype=jnp.float32)
        router_w = jax.random.normal(k2, (E, D), dtype=jnp.float32) * 0.02
        A = jax.random.normal(k3, (E, R, D), dtype=jnp.float32) * 0.02
        B = jax.random.normal(k4, (O,), dtype=jnp.float32)
        B = jax.random.normal(k4, (E, O, R), dtype=jnp.float32) * 0.02
        return {'x': x, 'router_w': router_w, 'A': A, 'B': B}
    _L0_ffn_in = _L0_ffn_setup()
    _L0_c = _w((lambda *s: np.random.randn(*s).astype(np.float32) * 0.05)(8, 512))
    _L0_wmod = _w((lambda *s: np.random.randn(*s).astype(np.float32) * 0.05)(512, 6 * 512) * 512 ** (-0.5))

    def _L1_attn_setup():
        import jax, jax.numpy as jnp
        import numpy as np
        B, S, D = (2, 256, 512)
        H = 32
        HD = D // H
        THETA = 10000.0

        def _rope_cos_sin(seq_len, head_dim, theta=THETA):
            inv = 1.0 / theta ** (np.arange(0, head_dim, 2)[:head_dim // 2].astype(np.float32) / head_dim)
            t = np.arange(seq_len)
            f = np.outer(t, inv).astype(np.float32)
            return (jnp.asarray(np.cos(f)), jnp.asarray(np.sin(f)))

        def _apply_rotary(x, cos, sin):
            xr = x.astype(jnp.float32).reshape(*x.shape[:-1], HD // 2, 2)
            x0, x1 = (xr[..., 0], xr[..., 1])
            c = cos[None, :, None, :]
            s = sin[None, :, None, :]
            o0 = x0 * c - x1 * s
            o1 = x0 * s + x1 * c
            return jnp.stack((o0, o1), axis=-1).reshape(*x.shape[:-1], HD)
        key = jax.random.key(seed)
        ks = jax.random.split(key, 5)
        std = 0.02
        return {'x': jax.random.normal(ks[0], (B, S, D), dtype=jnp.float32), 'wq': jax.random.normal(ks[1], (D, D), dtype=jnp.float32) * std, 'wk': jax.random.normal(ks[2], (D, D), dtype=jnp.float32) * std, 'wv': jax.random.normal(ks[3], (D, D), dtype=jnp.float32) * std, 'wo': jax.random.normal(ks[4], (D, D), dtype=jnp.float32) * std}
    _L1_attn_in = _L1_attn_setup()

    def _L1_ffn_setup():
        import jax, jax.numpy as jnp
        import numpy as np
        SCALING = 32.0 / 16.0
        key = jax.random.key(seed)
        ks = jax.random.split(key, 7)
        B, T, D, O, R, E = (4, 256, 512, 512, 16, 8)
        x = jax.random.normal(ks[0], (B, T, D), dtype=jnp.float32)
        base_W = jax.random.normal(ks[1], (O, D), dtype=jnp.float32) * D ** (-0.5)
        base_b = jax.random.normal(ks[2], (O,), dtype=jnp.float32) * 0.01
        router_W = jax.random.normal(ks[3], (2 * E - 1, D), dtype=jnp.float32) * D ** (-0.5)
        router_b = jax.random.normal(ks[4], (2 * E - 1,), dtype=jnp.float32) * 0.01
        A = jax.random.normal(ks[5], (E, R, D), dtype=jnp.float32) * D ** (-0.5)
        Bm = jax.random.normal(ks[6], (E, O, R), dtype=jnp.float32) * R ** (-0.5)
        assigned_idx = 0
        others = [i for i in range(E) if i != assigned_idx]
        expert_map = jnp.array([assigned_idx] * E + others, dtype=jnp.int32)
        return {'x': x, 'base_W': base_W, 'base_b': base_b, 'router_W': router_W, 'router_b': router_b, 'A': A, 'B': Bm, 'expert_map': expert_map}
    _L1_ffn_in = _L1_ffn_setup()
    _L1_c = _w((lambda *s: np.random.randn(*s).astype(np.float32) * 0.05)(8, 512))
    _L1_wmod = _w((lambda *s: np.random.randn(*s).astype(np.float32) * 0.05)(512, 6 * 512) * 512 ** (-0.5))
    _d = {'L0_attn_hidden_states': _L0_attn_in['hidden_states'], 'L0_attn_Wq': _L0_attn_in['Wq'], 'L0_attn_Wkr': _L0_attn_in['Wkr'], 'L0_attn_Wdk': _L0_attn_in['Wdk'], 'L0_attn_Wupk': _L0_attn_in['Wupk'], 'L0_attn_Wupv': _L0_attn_in['Wupv'], 'L0_attn_Wo': _L0_attn_in['Wo'], 'L0_ffn_router_w': _L0_ffn_in['router_w'], 'L0_ffn_A': _L0_ffn_in['A'], 'L0_ffn_B': _L0_ffn_in['B'], 'L0_c': _L0_c, 'L0_wmod': _L0_wmod, 'L1_attn_wq': _L1_attn_in['wq'], 'L1_attn_wk': _L1_attn_in['wk'], 'L1_attn_wv': _L1_attn_in['wv'], 'L1_attn_wo': _L1_attn_in['wo'], 'L1_ffn_base_W': _L1_ffn_in['base_W'], 'L1_ffn_base_b': _L1_ffn_in['base_b'], 'L1_ffn_router_W': _L1_ffn_in['router_W'], 'L1_ffn_router_b': _L1_ffn_in['router_b'], 'L1_ffn_A': _L1_ffn_in['A'], 'L1_ffn_B': _L1_ffn_in['B'], 'L1_ffn_expert_map': _L1_ffn_in['expert_map'], 'L1_c': _L1_c, 'L1_wmod': _L1_wmod}
    _x0 = _d['L0_attn_hidden_states']
    _d['L0_attn_hidden_states'] = jax.random.normal(jax.random.fold_in(jax.random.key(seed), 1), (8, 256, 512), dtype=_x0.dtype)
    del _x0
    return _d

def reference(L0_attn_hidden_states, L0_attn_Wq, L0_attn_Wkr, L0_attn_Wdk, L0_attn_Wupk, L0_attn_Wupv, L0_attn_Wo, L0_ffn_router_w, L0_ffn_A, L0_ffn_B, L0_c, L0_wmod, L1_attn_wq, L1_attn_wk, L1_attn_wv, L1_attn_wo, L1_ffn_base_W, L1_ffn_base_b, L1_ffn_router_W, L1_ffn_router_b, L1_ffn_A, L1_ffn_B, L1_ffn_expert_map, L1_c, L1_wmod):

    def _L0_attn_ref(hidden_states, Wq, Wkr, Wdk, Wupk, Wupv, Wo):
        import jax, jax.numpy as jnp
        import numpy as np
        HIDDEN = 512
        N_HEADS = 32
        KV_HEADS = 8
        HEAD_DIM = 128
        LOW_RANK = 64
        TOP_K_ROPE = 32
        ROPE_THETA = 10000.0
        B, S = (2, 256)
        GROUPS = N_HEADS // KV_HEADS
        _half = HEAD_DIM // 2
        _m = np.ones(_half, dtype=bool)
        _m[:TOP_K_ROPE] = False
        _m = np.concatenate([_m, _m])
        NOPE_MASK = np.tile(_m, KV_HEADS)
        ROPE_IDX = jnp.asarray(np.where(~NOPE_MASK)[0])
        NOPE_IDX = jnp.asarray(np.where(NOPE_MASK)[0])
        R_DIM = int((~NOPE_MASK).sum())
        C_DIM = LOW_RANK * KV_HEADS

        def _rope_tables(seq_len, dtype):
            inv_freq = 1.0 / ROPE_THETA ** (np.arange(0, HEAD_DIM, 2, dtype=np.float32) / HEAD_DIM)
            pos = np.arange(seq_len, dtype=np.float32)
            freqs = np.outer(pos, inv_freq)
            emb = np.concatenate([freqs, freqs], axis=-1)
            return (jnp.asarray(np.cos(emb), dtype), jnp.asarray(np.sin(emb), dtype))

        def _rotate_half(x):
            x1, x2 = (x[..., :HEAD_DIM // 2], x[..., HEAD_DIM // 2:])
            return jnp.concatenate([-x2, x1], axis=-1)
        bsz, q_len, _ = hidden_states.shape
        dt = hidden_states.dtype
        q = (hidden_states @ Wq.T).reshape(bsz, q_len, N_HEADS, HEAD_DIM).transpose(0, 2, 1, 3)
        k_r0 = hidden_states @ Wkr.T
        key_flat = jnp.zeros((bsz, q_len, KV_HEADS * HEAD_DIM), dt).at[..., ROPE_IDX].set(k_r0)
        k = key_flat.reshape(bsz, q_len, KV_HEADS, HEAD_DIM).transpose(0, 2, 1, 3)
        cos, sin = _rope_tables(q_len, dt)
        cos, sin = (cos[None, None], sin[None, None])
        q = q * cos + _rotate_half(q) * sin
        k = k * cos + _rotate_half(k) * sin
        k_r = k.transpose(0, 2, 1, 3).reshape(bsz, q_len, KV_HEADS * HEAD_DIM)[..., ROPE_IDX]
        c_kv = hidden_states @ Wdk.T
        k_c = c_kv @ Wupk.T
        v = (c_kv @ Wupv.T).reshape(bsz, q_len, KV_HEADS, HEAD_DIM).transpose(0, 2, 1, 3)
        key_full = jnp.zeros((bsz, q_len, KV_HEADS * HEAD_DIM), dt).at[..., NOPE_IDX].set(k_c).at[..., ROPE_IDX].set(k_r)
        k = key_full.reshape(bsz, q_len, KV_HEADS, HEAD_DIM).transpose(0, 2, 1, 3)
        k = jnp.repeat(k, GROUPS, axis=1)
        v = jnp.repeat(v, GROUPS, axis=1)
        scale = 1.0 / jnp.sqrt(jnp.asarray(HEAD_DIM, dt))
        scores = jnp.einsum('bhqd,bhkd->bhqk', q, k) * scale
        causal = jnp.tril(jnp.ones((q_len, q_len), bool))
        scores = jnp.where(causal[None, None], scores, jnp.asarray(-1000000000.0, dt))
        attn = jax.nn.softmax(scores, axis=-1)
        out = jnp.einsum('bhqk,bhkd->bhqd', attn, v)
        out = out.transpose(0, 2, 1, 3).reshape(bsz, q_len, N_HEADS * HEAD_DIM)
        return out @ Wo.T

    def _L0_ffn_ref(x, router_w, A, B):
        import jax, jax.numpy as jnp
        import numpy as np
        LORA_SCALE = 16.0 / jnp.sqrt(16.0)
        TOP_K = 2
        D = x.shape[-1]
        flat = x.reshape(-1, D)
        logits = flat @ router_w.T
        topk_vals, topk_idx = jax.lax.top_k(logits, TOP_K)
        sparse = jnp.full_like(logits, -jnp.inf)
        rows = jnp.arange(logits.shape[0])[:, None]
        sparse = sparse.at[rows, topk_idx].set(topk_vals)
        gates = jax.nn.softmax(sparse, axis=-1)
        mid = jnp.einsum('tf,erf->ter', flat, A)
        all_deltas = jnp.einsum('ter,eor->teo', mid, B) * LORA_SCALE
        delta = jnp.einsum('te,teo->to', gates, all_deltas)
        return delta.reshape(*x.shape[:-1], -1)

    def _L1_attn_ref(x, wq, wk, wv, wo):
        import jax, jax.numpy as jnp
        import numpy as np
        B, S, D = (2, 256, 512)
        H = 32
        HD = D // H
        THETA = 10000.0

        def _rope_cos_sin(seq_len, head_dim, theta=THETA):
            inv = 1.0 / theta ** (np.arange(0, head_dim, 2)[:head_dim // 2].astype(np.float32) / head_dim)
            t = np.arange(seq_len)
            f = np.outer(t, inv).astype(np.float32)
            return (jnp.asarray(np.cos(f)), jnp.asarray(np.sin(f)))

        def _apply_rotary(x, cos, sin):
            xr = x.astype(jnp.float32).reshape(*x.shape[:-1], HD // 2, 2)
            x0, x1 = (xr[..., 0], xr[..., 1])
            c = cos[None, :, None, :]
            s = sin[None, :, None, :]
            o0 = x0 * c - x1 * s
            o1 = x0 * s + x1 * c
            return jnp.stack((o0, o1), axis=-1).reshape(*x.shape[:-1], HD)
        b, s, d = x.shape
        q = (x @ wq).reshape(b, s, H, HD)
        k = (x @ wk).reshape(b, s, H, HD)
        v = (x @ wv).reshape(b, s, H, HD)
        cos, sin = _rope_cos_sin(s, HD)
        q = _apply_rotary(q, cos, sin)
        k = _apply_rotary(k, cos, sin)
        scale = 1.0 / jnp.sqrt(jnp.float32(HD))
        scores = jnp.einsum('bqhd,bkhd->bhqk', q, k) * scale
        causal = jnp.tril(jnp.ones((s, s), dtype=bool))
        scores = jnp.where(causal[None, None], scores, jnp.finfo(scores.dtype).min)
        probs = jax.nn.softmax(scores, axis=-1)
        out = jnp.einsum('bhqk,bkhd->bqhd', probs, v).reshape(b, s, d)
        return out @ wo

    def _L1_ffn_ref(x, base_W, base_b, router_W, router_b, A, B, expert_map):
        import jax, jax.numpy as jnp
        import numpy as np
        SCALING = 32.0 / 16.0
        E = A.shape[0]
        base_out = jnp.einsum('btd,od->bto', x, base_W) + base_b
        logits = jnp.einsum('btd,nd->btn', x, router_W) + router_b
        probs = jax.nn.softmax(logits, axis=-1)
        topk_p, topk_i = jax.lax.top_k(probs, E)
        mapped = expert_map[topk_i]
        onehot = (mapped[..., None] == jnp.arange(E)).astype(x.dtype)
        w = jnp.einsum('btk,btke->bte', topk_p, onehot)
        h = jnp.einsum('btd,erd->bter', x, A)
        lora = jnp.einsum('bter,eor->bto', h * w[..., None], B) * SCALING
        return base_out + lora
    x = L0_attn_hidden_states
    mod = (_silu(L0_c) @ L0_wmod).reshape(L0_c.shape[0], 6, 1, -1)
    sa, ca, ga, sb, cb, gb = (mod[:, 0], mod[:, 1], mod[:, 2], mod[:, 3], mod[:, 4], mod[:, 5])
    ga = (2 * (ga >= 0) - 1) * jnp.maximum(jnp.abs(ga), 0.25)
    gb = (2 * (gb >= 0) - 1) * jnp.maximum(jnp.abs(gb), 0.25)
    h = _layernorm(x, axis=-1) * (1 + ca) + sa
    x = x + ga * _L0_attn_ref(h, L0_attn_Wq, L0_attn_Wkr, L0_attn_Wdk, L0_attn_Wupk, L0_attn_Wupv, L0_attn_Wo)
    h = _layernorm(x, axis=-1) * (1 + cb) + sb
    x = x + gb * _L0_ffn_ref(h, L0_ffn_router_w, L0_ffn_A, L0_ffn_B)
    mod = (_silu(L1_c) @ L1_wmod).reshape(L1_c.shape[0], 6, 1, -1)
    sa, ca, ga, sb, cb, gb = (mod[:, 0], mod[:, 1], mod[:, 2], mod[:, 3], mod[:, 4], mod[:, 5])
    ga = (2 * (ga >= 0) - 1) * jnp.maximum(jnp.abs(ga), 0.25)
    gb = (2 * (gb >= 0) - 1) * jnp.maximum(jnp.abs(gb), 0.25)
    h = _layernorm(x, axis=-1) * (1 + ca) + sa
    x = x + ga * _L1_attn_ref(h, L1_attn_wq, L1_attn_wk, L1_attn_wv, L1_attn_wo)
    h = _layernorm(x, axis=-1) * (1 + cb) + sb
    x = x + gb * _L1_ffn_ref(h, L1_ffn_base_W, L1_ffn_base_b, L1_ffn_router_W, L1_ffn_router_b, L1_ffn_A, L1_ffn_B, L1_ffn_expert_map)
    return x

_drawn_inputs = setup_inputs


def setup_inputs(seed=0):
    import zlib

    import numpy as np

    out = dict(_drawn_inputs(seed))
    spreads = {}
    factors = {'L0_attn_Wq': 8.0,
     'L0_attn_Wkr': 8.0,
     'L0_attn_Wdk': 5.268,
     'L0_attn_Wupk': 8.0,
     'L0_attn_Wupv': 5.259,
     'L0_attn_Wo': 5.179,
     'L0_ffn_router_w': 23.064,
     'L1_attn_wq': 8.0,
     'L1_attn_wk': 8.0,
     'L1_attn_wv': 6.692,
     'L1_attn_wo': 6.706,
     'L1_ffn_base_b': 200.0,
     'L1_ffn_router_b': 200.0,
     'L0_ffn_A': 8.0,
     'L0_ffn_B': 8.0,
     'L1_ffn_router_W': 4.136}
    for name, (base, spread) in spreads.items():
        noise = np.random.default_rng([zlib.crc32(name.encode()), seed]).standard_normal(out[name].shape)
        drawn = base * np.exp(spread * noise) if base else spread * noise
        out[name] = jnp.asarray(drawn.astype(out[name].dtype))
    for name, factor in factors.items():
        out[name] = (out[name] * factor).astype(out[name].dtype)
    return out
```

```python
from contextlib import ExitStack

import numpy as np

import concourse.bass as bass
from concourse import mybir

F32 = mybir.dt.float32
F32R = mybir.dt.float32r
BF16 = mybir.dt.bfloat16
I32 = mybir.dt.int32
ALU = mybir.AluOpType
ACT = mybir.ActivationFunctionType
AX = mybir.AxisListType.X

P = 128
B, S, D = 8, 256, 512
KT = D // P
TT = S // P
NT = B * TT
EPS = 1e-5

H0, G0, HD0 = 32, 8, 128
HG = H0 // G0
SCALE0 = HD0 ** -0.5
ROPE0 = 32
HB0 = HD0 // 2
LORA0_E, LORA0_R, LORA0_SCALE = 4, 16, 4.0
NEG = -1.0e30

H1 = 32
HD1 = D // H1
SCALE1 = HD1 ** -0.5
LORA1_E, LORA1_R, LORA1_SCALE = 8, 16, 2.0
NR = 2 * LORA1_E - 1

THETA = 10000.0
GATE_MIN = 0.25


def f32(ap):
    return ap.bitcast(F32)


def pair(table):
    n, w = table.shape
    return table.rearrange("p (o s) -> p o s", o=1).broadcast_to([n, 2, w])


class Kept:
    pass


def phase_setup(nc, io, keep):
    with ExitStack() as ctx:
        def sb(name, shape, dt=F32):
            return ctx.enter_context(nc.sbuf_tensor(name, shape, dt))

        def sem(name):
            return ctx.enter_context(nc.semaphore(name))

        cond = sb("cond", [P, 2, KT, B])
        cond_e = sb("cond_e", [P, 2, KT, B])
        cond_s = sb("cond_s", [P, 2, KT, B])
        NW = 2
        wmod = [sb(f"wmod{i}", [P, KT, D]) for i in range(NW)]
        wdk = sb("wdk", [P, KT, D])
        wup = [sb(f"wup{i}", [P, KT, D]) for i in range(2)]
        wkr = sb("wkr", [P, KT, D])
        gate_raw = sb("gate_raw", [B, 4, D])
        gate_sign = sb("gate_sign", [B, 2, D])
        gate_mag = sb("gate_mag", [B, 2, D])
        ps_mod = [ctx.enter_context(nc.psum_tensor(f"ps_mod{i}", [P, D], F32)) for i in range(2)]
        ps_w = [ctx.enter_context(nc.psum_tensor(f"ps_w{i}", [P, D], F32)) for i in range(2)]

        cond_in = sem("cond_in")
        wmod_in = [sem(f"wmod_in{i}") for i in range(NW)]
        wdk_in = sem("wdk_in")
        wup_in = [sem(f"wup_in{i}") for i in range(3)]
        wkr_in = sem("wkr_in")
        cond_exp = sem("cond_exp")
        silu_step = sem("silu_step")
        mod_done = sem("mod_done")
        mod_taken = sem("mod_taken")
        prod_done = sem("prod_done")
        prod_hi = sem("prod_hi")
        prod_lo = sem("prod_lo")
        kr_split = sem("kr_split")
        kr_hi = sem("kr_hi")
        gate_step = sem("gate_step")
        gate_out_done = sem("gate_out_done")

        mods = [(l, v) for l in range(2) for v in (0, 1, 2, 3, 4, 5)]
        vec_slot = {0: 0, 1: 1, 3: 2, 4: 3}
        gate_slot = {2: 0, 5: 1}
        prods = [(m, h) for h in (None, 0, 1) for m in range(KT)]

        with nc.Block() as block:
            @block.sync
            def _(sp):
                sp.dma_start(cond[:, 0], io["c0"]).then_inc(cond_in, 16)
                sp.dma_start(cond[:, 1], io["c1"]).then_inc(cond_in, 16)
                sp.dma_start(wdk[:], io["wdk"]).then_inc(wdk_in, 16)
                sp.dma_start(wup[0][:], io["wupk"]).then_inc(wup_in[0], 16)
                sp.dma_start(wkr[:], io["wkr"]).then_inc(wkr_in, 16)
                sp.dma_start(wup[1][:], io["wupv"][:, :, 0:D]).then_inc(wup_in[1], 16)
                for n, (l, v) in enumerate(mods):
                    if n == NW:
                        sp.wait_ge(prod_done, KT)
                        sp.dma_start(wup[0][:], io["wupv"][:, :, D:2 * D]).then_inc(wup_in[2], 16)
                    if n >= NW:
                        sp.wait_ge(mod_done, n - NW + 1)
                    sp.dma_start(wmod[n % NW][:], io["wmod"][l][:, :, v * D:(v + 1) * D]).then_inc(wmod_in[n % NW], 16)
                sp.wait_ge(gate_step, 10)
                sp.dma_start(keep.gates.rearrange("n b d -> b n d"), gate_raw[:]).then_inc(gate_out_done, 16)
                sp.wait_ge(gate_out_done, 16)

            @block.scalar
            def _(act):
                act.wait_ge(cond_in, 32)
                nc.scalar.activation(cond_e[:], cond[:], ACT.Exp, scale=-1.0).then_inc(cond_exp, 1)
                for n, (m, h) in enumerate(prods):
                    act.wait_ge(prod_done, n + 1)
                    src = ps_w[n % 2][:]
                    if h is None:
                        dst = keep.wk_hi[:, m].rearrange("p (g q c) -> p g q c", g=G0, q=4)[:, :, 1:4:2, :]
                        src = src.rearrange("p (g q c) -> p g q c", g=G0, q=2)
                    else:
                        dst = keep.wv_hi[:, m, h * D:(h + 1) * D]
                    nc.scalar.activation(dst, src, ACT.Copy).then_inc(prod_hi, 1)
                act.wait_ge(wkr_in, 16)
                for m in range(KT):
                    dst = keep.wk_hi[:, m].rearrange("p (g q c) -> p g q c", g=G0, q=4)[:, :, 0:4:2, :]
                    nc.scalar.activation(dst, wkr[:, m].rearrange("p (g q c) -> p g q c", g=G0, q=2),
                                         ACT.Copy).then_inc(kr_hi, 1)

            @block.tensor
            def _(pe):
                pe.wait_ge(wdk_in, 16)
                for n, (m, h) in enumerate(prods):
                    if m == 0:
                        pe.wait_ge(wup_in[0 if h is None else 1 + h], 16)
                    if n >= 2:
                        pe.wait_ge(prod_lo, n - 1)
                        pe.wait_ge(prod_hi, n - 1)
                    rhs = wup[1 if h == 0 else 0]
                    for k in range(KT):
                        mm = nc.tensor.matmul(ps_w[n % 2][:], wdk[:, k, m * P:(m + 1) * P],
                                              rhs[:, k, :], start=(k == 0), stop=(k == KT - 1))
                    mm.then_inc(prod_done, 1)
                pe.wait_ge(silu_step, 3)
                for n, (l, v) in enumerate(mods):
                    pe.wait_ge(wmod_in[n % NW], 16 * (n // NW + 1))
                    if n >= 2:
                        pe.wait_ge(mod_taken, n - 1)
                    if v in vec_slot:
                        for m in range(KT):
                            for k in range(KT):
                                mm = nc.tensor.matmul(ps_mod[n % 2][:, m * B:(m + 1) * B], wmod[n % NW][:, k, m * P:(m + 1) * P],
                                                      cond_s[:, l, k], start=(k == 0), stop=(k == KT - 1))
                    else:
                        for k in range(KT):
                            mm = nc.tensor.matmul(ps_mod[n % 2][0:B], cond_s[:, l, k], wmod[n % NW][:, k],
                                                  start=(k == 0), stop=(k == KT - 1))
                    mm.then_inc(mod_done, 1)

            @block.vector
            def _(dve):
                dve.wait_ge(cond_exp, 1)
                nc.vector.tensor_scalar(cond_e[:], cond_e[:], 1.0, None, ALU.add).then_inc(silu_step, 1)
                dve.wait_ge(silu_step, 1)
                nc.vector.reciprocal(cond_s[:], cond_e[:]).then_inc(silu_step, 1)
                dve.wait_ge(silu_step, 2)
                nc.vector.tensor_tensor(cond_s[:], cond_s[:], cond[:], ALU.mult).then_inc(silu_step, 1)
                for n, (m, h) in enumerate(prods):
                    dve.wait_ge(prod_hi, n + 1)
                    src = ps_w[n % 2][:]
                    if h is None:
                        parts = [t[:, m].rearrange("p (g q c) -> p g q c", g=G0, q=4)[:, :, 1:4:2, :]
                                 for t in (keep.wk_hi, keep.wk_lo)]
                        src = src.rearrange("p (g q c) -> p g q c", g=G0, q=2)
                    else:
                        parts = [t[:, m, h * D:(h + 1) * D] for t in (keep.wv_hi, keep.wv_lo)]
                    nc.vector.tensor_tensor(parts[1], src, f32(parts[0]), ALU.subtract).then_inc(prod_lo, 1)
                for m in range(KT):
                    dve.wait_ge(kr_hi, m + 1)
                    parts = [t[:, m].rearrange("p (g q c) -> p g q c", g=G0, q=4)[:, :, 0:4:2, :]
                             for t in (keep.wk_hi, keep.wk_lo)]
                    nc.vector.tensor_tensor(parts[1], wkr[:, m].rearrange("p (g q c) -> p g q c", g=G0, q=2),
                                            f32(parts[0]), ALU.subtract).then_inc(kr_split, 1)
                for n, (l, v) in enumerate(mods):
                    dve.wait_ge(mod_done, n + 1)
                    if v in vec_slot:
                        i = vec_slot[v]
                        add = 1.0 if v in (1, 4) else 0.0
                        nc.vector.tensor_scalar(keep.mod[:, l, i], ps_mod[n % 2][:, 0:KT * B].rearrange("p (k b) -> p k b", b=B), add, None,
                                                ALU.add).then_inc(mod_taken, 1)
                    else:
                        nc.vector.tensor_copy(gate_raw[:, 2 * l + gate_slot[v]], ps_mod[n % 2][0:B]).then_inc(mod_taken, 1)
                dve.wait_ge(mod_taken, 12)
                for l in range(2):
                    g = gate_raw[:, 2 * l:2 * l + 2]
                    n = 5 * l
                    nc.vector.tensor_scalar(gate_sign[:], g, 0.0, 2.0, ALU.is_ge, ALU.mult).then_inc(gate_step, 1)
                    nc.vector.tensor_scalar(gate_mag[:], g, -1.0, None, ALU.mult).then_inc(gate_step, 1)
                    dve.wait_ge(gate_step, n + 2)
                    nc.vector.tensor_tensor(gate_mag[:], g, gate_mag[:], ALU.max).then_inc(gate_step, 1)
                    dve.wait_ge(gate_step, n + 3)
                    nc.vector.tensor_scalar(gate_mag[:], gate_mag[:], GATE_MIN, None, ALU.max).then_inc(gate_step, 1)
                    dve.wait_ge(gate_step, n + 4)
                    nc.vector.scalar_tensor_tensor(g, gate_sign[:], 1.0, gate_mag[:],
                                                   ALU.subtract, ALU.mult).then_inc(gate_step, 1)
                    dve.wait_ge(gate_step, n + 5)


def phase_keys(nc, io, keep):
    with ExitStack() as ctx:
        def sb(name, shape, dt=F32):
            return ctx.enter_context(nc.sbuf_tensor(name, shape, dt))

        def sem(name):
            return ctx.enter_context(nc.semaphore(name))

        x = sb("x_in", [P, TT, D])
        stats = sb("ln_stats", [P, TT, 6])
        mv = sb("ln_mv", [P, TT, 2])
        std = sb("ln_std", [P, TT])
        rstd = sb("ln_rstd", [P, TT])
        xn = sb("xn", [P, TT, D])
        ht = sb("ht", [P, KT, S])
        hs = [sb(f"hs{i}", [P, KT, S], F32R) for i in range(2)]
        cos = sb("kcos", [P, S])
        sin = sb("ksin", [P, S])
        kcos = sb("k_cos", [P, 2, S])
        kswap = sb("k_swap", [P, 2, S])
        krot = sb("k_rot", [P, 2, S])
        kp = [[sb(f"k_part{i}{n}", [P, 2, S], F32R) for n in range(2)] for i in range(2)]
        vp = [sb(f"v_part{i}", [P, TT, 2 * D], F32R) for i in range(2)]
        ps_t = ctx.enter_context(nc.psum_tensor("ps_t", [P, KT, S], F32))
        ps_k = [ctx.enter_context(nc.psum_tensor(f"ps_k{i}", [P, 2, S], F32)) for i in range(2)]
        ps_v = [ctx.enter_context(nc.psum_tensor(f"ps_v{i}", [P, D], F32)) for i in range(2)]

        rot_in = sem("rot_in")
        x_in = sem("x_in_s")
        ln_step = sem("ln_step")
        ln_sqrt = sem("ln_sqrt")
        t_done = sem("t_done")
        ht_done = sem("ht_done")
        hi_done = sem("hi_done")
        lo_done = sem("lo_done")
        kept = sem("kept")
        v_done = sem("v_done")
        v_hi = sem("v_hi")
        v_lo = sem("v_lo")
        v_out = sem("v_out")
        k_done = sem("k_done")
        k_cos = sem("k_cos_s")
        k_rot = sem("k_rot_s")
        k_hi = sem("k_hi")
        k_lo = sem("k_lo")
        k_out = [sem(f"k_out{n}") for n in range(2)]

        NP = G0 // 2
        NV = TT * 2

        with nc.Block() as block:
            @block.sync
            def _(sp):
                for s in k_out:
                    sp.sem_inc(s, 32)
                sp.dma_start(x[:], io["x"][0]).then_inc(x_in, 16)
                sp.dma_start(cos[:], io["kcos"]).then_inc(rot_in, 16)
                sp.dma_start(sin[:], io["ksin"]).then_inc(rot_in, 16)

                def stores(b):
                    sp.wait_ge(lo_done, b + 1)
                    sp.wait_ge(hi_done, b + 1)
                    sp.dma_start(f32(keep.ht_hi[:, bass.ds(b, 1)]), f32(hs[0][:].rearrange("p (o k) s -> p o k s", o=1))).then_inc(kept, 16)
                    sp.dma_start(f32(keep.ht_lo[:, bass.ds(b, 1)]), f32(hs[1][:].rearrange("p (o k) s -> p o k s", o=1))).then_inc(kept, 16)

                def store_values(b):
                    sp.wait_ge(v_lo, NV * (b + 1))
                    for i in range(2):
                        for t in range(TT):
                            sp.dma_start(keep.v_by_element[i][bass.ds(b, 1), :, t].rearrange("o p g c -> p (o g) c"),
                                         f32(vp[i][:, t].rearrange("p (g c) -> p g c", g=G0))).then_inc(v_out, 16)

                def store_keys(b):
                    for g in range(NP):
                        sp.wait_ge(k_lo, NP * b + g + 1)
                        for i in range(2):
                            sp.dma_start(keep.k_by_element[i][bass.ds(b, 1), :, 2 * g:2 * g + 2].rearrange("o p g s -> p (o g) s"),
                                         f32(kp[i][g % 2][:])).then_inc(k_out[g % 2], 16)

                stores(0)
                with sp.Fori(0, B - 1) as b:
                    sp.wait_ge(ln_step, 7 * b + 7)
                    sp.dma_start(x[:], io["x"][bass.ds(b + 1, 1)].rearrange("o p t d -> p (o t) d")).then_inc(x_in, 16)
                    store_values(b)
                    stores(b + 1)
                    store_keys(b)
                store_values(B - 1)
                store_keys(B - 1)
                sp.wait_ge(kept, 32 * B)
                sp.wait_ge(v_out, 64 * B)
                for s in k_out:
                    sp.wait_ge(s, 32 * (NP // 2 * B) + 32)

            @block.vector
            def _(dve):
                def normalize(b):
                    n = 7 * b
                    dve.wait_ge(x_in, 16 * (b + 1))
                    for t in range(TT):
                        nc.vector.bn_stats(stats[:, t], x[:, t]).then_inc(ln_step, 1)
                    dve.wait_ge(ln_step, n + 2)
                    nc.vector.memset(rstd[:], 0.0)
                    for t in range(TT):
                        nc.vector.bn_aggr(mv[:, t], stats[:, t]).then_inc(ln_step, 1)
                    dve.wait_ge(ln_sqrt, b + 1)
                    nc.vector.reciprocal(rstd[:], std[:]).then_inc(ln_step, 1)
                    dve.wait_ge(ln_step, n + 5)
                    for t in range(TT):
                        nc.vector.tensor_scalar(xn[:, t], x[:, t], mv[:, t, 0:1], rstd[:, t:t + 1],
                                                ALU.subtract, ALU.mult).then_inc(ln_step, 1)

                def split_h(b):
                    dve.wait_ge(hi_done, b + 1)
                    nc.vector.tensor_tensor(hs[1][:], ht[:], f32(hs[0][:]), ALU.subtract).then_inc(lo_done, 1)

                def values(b):
                    for n in range(NV):
                        dve.wait_ge(v_hi, NV * b + n + 1)
                        t, h = n // 2, n % 2
                        nc.vector.tensor_tensor(vp[1][:, t, h * D:(h + 1) * D], ps_v[n % 2][:],
                                                f32(vp[0][:, t, h * D:(h + 1) * D]), ALU.subtract).then_inc(v_lo, 1)

                def keys(b):
                    for g in range(NP):
                        dve.wait_ge(k_done, NP * b + g + 1)
                        src = ps_k[g % 2]
                        if g:
                            dve.wait_ge(k_rot, NP * b + g)
                        nc.vector.tensor_tensor(kcos[:], src[:], pair(cos[:]), ALU.mult)
                        nc.vector.tensor_tensor(kswap[0:HB0], src[HB0:P], pair(sin[HB0:P]), ALU.mult)
                        nc.vector.tensor_tensor(kswap[HB0:P], src[0:HB0], pair(sin[0:HB0]), ALU.mult).then_inc(k_cos, 1)
                        dve.wait_ge(k_hi, NP * b + g + 1)
                        nc.vector.tensor_tensor(kp[1][g % 2][:], krot[:], f32(kp[0][g % 2][:]), ALU.subtract).then_inc(k_lo, 1)

                normalize(0)
                split_h(0)
                dve.wait_ge(rot_in, 32)
                with dve.Fori(0, B - 1) as b:
                    dve.wait_ge(t_done, b + 1)
                    normalize(b + 1)
                    values(b)
                    dve.wait_ge(kept, 32 * (b + 1))
                    dve.wait_ge(v_done, NV * (b + 1))
                    split_h(b + 1)
                    keys(b)
                values(B - 1)
                keys(B - 1)

            @block.scalar
            def _(act):
                def roots(b):
                    act.wait_ge(ln_step, 7 * b + 4)
                    nc.scalar.activation(std[:], mv[:, :, 1], ACT.Sqrt, bias=keep.eps[:, 0:1]).then_inc(ln_sqrt, 1)

                def modulate(b):
                    act.wait_ge(t_done, b + 1)
                    for k in range(KT):
                        nc.scalar.activation(ht[:, k], ps_t[:, k], ACT.Identity,
                                             bias=keep.mod[:, 0, 0, k, bass.ds(b, 1)],
                                             scale=keep.mod[:, 0, 1, k, bass.ds(b, 1)]).then_inc(ht_done, 1)
                    act.wait_ge(ht_done, KT * (b + 1))
                    nc.scalar.activation(hs[0][:], ht[:], ACT.Copy).then_inc(hi_done, 1)

                def values(b):
                    for n in range(NV):
                        act.wait_ge(v_done, NV * b + n + 1)
                        t, h = n // 2, n % 2
                        nc.scalar.activation(vp[0][:, t, h * D:(h + 1) * D], ps_v[n % 2][:], ACT.Copy).then_inc(v_hi, 1)

                def keys(b):
                    for g in range(NP):
                        act.wait_ge(k_rot, NP * b + g + 1)
                        act.wait_ge(k_out[g % 2], 32 * (NP // 2 * b + g // 2) + 32)
                        nc.scalar.activation(kp[0][g % 2][:], krot[:], ACT.Copy).then_inc(k_hi, 1)

                roots(0)
                modulate(0)
                with act.Fori(0, B - 1) as b:
                    roots(b + 1)
                    values(b)
                    act.wait_ge(kept, 32 * (b + 1))
                    act.wait_ge(v_done, NV * (b + 1))
                    modulate(b + 1)
                    keys(b)
                    act.wait_ge(v_out, 64 * (b + 1))
                values(B - 1)
                keys(B - 1)

            @block.gpsimd
            def _(pool):
                with pool.Fori(0, B) as b:
                    for g in range(NP):
                        pool.wait_ge(k_cos, NP * b + g + 1)
                        nc.gpsimd.tensor_tensor(krot[:], kcos[:], kswap[:], ALU.add).then_inc(k_rot, 1)

            @block.tensor
            def _(pe):
                def transposes(b):
                    pe.wait_ge(ln_step, 7 * b + 7)
                    for t in range(TT):
                        for k in range(KT):
                            mm = nc.tensor.transpose(ps_t[:, k, t * P:(t + 1) * P], xn[:, t, k * P:(k + 1) * P],
                                                     keep.ident[:])
                    mm.then_inc(t_done, 1)

                def values(b):
                    pe.wait_ge(lo_done, b + 1)
                    for n in range(NV):
                        t, h = n // 2, n % 2
                        if n >= 2:
                            pe.wait_ge(v_lo, NV * b + n - 1)
                        passes = [(hs[i], w, k) for i, w in ((0, keep.wv_hi), (1, keep.wv_hi), (0, keep.wv_lo)) for k in range(KT)]
                        for j, (a, w, k) in enumerate(passes):
                            mm = nc.tensor.matmul(ps_v[n % 2][:], a[:, k, t * P:(t + 1) * P], w[:, k, h * D:(h + 1) * D],
                                                  start=(j == 0), stop=(j == len(passes) - 1))
                        mm.then_inc(v_done, 1)

                def keys(b):
                    pe.wait_ge(kept, 32 * (b + 1))
                    for g in range(NP):
                        if g >= 2:
                            pe.wait_ge(k_cos, NP * b + g - 1)
                        for e in range(2):
                            passes = [(w, r, k) for w, r in ((keep.wk_hi, keep.ht_hi), (keep.wk_lo, keep.ht_hi), (keep.wk_hi, keep.ht_lo))
                                      for k in range(KT)]
                            for j, (w, r, k) in enumerate(passes):
                                mm = nc.tensor.matmul(ps_k[g % 2][:, e], w[:, k, (2 * g + e) * P:(2 * g + e + 1) * P],
                                                      r[:, bass.ds(b, 1), k].rearrange("p o s -> p (o s)"), start=(j == 0), stop=(j == len(passes) - 1))
                        mm.then_inc(k_done, 1)

                transposes(0)
                with pe.Fori(0, B - 1) as b:
                    values(b)
                    transposes(b + 1)
                    keys(b)
                    pe.wait_ge(v_lo, NV * (b + 1))
                    pe.wait_ge(k_cos, NP * (b + 1))
                values(B - 1)
                keys(B - 1)


def phase_attention0(nc, io, keep):
    U = G0 * B
    with ExitStack() as ctx:
        def sb(name, shape, dt=F32):
            return ctx.enter_context(nc.sbuf_tensor(name, shape, dt))

        def sem(name):
            return ctx.enter_context(nc.semaphore(name))

        shared_at = -(-nc.sbuf_base // 32) * 32
        pt = [sb(f"pt{i}", [P, 3, HG * P], F32R) for i in range(2)]
        W = KT * D
        WP = W // B
        WO_LATE = 2
        wq = [sb(f"wq{i}", [P, 2 * W], F32R) for i in range(2)]
        wo = [sb(f"wo{i}", [P, 2 * W], F32R) for i in range(2)]
        wq_new = sb("wq_new", [P, WP])
        wo_new = sb("wo_new", [P, WP])
        kk = [sb(f"kk{i}", [P, S], F32R) for i in range(2)]
        vv = [sb(f"vv{i}", [P, TT, HD0], F32R) for i in range(2)]
        qrot = [sb(f"q_rot{i}", [P, 2, S]) for i in range(2)]
        qswap = [sb(f"q_swap{i}", [P, 2, S]) for i in range(2)]
        q = [sb(f"q{i}", [P, HG, S], F32R) for i in range(2)]
        prob = nc.alloc_sbuf_tensor_at("prob", [P, 3 * HG * P], F32, offset=shared_at)
        row_max = sb("row_max", [P, 2, HG])
        neg_max = sb("neg_max", [P, 2, HG])
        row_sum = sb("row_sum", [P, 2, HG])
        inv_sum = sb("inv_sum", [P, 2, HG])
        ot = [sb(f"ot{i}", [P, TT, HG * P], F32R) for i in range(2)]
        ps_q = [ctx.enter_context(nc.psum_tensor(f"ps_q{i}", [P, 2, S], F32)) for i in range(2)]
        ps_s = ctx.enter_context(nc.psum_tensor("ps_s", [P, 3, D], F32))
        ps_o = [ctx.enter_context(nc.psum_tensor(f"ps_o{i}", [P, D], F32)) for i in range(2)]
        ps_y = [ps_o[0], ctx.enter_context(nc.psum_tensor("ps_y1", [P, D], F32))]
        s0 = ps_s[:, 0].rearrange("p (h k) -> p h k", h=HG)
        s1 = ps_s[:, 1:3].rearrange("p a (h k) -> p (a h) k", h=2)
        p0 = prob[:, 0:HG * P].rearrange("p (h k) -> p h k", h=HG)
        p1 = prob[:, HG * P:].rearrange("p (h k) -> p h k", h=HG)

        wq_in = sem("wq_in")
        wq_hi = sem("wq_hi")
        wq_lo = sem("wq_lo")
        wo_in = sem("wo_in")
        wo_hi = sem("wo_hi")
        wo_lo = sem("wo_lo")
        k_in = sem("k_in")
        v_in = sem("v_in")
        q_done = sem("q_done")
        q_mul = sem("q_mul")
        q_add = sem("q_add")
        q_hi = sem("q_hi")
        q_lo = sem("q_lo")
        s_done = sem("s_done")
        smax = sem("smax")
        p_exp = sem("p_exp")
        p_rcp = sem("p_rcp")
        p0_norm = sem("p0_norm")
        p1_norm = sem("p1_norm")
        t_done = sem("pt_done")
        t_hi = sem("t_hi")
        t_lo = sem("t_lo")
        o_done = sem("o_done")
        o_hi = sem("o_hi")
        o_lo = sem("o_lo")
        y_done = sem("y_done")
        y_acc = sem("y_acc")

        PARTS = ((1, U - B, True, True), (U - B, U - B + WO_LATE, False, True), (U - B + WO_LATE, U, False, False))

        with nc.Block() as block:
            @block.sync
            def _(sp):
                def load_wq(n):
                    sp.dma_start(wq_new[:], io["wq_pieces"][bass.ds(n, 1)].rearrange("o p c -> p (o c)")).then_inc(wq_in, 16)

                def load_wo(n):
                    sp.dma_start(wo_new[:], io["wo_pieces"][bass.ds(n, 1)].rearrange("o p c -> p (o c)")).then_inc(wo_in, 16)

                def load_keys(u):
                    for i in range(2):
                        sp.dma_start(f32(kk[i][:]), keep.k[i][bass.ds(u, 1)].rearrange("o p s -> p (o s)")).then_inc(k_in, 16)

                def load_values(u):
                    for i in range(2):
                        sp.dma_start(f32(vv[i][:]), keep.v[i][bass.ds(u, 1)].rearrange("o p t c -> p (o t) c")).then_inc(v_in, 16)

                def step(v, with_wq, with_wo):
                    if with_wq:
                        sp.wait_ge(wq_lo, v + B)
                        load_wq(v + B)
                    sp.wait_ge(s_done, v)
                    load_keys(v)
                    if with_wo:
                        sp.wait_ge(wo_lo, v + B - WO_LATE + B)
                        load_wo(v + B - WO_LATE)
                    sp.wait_ge(o_done, 2 * v)
                    load_values(v)

                load_wq(0)
                load_keys(0)
                load_values(0)
                for n in range(1, B):
                    sp.wait_ge(wq_lo, n)
                    load_wq(n)
                    if n > WO_LATE:
                        if n > WO_LATE + 1:
                            sp.wait_ge(wo_lo, n - WO_LATE - 1 + B)
                        load_wo(n - WO_LATE - 1)
                sp.wait_ge(wo_lo, B - WO_LATE - 1 + B)
                load_wo(B - WO_LATE - 1)
                sp.wait_ge(wq_lo, B)
                load_wq(B)
                sp.wait_ge(wo_lo, B - WO_LATE + B)
                load_wo(B - WO_LATE)
                for first, last, with_wq, with_wo in PARTS:
                    with sp.Fori(first, last) as v:
                        step(v, with_wq, with_wo)

            def piece(w, n):
                return w[:, bass.ds((n % (2 * B)) * WP, WP)]

            @block.scalar
            def _(act):
                def split_wq(n):
                    act.wait_ge(wq_in, 16 * n + 16)
                    nc.scalar.activation(piece(wq[0], n), wq_new[:], ACT.Identity).then_inc(wq_hi, 1)

                def split_wo(n):
                    act.wait_ge(wo_in, 16 * n + 16)
                    nc.scalar.activation(piece(wo[0], n), wo_new[:], ACT.Identity).then_inc(wo_hi, 1)

                def exponentials(u):
                    act.wait_ge(smax, 3 * u + 3)
                    for t, (p, sc) in enumerate(((p0, s0), (p1, s1))):
                        for h in range(HG):
                            nc.scalar.activation(p[:, h], sc[:, h], ACT.Exp, bias=neg_max[:, t, h:h + 1], scale=SCALE0,
                                                 accum_out=row_sum[:, t, h:h + 1]).then_inc(p_exp, 1)

                def transposed(u):
                    for j in range(3):
                        act.wait_ge(t_done, 3 * u + (1 if j == 0 else 3))
                        nc.scalar.activation(pt[0][:, j], ps_s[:, j], ACT.Identity).then_inc(t_hi, 1)

                def queries(u):
                    for j in range(2):
                        act.wait_ge(q_add, 2 * u + j + 1)
                        nc.scalar.activation(q[0][:, 2 * j:2 * j + 2], qrot[j][:], ACT.Identity).then_inc(q_hi, 1)

                def output(u):
                    for j in range(TT):
                        act.wait_ge(o_done, 2 * u + j + 1)
                        nc.scalar.activation(ot[0][:, j], ps_o[j][:], ACT.Identity).then_inc(o_hi, 1)

                def step(v, with_wq, with_wo):
                    exponentials(v - 1)
                    if with_wq:
                        split_wq(v + B)
                    transposed(v - 1)
                    queries(v)
                    output(v - 1)
                    if with_wo:
                        split_wo(v + B - WO_LATE)

                for n in range(B):
                    split_wq(n)
                    if n > WO_LATE:
                        split_wo(n - WO_LATE - 1)
                queries(0)
                split_wo(B - WO_LATE - 1)
                nc.scalar.preload_act_table(ACT.Exp)
                act.wait_ge(q_done, 2)
                split_wq(B)
                split_wo(B - WO_LATE)
                for first, last, with_wq, with_wo in PARTS:
                    with act.Fori(first, last) as v:
                        step(v, with_wq, with_wo)
                exponentials(U - 1)
                transposed(U - 1)
                output(U - 1)

            @block.vector
            def _(dve):
                def rest_of_transposed(u):
                    for j in range(3):
                        dve.wait_ge(t_hi, 3 * u + j + 1)
                        nc.vector.tensor_tensor(pt[1][:, j], ps_s[:, j], f32(pt[0][:, j]), ALU.subtract).then_inc(t_lo, 1)

                def rest_of_output(u):
                    for j in range(TT):
                        dve.wait_ge(o_hi, 2 * u + j + 1)
                        nc.vector.tensor_tensor(ot[1][:, j], ps_o[j][:], f32(ot[0][:, j]), ALU.subtract).then_inc(o_lo, 1)

                def accumulate(u, j):
                    dve.wait_ge(y_done, 2 * u + j + 3)
                    a = keep.acc[:, bass.ds(((u + B) % B) * TT + j, 1)].rearrange("p o c -> p (o c)")
                    nc.vector.tensor_tensor(a, ps_y[j][:], a, ALU.add).then_inc(y_acc, 1)

                def rotate(u):
                    for j in range(2):
                        dve.wait_ge(q_done, 2 * u + j + 1)
                        src = ps_q[j]
                        nc.vector.tensor_tensor(qrot[j][:], src[:], pair(keep.qcos[:]), ALU.mult)
                        nc.vector.tensor_tensor(qswap[j][0:HB0], src[HB0:P], pair(keep.qsin[HB0:P]), ALU.mult)
                        nc.vector.tensor_tensor(qswap[j][HB0:P], src[0:HB0], pair(keep.qsin[0:HB0]), ALU.mult).then_inc(q_mul, 1)

                def maxima(u):
                    dve.wait_ge(s_done, u + 1)
                    nc.vector.tensor_reduce(row_max[:, 0], s0, AX, ALU.max).then_inc(smax, 1)
                    nc.vector.tensor_reduce(row_max[:, 1], s1, AX, ALU.max).then_inc(smax, 1)
                    dve.wait_ge(smax, 3 * u + 2)
                    nc.vector.tensor_scalar(neg_max[:], row_max[:], -SCALE0, None, ALU.mult).then_inc(smax, 1)

                def normalize(u):
                    dve.wait_ge(p_exp, 8 * u + 8)
                    nc.vector.reciprocal(inv_sum[:], row_sum[:]).then_inc(p_rcp, 1)
                    dve.wait_ge(p_rcp, u + 1)
                    inv = inv_sum[:, 1].rearrange("p (h o) -> p h o", o=1).broadcast_to([P, HG, S])
                    nc.vector.tensor_tensor(p1, p1, inv, ALU.mult).then_inc(p1_norm, 1)

                for i in range(2):
                    nc.vector.memset(f32(wo[i][:, W:2 * W]), 0.0).then_inc(wo_lo, B // 2)
                    nc.vector.memset(f32(ot[i][:]), 0.0).then_inc(o_lo, 1)
                nc.vector.memset(keep.acc[:], 0.0).then_inc(y_acc, 2)
                dve.wait_ge(y_acc, 2)
                rotate(0)
                with dve.Fori(1, U) as v:
                    maxima(v - 1)
                    accumulate(v - 2, 0)
                    normalize(v - 1)
                    rotate(v)
                    rest_of_transposed(v - 1)
                    accumulate(v - 2, 1)
                    rest_of_output(v - 1)
                maxima(U - 1)
                accumulate(U - 2, 0)
                normalize(U - 1)
                rest_of_transposed(U - 1)
                accumulate(U - 2, 1)
                rest_of_output(U - 1)
                for j in range(TT):
                    accumulate(U - 1, j)

            @block.gpsimd
            def _(pool):
                def split_wq(n):
                    pool.wait_ge(wq_hi, n + 1)
                    nc.gpsimd.tensor_tensor(piece(wq[1], n), wq_new[:], f32(piece(wq[0], n)), ALU.subtract).then_inc(wq_lo, 1)

                def split_wo(n):
                    pool.wait_ge(wo_hi, n + 1)
                    nc.gpsimd.tensor_tensor(piece(wo[1], n), wo_new[:], f32(piece(wo[0], n)), ALU.subtract).then_inc(wo_lo, 1)

                def normalize(u):
                    pool.wait_ge(p_rcp, u + 1)
                    inv = inv_sum[:, 0].rearrange("p (h o) -> p h o", o=1).broadcast_to([P, HG, P])
                    nc.gpsimd.tensor_tensor(p0, p0, inv, ALU.mult).then_inc(p0_norm, 1)

                def queries(u):
                    for j in range(2):
                        pool.wait_ge(q_mul, 2 * u + j + 1)
                        nc.gpsimd.tensor_tensor(qrot[j][:], qrot[j][:], qswap[j][:], ALU.add).then_inc(q_add, 1)
                    for j in range(2):
                        pool.wait_ge(q_hi, 2 * u + j + 1)
                        nc.gpsimd.tensor_tensor(q[1][:, 2 * j:2 * j + 2], qrot[j][:], f32(q[0][:, 2 * j:2 * j + 2]), ALU.subtract).then_inc(q_lo, 1)

                def step(v, with_wq, with_wo):
                    normalize(v - 1)
                    if with_wq:
                        split_wq(v + B)
                    queries(v)
                    if with_wo:
                        split_wo(v + B - WO_LATE)

                for n in range(B):
                    split_wq(n)
                    if n > WO_LATE:
                        split_wo(n - WO_LATE - 1)
                queries(0)
                split_wo(B - WO_LATE - 1)
                split_wq(B)
                split_wo(B - WO_LATE)
                for first, last, with_wq, with_wo in PARTS:
                    with pool.Fori(first, last) as v:
                        step(v, with_wq, with_wo)
                normalize(U - 1)

            @block.tensor
            def _(pe):
                def queries(par, u):
                    for j in range(2):
                        for e in range(2):
                            h = 2 * j + e
                            passes = [(w, r, k) for w, r in ((wq[0], keep.ht_hi), (wq[1], keep.ht_hi), (wq[0], keep.ht_lo)) for k in range(KT)]
                            for n, (w, r, k) in enumerate(passes):
                                c = par * W + k * D + h * HD0
                                mm = nc.tensor.matmul(ps_q[j][:, e], w[:, c:c + HD0],
                                                      r[:, bass.ds(u % B, 1), k].rearrange("p o s -> p (o s)"),
                                                      start=(n == 0), stop=(n == len(passes) - 1))
                        mm.then_inc(q_done, 1)

                def values(u):
                    pe.wait_ge(v_in, 32 * u + 32)
                    for j, blocks in ((0, ((0, 0),)), (1, ((0, 1), (1, 2)))):
                        pe.wait_ge(t_lo, 3 * u + 1 + 2 * j)
                        if j == 0:
                            pe.wait_ge(y_acc, 2 * u + 3)
                        passes = [(a, p, k, n) for a, p in split_passes(vv, pt) for k, n in blocks]
                        for n, (a, p, k, blk) in enumerate(passes):
                            mm = nc.tensor.matmul(ps_o[j][:], a[:, k], p[:, blk], start=(n == 0), stop=(n == len(passes) - 1))
                        mm.then_inc(o_done, 1)

                def scores(u):
                    pe.wait_ge(k_in, 32 * u + 32)
                    for h in range(HG):
                        if h % 2 == 0:
                            pe.wait_ge(q_lo, 2 * u + h // 2 + 1)
                        for t in range(TT):
                            out = s0[:, h] if t == 0 else s1[:, h]
                            keys = P * (t + 1)
                            for n, (a, r) in enumerate(split_passes(q, kk)):
                                nc.tensor.matmul(out, a[:, h, t * P:(t + 1) * P], r[:, 0:keys],
                                                 start=(n == 0), stop=False, skip_group_check=True)
                            mm = nc.tensor.matmul(out[:, t * P:(t + 1) * P], keep.ident_b[:], keep.mask_b[:],
                                                  start=False, stop=True, skip_group_check=True)
                    mm.then_inc(s_done, 1)

                def outputs(u, j):
                    pe.wait_ge(wo_lo, (u + 2 * B) // B * B)
                    pe.wait_ge(o_lo, 2 * u + j + 3)
                    pe.wait_ge(y_acc, 2 * u + j + 3)
                    at = ((u + 2 * B) // B % 2) * W
                    passes = [(o, w, h) for o, w in split_passes(ot, wo) for h in range(HG)]
                    for n, (o, w, h) in enumerate(passes):
                        mm = nc.tensor.matmul(ps_y[j][:], o[:, j, h * P:(h + 1) * P], w[:, bass.ds(at + h * D, D)],
                                              start=(n == 0), stop=(n == len(passes) - 1))
                    mm.then_inc(y_done, 1)

                def transposes(u):
                    for blk in range(3):
                        if blk == 0:
                            pe.wait_ge(p0_norm, u + 1)
                        if blk == 1:
                            pe.wait_ge(p1_norm, u + 1)
                        for h in range(HG):
                            src = (p0[:, h], p1[:, h, 0:P], p1[:, h, P:S])[blk]
                            mm = nc.tensor.transpose(ps_s[:, blk, h * P:(h + 1) * P], src, keep.ident[:])
                        mm.then_inc(t_done, 1)

                def step(v, par):
                    scores(v - 1)
                    outputs(v - 2, 0)
                    if par is not None:
                        pe.wait_ge(wq_lo, v // B * B + B)
                        queries(par, v)
                    transposes(v - 1)
                    outputs(v - 2, 1)
                    values(v - 1)

                pe.wait_ge(wq_lo, B)
                queries(0, 0)
                with pe.Fori(1, B) as v:
                    step(v, 0)
                with pe.Fori(B, 2 * B) as v:
                    step(v, 1)
                with pe.Fori(1, G0 // 2) as g2:
                    for par in range(2):
                        with pe.Fori(0, B) as b:
                            step(g2 * (2 * B) + par * B + b, par)
                step(U, None)
                for j in range(TT):
                    outputs(U - 1, j)


class NormedTokens:

    def __init__(self, nc, ctx, keep, layer, shift, name):
        def sb(n, shape, dt=F32):
            return ctx.enter_context(nc.sbuf_tensor(f"{name}_{n}", shape, dt))

        self.nc, self.keep, self.layer, self.shift = nc, keep, layer, shift
        self.stats = sb("stats", [P, TT, 6])
        self.mv = sb("mv", [P, TT, 2])
        self.std = sb("std", [P, TT])
        self.rstd = sb("rstd", [P, TT])
        self.xn = sb("xn", [P, TT, D])
        self.ht = sb("ht", [P, KT, S])
        self.ps = ctx.enter_context(nc.psum_tensor(f"{name}_ps_t", [P, KT, S], F32))
        self.step = ctx.enter_context(nc.semaphore(f"{name}_step"))
        self.rooted = ctx.enter_context(nc.semaphore(f"{name}_rooted"))
        self.turned = ctx.enter_context(nc.semaphore(f"{name}_turned"))
        self.ready = ctx.enter_context(nc.semaphore(f"{name}_ready"))

    def start(self, pe):
        pe.sem_inc(self.turned, 1)

    def normalize(self, dve, src, b):
        n, v = 7 * b, self.nc.vector
        v.memset(self.rstd[:], 0.0)
        for t in range(TT):
            v.bn_stats(self.stats[:, t], src[:, t]).then_inc(self.step, 1)
        dve.wait_ge(self.step, n + 2)
        v.memset(self.rstd[:], 0.0)
        for t in range(TT):
            v.bn_aggr(self.mv[:, t], self.stats[:, t]).then_inc(self.step, 1)
        dve.wait_ge(self.rooted, b + 1)
        v.reciprocal(self.rstd[:], self.std[:]).then_inc(self.step, 1)
        dve.wait_ge(self.step, n + 5)
        dve.wait_ge(self.turned, b + 1)
        for t in range(TT):
            v.tensor_scalar(self.xn[:, t], src[:, t], self.mv[:, t, 0:1], self.rstd[:, t:t + 1],
                            ALU.subtract, ALU.mult).then_inc(self.step, 1)

    def roots(self, act, b):
        act.wait_ge(self.step, 7 * b + 4)
        self.nc.scalar.activation(self.std[:], self.mv[:, :, 1], ACT.Sqrt,
                                  bias=self.keep.eps[:, 0:1]).then_inc(self.rooted, 1)

    def transposes(self, pe, b):
        pe.wait_ge(self.step, 7 * b + 7)
        for t in range(TT):
            for k in range(KT):
                mm = self.nc.tensor.transpose(self.ps[:, k, t * P:(t + 1) * P], self.xn[:, t, k * P:(k + 1) * P],
                                              self.keep.ident[:])
        mm.then_inc(self.turned, 1)

    def modulate(self, act, b):
        act.wait_ge(self.turned, b + 2)
        for k in range(KT):
            self.nc.scalar.activation(self.ht[:, k], self.ps[:, k], ACT.Identity,
                                      bias=self.keep.mod[:, self.layer, self.shift, k, bass.ds(b, 1)],
                                      scale=self.keep.mod[:, self.layer, self.shift + 1, k, bass.ds(b, 1)]).then_inc(self.ready, 1)


def split_passes(a, b):
    return ((a[0], b[0]), (a[1], b[0]), (a[0], b[1]))


def element(tensor, b):
    return tensor[:, bass.ds(b * TT, TT)]


def over_tiles(row):
    return row.rearrange("p (o d) -> p o d", o=1).broadcast_to([P, TT, row.shape[1]])


def keep_best(nc, dve, step, base, value, cmp_a, cmp_b, rank, keepers, earlier, count):
    _, t, n = value.shape
    as_m = value.rearrange("p t (o m) -> p t o m", o=1).broadcast_to([P, t, n, n])
    as_n = value.rearrange("p t (n o) -> p t n o", o=1).broadcast_to([P, t, n, n])
    first = earlier.rearrange("p (o n m) -> p o n m", o=1, n=n).broadcast_to([P, t, n, n])
    v = nc.vector
    v.tensor_tensor(cmp_a, as_m, as_n, ALU.is_gt).then_inc(step, 1)
    v.tensor_tensor(cmp_b, as_m, as_n, ALU.is_equal).then_inc(step, 1)
    dve.wait_ge(step, base + 2)
    v.tensor_tensor(cmp_b, cmp_b, first, ALU.mult).then_inc(step, 1)
    dve.wait_ge(step, base + 3)
    v.tensor_tensor(cmp_a, cmp_a, cmp_b, ALU.add).then_inc(step, 1)
    dve.wait_ge(step, base + 4)
    v.tensor_reduce(rank, cmp_a, AX, ALU.add).then_inc(step, 1)
    dve.wait_ge(step, base + 5)
    v.tensor_scalar(keepers, rank, count - 0.5, None, ALU.is_lt).then_inc(step, 1)
    dve.wait_ge(step, base + 6)


def phase_router0(nc, io, keep):
    with ExitStack() as ctx:
        def sb(name, shape, dt=F32):
            return ctx.enter_context(nc.sbuf_tensor(name, shape, dt))

        def sem(name):
            return ctx.enter_context(nc.semaphore(name))

        E, R = LORA0_E, LORA0_R
        x = sb("d_x", [P, TT, D])
        gate = sb("d_gate", [P, D])
        ra = sb("d_ra", [P, KT, E + E * R])
        norm = NormedTokens(nc, ctx, keep, 0, 2, "d")
        ps_r = ctx.enter_context(nc.psum_tensor("d_ps_r", [P, TT, E + E * R], F32))
        logits = sb("d_logits", [P, NT, E])
        earlier = sb("d_earlier", [P, E * E])
        cmp_a = sb("d_cmp_a", [P, NT, E, E])
        cmp_b = sb("d_cmp_b", [P, NT, E, E])
        rank = sb("d_rank", [P, NT, E])
        keepers = sb("d_keepers", [P, NT, E])
        top = sb("d_top", [P, NT])
        e = sb("d_e", [P, NT, E])
        total = sb("d_total", [P, NT])

        w_in = sem("d_w_in")
        x_in = sem("d_x_in")
        x1_step = sem("d_x1_step")
        r_done = sem("d_r_done")
        r_out = sem("d_r_out")
        g_step = sem("d_g_step")
        g_exp = sem("d_g_exp")

        with nc.Block() as block:
            @block.sync
            def _(sp):
                sp.dma_start(ra[:, :, 0:E], io["router0"]).then_inc(w_in, 16)
                sp.dma_start(ra[:, :, E:], io["a0"]).then_inc(w_in, 16)
                sp.dma_start(earlier[:], io["earlier0"]).then_inc(w_in, 16)
                sp.dma_start(x[:], io["x"][0]).then_inc(x_in, 16)
                sp.dma_start(gate[:], keep.gates[0, 0:1].partition_broadcast(P)).then_inc(x_in, 16)
                with sp.Fori(1, B) as b:
                    sp.wait_ge(x1_step, 2 * b)
                    sp.dma_start(x[:], io["x"][bass.ds(b, 1)].rearrange("o p t d -> p (o t) d")).then_inc(x_in, 16)
                    sp.dma_start(gate[:], keep.gates[0, bass.ds(b, 1)].partition_broadcast(P)).then_inc(x_in, 16)

            @block.vector
            def _(dve):
                with dve.Fori(0, B) as b:
                    x1 = element(keep.acc, b)
                    dve.wait_ge(x_in, 32 * b + 32)
                    nc.vector.tensor_tensor(x1, x1, over_tiles(gate[:]), ALU.mult).then_inc(x1_step, 1)
                    dve.wait_ge(x1_step, 2 * b + 1)
                    nc.vector.tensor_tensor(x1, x1, x[:], ALU.add).then_inc(x1_step, 1)
                    dve.wait_ge(x1_step, 2 * b + 2)
                    norm.normalize(dve, x1, b)
                dve.wait_ge(w_in, 48)
                dve.wait_ge(r_out, 2 * B)
                keep_best(nc, dve, g_step, 0, logits[:], cmp_a[:], cmp_b[:], rank[:], keepers[:], earlier[:], 2)
                nc.vector.tensor_reduce(top[:], logits[:], AX, ALU.max).then_inc(g_step, 1)
                dve.wait_ge(g_step, 7)
                nc.vector.tensor_tensor(e[:], logits[:], top[:].rearrange("p (t o) -> p t o", o=1).broadcast_to([P, NT, E]),
                                        ALU.subtract).then_inc(g_step, 1)
                dve.wait_ge(g_exp, 1)
                nc.vector.tensor_tensor(e[:], e[:], keepers[:], ALU.mult).then_inc(g_step, 1)
                dve.wait_ge(g_step, 9)
                nc.vector.tensor_reduce(total[:], e[:], AX, ALU.add).then_inc(g_step, 1)
                dve.wait_ge(g_step, 10)
                nc.vector.reciprocal(total[:], total[:]).then_inc(g_step, 1)
                dve.wait_ge(g_step, 11)
                nc.vector.tensor_scalar(total[:], total[:], LORA0_SCALE, None, ALU.mult).then_inc(g_step, 1)
                dve.wait_ge(g_step, 12)
                nc.vector.tensor_tensor(e[:], e[:], total[:].rearrange("p (t o) -> p t o", o=1).broadcast_to([P, NT, E]),
                                        ALU.mult).then_inc(g_step, 1)
                dve.wait_ge(g_step, 13)
                for i in range(E):
                    m = keep.mid0[:, :, i * R:(i + 1) * R]
                    nc.vector.tensor_tensor(m, m, e[:, :, i:i + 1].broadcast_to([P, NT, R]), ALU.mult).then_inc(g_step, 1)

            @block.scalar
            def _(act):
                nc.scalar.preload_act_table(ACT.Sqrt)
                with act.Fori(0, B) as b:
                    norm.roots(act, b)
                    act.wait_ge(r_done, b + 1)
                    norm.modulate(act, b)
                    act.wait_ge(r_done, b + 2)
                    nc.scalar.activation(element(logits, b), ps_r[:, :, 0:E], ACT.Identity).then_inc(r_out, 1)
                    nc.scalar.activation(element(keep.mid0, b), ps_r[:, :, E:], ACT.Identity).then_inc(r_out, 1)
                act.wait_ge(g_step, 8)
                nc.scalar.activation(e[:], e[:], ACT.Exp).then_inc(g_exp, 1)

            @block.tensor
            def _(pe):
                norm.start(pe)
                pe.sem_inc(r_done, 1)
                pe.wait_ge(w_in, 48)
                with pe.Fori(0, B) as b:
                    norm.transposes(pe, b)
                    pe.wait_ge(norm.ready, KT * b + KT)
                    for t in range(TT):
                        for k in range(KT):
                            mm = nc.tensor.matmul(ps_r[:, t], norm.ht[:, k, t * P:(t + 1) * P], ra[:, k],
                                                  start=(k == 0), stop=(k == KT - 1))
                    mm.then_inc(r_done, 1)
                    pe.wait_ge(r_out, 2 * b + 2)


def phase_queries1(nc, io, keep):
    with ExitStack() as ctx:
        def sb(name, shape, dt=F32):
            return ctx.enter_context(nc.sbuf_tensor(name, shape, dt))

        def sem(name):
            return ctx.enter_context(nc.semaphore(name))

        ER = LORA0_E * LORA0_R
        gate = sb("e_gate", [P, D])
        b0 = sb("e_b0", [2 * ER, TT, D])
        shared_at = -(-nc.sbuf_base // 32) * 32
        hs = [sb(f"e_hs{i}", [P, KT, S], F32R) for i in range(2)]
        wst = nc.alloc_sbuf_tensor_at("e_wst", [P, KT, D], F32, offset=shared_at)
        vst = [sb(f"e_vst{i}", [P, 8, D // 8]) for i in range(2)]
        w = [[sb(f"e_w{n}{i}", [P, KT, D], F32R) for i in range(2)] for n in range(3)]
        mid = sb("e_mid", [P, TT, ER])
        midt = sb("e_midt", [TT * ER, P])
        delta = sb("e_delta", [P, TT, D])
        norm = NormedTokens(nc, ctx, keep, 1, 0, "e")
        rcos = sb("e_rcos", [P, D])
        rswap = sb("e_rswap", [P, D])
        cos = sb("e_cos", [P, TT, HD1])
        sin = sb("e_sin", [P, TT, HD1])
        ps_m = ctx.enter_context(nc.psum_tensor("e_ps_m", [TT * ER, P], F32))
        ps_d = ctx.enter_context(nc.psum_tensor("e_ps_d", [P, TT, D], F32))
        ps_p = [ctx.enter_context(nc.psum_tensor(f"e_ps_p{i}", [P, D], F32)) for i in range(3)]

        b0_zero = sem("e_b0_zero")
        w_in = sem("e_w_in")
        w_hi = sem("e_w_hi")
        w_lo = sem("e_w_lo")
        tab_in = sem("e_tab_in")
        gate_in = sem("e_gate_in")
        mid_ready = sem("e_mid_ready")
        m_done = sem("e_m_done")
        m_out = sem("e_m_out")
        d_done = sem("e_d_done")
        x2_step = sem("e_x2_step")
        h_hi = sem("e_h_hi")
        h_lo = sem("e_h_lo")
        p_done = sem("e_p_done")
        p_mul = sem("e_p_mul")
        p_out = sem("e_p_out")
        v_out = sem("e_v_out")
        v_stored = [sem(f"e_v_stored{t}") for t in range(TT)]

        with nc.Block() as block:
            @block.sync
            def _(sp):
                sp.wait_ge(b0_zero, 1)
                for t in range(TT):
                    sp.dma_start(b0[t * ER:(t + 1) * ER, t], io["b0"]).then_inc(tab_in, 16)
                sp.dma_start(cos[:], io["cos1"]).then_inc(tab_in, 16)
                sp.dma_start(sin[:], io["sin1"]).then_inc(tab_in, 16)
                sp.dma_start(gate[:], keep.gates[1, 0:1].partition_broadcast(P)).then_inc(gate_in, 16)
                for n, name in enumerate(("wq1", "wk1", "wv1")):
                    if n:
                        sp.wait_ge(w_lo, n)
                    sp.dma_start(wst[:], io[name]).then_inc(w_in, 16)

                def store_values(b):
                    for t in range(TT):
                        sp.wait_ge(v_out, TT * b + t + 1)
                        sp.dma_start(keep.v1_dram[:, bass.ds(b * 8, 8), t], vst[t][:]).then_inc(v_stored[t], 16)

                for s in v_stored:
                    sp.sem_inc(s, 16)
                with sp.Fori(1, B) as b:
                    sp.wait_ge(x2_step, 2 * b)
                    sp.dma_start(gate[:], keep.gates[1, bass.ds(b, 1)].partition_broadcast(P)).then_inc(gate_in, 16)
                    store_values(b - 1)
                store_values(B - 1)
                for s in v_stored:
                    sp.wait_ge(s, 16 * B + 16)

            @block.scalar
            def _(act):
                for n in range(3):
                    act.wait_ge(w_in, 16 * (n + 1))
                    nc.scalar.activation(w[n][0][:], wst[:], ACT.Identity).then_inc(w_hi, 1)

                def lora_in(b):
                    nc.scalar.activation(mid[:], element(keep.mid0, b), ACT.Identity).then_inc(mid_ready, 1)
                    act.wait_ge(m_done, b + 1)
                    nc.scalar.activation(midt[:], ps_m[:], ACT.Identity).then_inc(m_out, 1)

                def values(b, t):
                    act.wait_ge(p_done, 6 * b + 3 * t + 3)
                    act.wait_ge(v_stored[t], 16 * b + 16)
                    nc.scalar.activation(vst[t][:], ps_p[2][:].rearrange("p (g c) -> p g c", g=8),
                                         ACT.Identity).then_inc(v_out, 1)

                def split_h(b):
                    act.wait_ge(norm.ready, KT * b + KT)
                    nc.scalar.activation(hs[0][:], norm.ht[:], ACT.Identity).then_inc(h_hi, 1)

                lora_in(0)
                norm.roots(act, 0)
                norm.modulate(act, 0)
                split_h(0)
                with act.Fori(0, B - 1) as b:
                    lora_in(b + 1)
                    values(b, 0)
                    norm.roots(act, b + 1)
                    values(b, 1)
                    act.wait_ge(h_lo, b + 1)
                    norm.modulate(act, b + 1)
                    act.wait_ge(p_done, 6 * b + 6)
                    split_h(b + 1)
                values(B - 1, 0)
                values(B - 1, 1)

            @block.vector
            def _(dve):
                nc.vector.memset(b0[:], 0.0).then_inc(b0_zero, 1)
                for n in range(3):
                    dve.wait_ge(w_hi, n + 1)
                    nc.vector.tensor_tensor(w[n][1][:], wst[:], f32(w[n][0][:]), ALU.subtract).then_inc(w_lo, 1)
                dve.wait_ge(tab_in, 64)

                def add_lora(b):
                    x2 = element(keep.acc, b)
                    dve.wait_ge(gate_in, 16 * b + 16)
                    dve.wait_ge(d_done, b + 1)
                    nc.vector.tensor_tensor(delta[:], ps_d[:], over_tiles(gate[:]), ALU.mult).then_inc(x2_step, 1)
                    dve.wait_ge(x2_step, 2 * b + 1)
                    nc.vector.tensor_tensor(x2, x2, delta[:], ALU.add).then_inc(x2_step, 1)
                    dve.wait_ge(x2_step, 2 * b + 2)
                    norm.normalize(dve, x2, b)

                def split_h(b):
                    dve.wait_ge(h_hi, b + 1)
                    nc.vector.tensor_tensor(hs[1][:], norm.ht[:], f32(hs[0][:]), ALU.subtract).then_inc(h_lo, 1)

                def rotate(b, t):
                    half = HD1 // 2
                    for n in range(2):
                        dve.wait_ge(p_done, 6 * b + 3 * t + n + 1)
                        dve.wait_ge(p_out, 4 * b + 2 * t + n + 1)
                        src = ps_p[n][:].rearrange("p (h c) -> p h c", h=H1)
                        c = cos[:, t].rearrange("p (o c) -> p o c", o=1).broadcast_to([P, H1, HD1])
                        sn = sin[:, t].rearrange("p (o c) -> p o c", o=1).broadcast_to([P, H1, HD1])
                        rs = rswap[:].rearrange("p (h c) -> p h c", h=H1)
                        nc.vector.tensor_tensor(rcos[:].rearrange("p (h c) -> p h c", h=H1), src, c, ALU.mult)
                        nc.vector.tensor_tensor(rs[:, :, 0:half], src[:, :, half:], sn[:, :, 0:half], ALU.mult)
                        nc.vector.tensor_tensor(rs[:, :, half:], src[:, :, 0:half], sn[:, :, half:], ALU.mult).then_inc(p_mul, 1)

                add_lora(0)
                split_h(0)
                with dve.Fori(0, B - 1) as b:
                    rotate(b, 0)
                    add_lora(b + 1)
                    rotate(b, 1)
                    dve.wait_ge(p_done, 6 * b + 6)
                    split_h(b + 1)
                rotate(B - 1, 0)
                rotate(B - 1, 1)

            @block.gpsimd
            def _(pool):
                pool.sem_inc(p_out, 1)
                with pool.Fori(0, B) as b:
                    for t in range(TT):
                        for n, dst in enumerate((keep.q1, keep.k1)):
                            pool.wait_ge(p_mul, 4 * b + 2 * t + n + 1)
                            nc.gpsimd.tensor_tensor(dst[:, bass.ds(b * 8, 8), t], rcos[:].rearrange("p (g c) -> p g c", g=8),
                                                    rswap[:].rearrange("p (g c) -> p g c", g=8), ALU.add).then_inc(p_out, 1)

            @block.tensor
            def _(pe):
                def lora_in(b):
                    pe.wait_ge(mid_ready, b + 1)
                    nc.tensor.transpose(ps_m[:], mid[:].rearrange("p t e -> p (t e)"), keep.ident[:]).then_inc(m_done, 1)

                def lora_out(b):
                    pe.wait_ge(m_out, b + 1)
                    for t in range(TT):
                        mm = nc.tensor.matmul(ps_d[:, t], midt[:], b0[:, t], start=True, stop=True)
                    mm.then_inc(d_done, 1)

                def project(b, t):
                    for n in range(3):
                        if t:
                            pe.wait_ge(*((p_mul, 4 * b + n + 1) if n < 2 else (v_out, 2 * b + 1)))
                        passes = [(a, r, k) for a, r in split_passes(hs, w[n]) for k in range(KT)]
                        for j, (a, r, k) in enumerate(passes):
                            mm = nc.tensor.matmul(ps_p[n][:], a[:, k, t * P:(t + 1) * P], r[:, k],
                                                  start=(j == 0), stop=(j == len(passes) - 1))
                        mm.then_inc(p_done, 1)

                norm.start(pe)
                pe.wait_ge(w_lo, 3)
                pe.wait_ge(tab_in, 64)
                lora_in(0)
                lora_out(0)
                norm.transposes(pe, 0)
                with pe.Fori(0, B - 1) as b:
                    lora_in(b + 1)
                    pe.wait_ge(h_lo, b + 1)
                    project(b, 0)
                    lora_out(b + 1)
                    project(b, 1)
                    norm.transposes(pe, b + 1)
                    pe.wait_ge(p_mul, 4 * b + 4)
                    pe.wait_ge(v_out, 2 * b + 2)
                pe.wait_ge(h_lo, B)
                project(B - 1, 0)
                project(B - 1, 1)


def phase_attention1(nc, io, keep):
    U = 8 * B
    HU = 4
    VW = 2 * HD1 + 2
    with ExitStack() as ctx:
        def sb(name, shape, dt=F32):
            return ctx.enter_context(nc.sbuf_tensor(name, shape, dt))

        def sem(name):
            return ctx.enter_context(nc.semaphore(name))

        stack = [sb(f"f_stack{n}", [P, TT * HU, 4, HD1]) for n in range(2)]
        kt = sb("f_kt", [P, 2, S], F32R)
        qt = [sb(f"f_qt{e}", [P, 2, S], F32R) for e in range(2)]
        vx = sb("f_vx", [P, TT, HU, HD1])
        vs = sb("f_vs", [P, TT, HU, VW], F32R)
        prob = sb("f_prob", [P, 3 * HU * P])
        row_max = sb("f_row_max", [P, 2, HU])
        neg_max = sb("f_neg_max", [P, 2, HU])
        inv_sum = sb("f_inv_sum", [P, TT * HU])
        pt = [sb(f"f_pt{i}", [P, 3, HU * P], F32R) for i in range(2)]
        osum = sb("f_osum", [P, TT * HU, HD1])
        ps_qk = [ctx.enter_context(nc.psum_tensor(f"f_ps_qk{n}", [P, 2, S], F32)) for n in range(2)]
        ps_s = ctx.enter_context(nc.psum_tensor("f_ps_s", [P, 3, D], F32))
        ps_t = [ctx.enter_context(nc.psum_tensor(f"f_ps_t{i}", [P, D], F32)) for i in range(2)]
        ps_o = ctx.enter_context(nc.psum_tensor("f_ps_o", [P, TT * HU, VW], F32))
        scores_of = (ps_s[:, 0].rearrange("p (h k) -> p h k", h=HU),
                     ps_s[:, 1:3].rearrange("p a (h k) -> p (a h) k", h=2))
        p0 = prob[:, 0:HU * P].rearrange("p (h k) -> p h k", h=HU)
        p1 = prob[:, HU * P:].rearrange("p (h k) -> p h k", h=HU)

        zeroed = sem("f_zeroed")
        v_in = sem("f_v_in")
        st_hi = sem("f_st_hi")
        st_lo = sem("f_st_lo")
        vs_hi = sem("f_vs_hi")
        vs_lo = sem("f_vs_lo")
        qk_done = sem("f_qk_done")
        qk_out = sem("f_qk_out")
        s_done = sem("f_s_done")
        smax = sem("f_smax")
        sneg = sem("f_sneg")
        p_exp = sem("f_p_exp")
        t_done = sem("f_t_done")
        t_hi = sem("f_t_hi")
        t_lo = sem("f_t_lo")
        o_done = sem("f_o_done")
        o_step = sem("f_o_step")

        def steps(engine, step):
            step(0, 0, 2)
            step(1, 1, 2)
            with engine.Fori(2, U - 2) as v:
                step(v, 2, 2)
            step(U - 2, 2, 1)
            step(U - 1, 2, 0)

        def heads(src, u):
            x = src[:, bass.ds(u, 1)].rearrange("p o t (h r c) -> p (o t h) r c", h=HU, r=1)
            return x.broadcast_to([P, TT * HU, 2, HD1])

        with nc.Block() as block:
            @block.sync
            def _(sp):
                def load_values(u):
                    sp.dma_start(vx[:].rearrange("p t h c -> p t (h c)"),
                                 keep.v1_dram[:, bass.ds(u, 1)].rearrange("p o t c -> p (o t) c")).then_inc(v_in, 16)

                load_values(0)
                with sp.Fori(1, U) as u:
                    sp.wait_ge(vs_lo, u)
                    load_values(u)

            @block.vector
            def _(dve):
                def stacks(u, first=False):
                    if not first:
                        dve.wait_ge(qk_done, 2 * u)
                    for n, (src, hi) in enumerate(((keep.q1, slice(0, 4, 2)), (keep.k1, slice(0, 2)))):
                        nc.vector.tensor_copy(stack[n][:, :, hi].bitcast(F32R), heads(src, u)).then_inc(st_hi, 1)

                def rest_of_transposed(u, blocks):
                    for j in blocks:
                        dve.wait_ge(t_hi, 3 * u + j + 1)
                        nc.vector.tensor_tensor(pt[1][:, j], ps_t[j % 2][:], f32(pt[0][:, j]), ALU.subtract).then_inc(t_lo, 1)

                def maxima(u, t):
                    dve.wait_ge(s_done, 2 * u + t + 1)
                    nc.vector.tensor_reduce(row_max[:, t], scores_of[t], AX, ALU.max).then_inc(smax, 1)
                    dve.wait_ge(smax, 2 * u + t + 1)
                    nc.vector.tensor_scalar(neg_max[:, t], row_max[:, t], -SCALE1, None, ALU.mult).then_inc(sneg, 1)

                def output(u):
                    dve.wait_ge(o_done, u + 1)
                    parts = ps_o[:, :, 0:2 * HD1].rearrange("p n (r c) -> p n c r", r=2)
                    nc.vector.tensor_reduce(osum[:], parts, AX, ALU.add).then_inc(o_step, 1)
                    nc.vector.reciprocal(inv_sum[:], ps_o[:, :, 2 * HD1]).then_inc(o_step, 1)
                    dve.wait_ge(o_step, 3 * u + 2)
                    inv = inv_sum[:].rearrange("p (n o) -> p n o", o=1).broadcast_to([P, TT * HU, HD1])
                    dst = keep.o1[:, bass.ds(u, 1)].rearrange("p o t (h c) -> p (o t h) c", h=HU)
                    nc.vector.tensor_tensor(dst, osum[:], inv, ALU.mult).then_inc(o_step, 1)

                def step(v, before, after):
                    maxima(v, 1)
                    if before:
                        rest_of_transposed(v - 1, (1, 2))
                    if after:
                        maxima(v + 1, 0)
                    rest_of_transposed(v, (0,))
                    if after >= 2:
                        stacks(v + 2)
                    if before:
                        output(v - 1)

                for tile in qt:
                    nc.vector.memset(f32(tile[:]), 0.0).then_inc(zeroed, 1)
                nc.vector.memset(f32(vs[:]), 1.0).then_inc(zeroed, 1)
                stacks(0, first=True)
                maxima(0, 0)
                stacks(1)
                steps(dve, step)
                rest_of_transposed(U - 1, (1, 2))
                output(U - 1)

            @block.scalar
            def _(act):
                def queries_keys(u):
                    act.wait_ge(qk_done, 2 * u + 1)
                    for e in range(2):
                        rows = slice(e * P // 2, (e + 1) * P // 2)
                        nc.scalar.activation(qt[e][rows], ps_qk[0][rows], ACT.Identity).then_inc(qk_out, 1)
                    act.wait_ge(qk_done, 2 * u + 2)
                    nc.scalar.activation(kt[:], ps_qk[1][:], ACT.Identity).then_inc(qk_out, 1)

                def transposed(u, blocks):
                    for j in blocks:
                        act.wait_ge(t_done, 3 * u + j + 1)
                        nc.scalar.activation(pt[0][:, j], ps_t[j % 2][:], ACT.Identity).then_inc(t_hi, 1)

                def exponentials(u, t):
                    act.wait_ge(sneg, 2 * u + t + 1)
                    for h in range(HU):
                        nc.scalar.activation((p0, p1)[t][:, h], scores_of[t][:, h], ACT.Exp, bias=neg_max[:, t, h:h + 1],
                                             scale=SCALE1).then_inc(p_exp, 1)

                def values(u, before):
                    act.wait_ge(v_in, 16 * u + 16)
                    if before:
                        act.wait_ge(o_done, u)
                    nc.scalar.activation(vs[:, :, :, 0:HD1], vx[:], ACT.Identity).then_inc(vs_hi, 1)

                def step(v, before, after):
                    exponentials(v, 0)
                    if before:
                        values(v - 1, before >= 2)
                        transposed(v - 1, (1, 2))
                    if after:
                        queries_keys(v + 1)
                    exponentials(v, 1)
                    transposed(v, (0,))

                nc.scalar.preload_act_table(ACT.Exp)
                act.wait_ge(zeroed, 3)
                queries_keys(0)
                steps(act, step)
                values(U - 1, True)
                transposed(U - 1, (1, 2))

            @block.gpsimd
            def _(pool):
                def stacks(u):
                    pool.wait_ge(st_hi, 2 * u + 2)
                    for n, (src, lo) in enumerate(((keep.q1, slice(1, 4, 2)), (keep.k1, slice(2, 4)))):
                        h2 = stack[n][:, :, 0:1].broadcast_to([P, TT * HU, 2, HD1])
                        nc.gpsimd.tensor_tensor(stack[n][:, :, lo].bitcast(F32R), heads(src, u), h2, ALU.subtract).then_inc(st_lo, 1)

                def values(u):
                    pool.wait_ge(vs_hi, u + 1)
                    nc.gpsimd.tensor_tensor(vs[:, :, :, HD1:2 * HD1], vx[:], f32(vs[:, :, :, 0:HD1]), ALU.subtract).then_inc(vs_lo, 1)

                stacks(0)
                stacks(1)
                with pool.Fori(2, U) as u:
                    values(u - 2)
                    stacks(u)
                values(U - 2)
                values(U - 1)

            @block.tensor
            def _(pe):
                def queries_keys(u):
                    for n in range(2):
                        pe.wait_ge(st_lo, 2 * u + n + 1)
                        for i in range(2):
                            for t in range(TT):
                                a = stack[n][:, t * HU + 2 * i:t * HU + 2 * i + 2].rearrange("p h r c -> p (h r c)")
                                mm = nc.tensor.transpose(ps_qk[n][:, i, t * P:(t + 1) * P], a, keep.ident[:])
                        mm.then_inc(qk_done, 1)

                def transposes(u, j, before=True):
                    if j == 0 and before:
                        pe.wait_ge(t_lo, 3 * u)
                    if j == 2:
                        pe.wait_ge(t_lo, 3 * u + 1)
                    pe.wait_ge(p_exp, 8 * u + (4 if j == 0 else 8))
                    src, at = ((p0, 0), (p1, 0), (p1, P))[j]
                    for h in range(HU):
                        mm = nc.tensor.transpose(ps_t[j % 2][:, h * P:(h + 1) * P], src[:, h, at:at + P], keep.ident[:])
                    mm.then_inc(t_done, 1)

                def scores(u, t):
                    pe.wait_ge(qk_out, 3 * u + 3)
                    for h in range(HU):
                        out = scores_of[t][:, h]
                        nc.tensor.matmul(out, qt[h % 2][:, h // 2, t * P:(t + 1) * P], kt[:, h // 2, 0:P * (t + 1)],
                                         start=True, stop=False, skip_group_check=True)
                        mm = nc.tensor.matmul(out[:, t * P:(t + 1) * P], keep.ident_b[:], keep.mask_b[:],
                                              start=False, stop=True, skip_group_check=True)
                    mm.then_inc(s_done, 1)

                def values(u, t, before):
                    if t == 0:
                        pe.wait_ge(vs_lo, u + 1)
                        if before:
                            pe.wait_ge(o_step, 3 * u)
                    pe.wait_ge(t_lo, 3 * u + 1 + 2 * t)
                    blocks = ((0, 1), (1, 2)) if t else ((0, 0),)
                    for h in range(HU):
                        passes = [(p, k, blk) for p in pt for k, blk in blocks]
                        for n, (p, k, blk) in enumerate(passes):
                            mm = nc.tensor.matmul(ps_o[:, t * HU + h], p[:, blk, h * P:(h + 1) * P], vs[:, k, h],
                                                  start=(n == 0), stop=(n == len(passes) - 1))
                    if t:
                        mm.then_inc(o_done, 1)

                def step(v, before, after):
                    if before:
                        transposes(v - 1, 1)
                    scores(v, 1)
                    if before:
                        transposes(v - 1, 2)
                    if after:
                        queries_keys(v + 1)
                    if before:
                        values(v - 1, 0, before >= 2)
                    transposes(v, 0, before > 0)
                    if after:
                        scores(v + 1, 0)
                    if before:
                        values(v - 1, 1, True)

                queries_keys(0)
                scores(0, 0)
                steps(pe, step)
                for j in (1, 2):
                    transposes(U - 1, j)
                for t in range(TT):
                    values(U - 1, t, True)


def phase_router1(nc, io, keep):
    with ExitStack() as ctx:
        def sb(name, shape, dt=F32):
            return ctx.enter_context(nc.sbuf_tensor(name, shape, dt))

        def sem(name):
            return ctx.enter_context(nc.semaphore(name))

        E, R = LORA1_E, LORA1_R
        ER = E * R
        gate = [sb(f"g_gate{i}", [P, D]) for i in range(2)]
        bias = sb("g_bias", [P, D])
        rl = sb("g_rl", [P, KT, NR + ER])
        wst = sb("g_wst", [P, KT, D])
        w = [[sb(f"g_w{n}{i}", [P, KT, D], F32R) for i in range(2)] for n in range(2)]
        o = sb("g_o", [P, TT, D])
        oh = [sb(f"g_oh{i}", [P, KT, S], F32R) for i in range(2)]
        hs = [sb(f"g_hs{i}", [P, KT, S], F32R) for i in range(2)]
        y = sb("g_y", [P, TT, D])
        base = sb("g_base", [P, TT, D])
        norm = NormedTokens(nc, ctx, keep, 1, 2, "g")
        ps_y = ctx.enter_context(nc.psum_tensor("g_ps_y", [P, TT, D], F32))
        ps_b = ctx.enter_context(nc.psum_tensor("g_ps_b", [P, TT, D], F32))
        ps_r = ctx.enter_context(nc.psum_tensor("g_ps_r", [P, TT, NR + ER], F32))
        logits = sb("g_logits", [P, NT, NR])
        rbias = sb("g_rbias", [P, NR])
        emap_i = sb("g_emap_i", [P, NR], I32)
        emap = sb("g_emap", [P, NR])
        expert = sb("g_expert", [P, E * NR])
        sel = sb("g_sel", [P, E, NR])
        earlier = sb("g_earlier", [P, NR * NR])
        top = sb("g_top", [P, NT])
        e = sb("g_e", [P, NT, NR])
        rank = sb("g_rank", [P, NT, NR])
        keepers = sb("g_keepers", [P, NT, NR])
        total = sb("g_total", [P, NT])
        wexp = sb("g_wexp", [P, NT, E])
        QT = 2
        cmp_a = sb("g_cmp_a", [P, QT, NR, NR])
        cmp_b = sb("g_cmp_b", [P, QT, NR, NR])
        mixed = sb("g_mixed", [P, QT, E, NR])

        tab_in = sem("g_tab_in")
        w_in = sem("g_w_in")
        w_hi = sem("g_w_hi")
        w_lo = sem("g_w_lo")
        ga_in = sem("g_ga_in")
        gb_in = sem("g_gb_in")
        o_in = sem("g_o_in")
        o_turned = sem("g_o_turned")
        o_hi = sem("g_o_hi")
        o_lo = sem("g_o_lo")
        y_done = sem("g_y_done")
        x3_step = sem("g_x3_step")
        h_hi = sem("g_h_hi")
        h_lo = sem("g_h_lo")
        b_done = sem("g_b_done")
        r_done = sem("g_r_done")
        r_out = sem("g_r_out")
        b_out = sem("g_b_out")
        b_step = sem("g_b_step")
        g_step = sem("g_g_step")
        g_exp = sem("g_g_exp")

        with nc.Block() as block:
            @block.sync
            def _(sp):
                sp.dma_start(wst[:], io["wo1"]).then_inc(w_in, 16)
                sp.dma_start(rl[:, :, 0:NR], io["router1"]).then_inc(tab_in, 16)
                sp.dma_start(rl[:, :, NR:], io["a1"]).then_inc(tab_in, 16)
                sp.dma_start(bias[:], io["base_b"].partition_broadcast(P)).then_inc(tab_in, 16)
                sp.dma_start(rbias[:], io["router_b"].partition_broadcast(P)).then_inc(tab_in, 16)
                sp.dma_start(emap_i[:], io["expert_map"].partition_broadcast(P)).then_inc(tab_in, 16)
                sp.dma_start(expert[:], io["expert"]).then_inc(tab_in, 16)
                sp.dma_start(earlier[:], io["earlier1"]).then_inc(tab_in, 16)
                sp.dma_start(gate[0][:], keep.gates[2, 0:1].partition_broadcast(P)).then_inc(ga_in, 16)
                sp.dma_start(gate[1][:], keep.gates[3, 0:1].partition_broadcast(P)).then_inc(gb_in, 16)
                sp.wait_ge(w_lo, 1)
                sp.dma_start(wst[:], io["base_w"]).then_inc(w_in, 16)
                with sp.Fori(1, B) as b:
                    sp.wait_ge(x3_step, 2 * b)
                    sp.dma_start(gate[0][:], keep.gates[2, bass.ds(b, 1)].partition_broadcast(P)).then_inc(ga_in, 16)
                    sp.wait_ge(b_step, 2 * b)
                    sp.dma_start(gate[1][:], keep.gates[3, bass.ds(b, 1)].partition_broadcast(P)).then_inc(gb_in, 16)

            @block.gpsimd
            def _(pool):
                def fetch(b):
                    for t in range(TT):
                        nc.gpsimd.tensor_copy(o[:, t].rearrange("p (g c) -> p g c", g=8),
                                              keep.o1[:, bass.ds(b * 8, 8), t]).then_inc(o_in, 1)

                def add_base(b):
                    pool.wait_ge(gb_in, 16 * b + 16)
                    pool.wait_ge(b_out, b + 2)
                    nc.gpsimd.tensor_tensor(base[:], base[:], over_tiles(gate[1][:]), ALU.mult).then_inc(b_step, 1)
                    pool.wait_ge(b_step, 2 * b + 1)
                    x3 = element(keep.acc, b)
                    nc.gpsimd.tensor_tensor(x3, x3, base[:], ALU.add).then_inc(b_step, 1)

                fetch(0)
                with pool.Fori(0, B - 1) as b:
                    pool.wait_ge(o_turned, b + 1)
                    fetch(b + 1)
                    add_base(b)
                add_base(B - 1)

            @block.scalar
            def _(act):
                def split_o(b):
                    act.wait_ge(o_turned, b + 1)
                    nc.scalar.activation(oh[0][:], norm.ps[:], ACT.Identity).then_inc(o_hi, 1)

                def split_h(b):
                    act.wait_ge(norm.ready, KT * b + KT)
                    nc.scalar.activation(hs[0][:], norm.ht[:], ACT.Identity).then_inc(h_hi, 1)

                def router_out(b):
                    act.wait_ge(r_done, b + 1)
                    nc.scalar.activation(element(logits, b), ps_r[:, :, 0:NR], ACT.Identity).then_inc(r_out, 1)
                    nc.scalar.activation(element(keep.mid1, b), ps_r[:, :, NR:], ACT.Identity).then_inc(r_out, 1)

                for n in range(2):
                    act.wait_ge(w_in, 16 * (n + 1))
                    nc.scalar.activation(w[n][0][:], wst[:], ACT.Identity).then_inc(w_hi, 1)
                split_o(0)
                norm.roots(act, 0)
                norm.modulate(act, 0)
                split_h(0)
                with act.Fori(0, B - 1) as b:
                    split_o(b + 1)
                    norm.roots(act, b + 1)
                    router_out(b)
                    act.wait_ge(h_lo, b + 1)
                    norm.modulate(act, b + 1)
                    split_h(b + 1)
                router_out(B - 1)
                act.wait_ge(g_step, 10)
                nc.scalar.activation(e[:], e[:], ACT.Exp).then_inc(g_exp, 1)

            @block.vector
            def _(dve):
                def split_o(b):
                    dve.wait_ge(o_hi, b + 1)
                    nc.vector.tensor_tensor(oh[1][:], norm.ps[:], f32(oh[0][:]), ALU.subtract).then_inc(o_lo, 1)

                def add_y(b):
                    x3 = element(keep.acc, b)
                    dve.wait_ge(ga_in, 16 * b + 16)
                    dve.wait_ge(y_done, b + 1)
                    nc.vector.tensor_tensor(y[:], ps_y[:], over_tiles(gate[0][:]), ALU.mult).then_inc(x3_step, 1)
                    dve.wait_ge(x3_step, 2 * b + 1)
                    nc.vector.tensor_tensor(x3, x3, y[:], ALU.add).then_inc(x3_step, 1)
                    dve.wait_ge(x3_step, 2 * b + 2)
                    norm.normalize(dve, x3, b)

                def split_h(b):
                    dve.wait_ge(h_hi, b + 1)
                    nc.vector.tensor_tensor(hs[1][:], norm.ht[:], f32(hs[0][:]), ALU.subtract).then_inc(h_lo, 1)

                def base_out(b):
                    dve.wait_ge(b_done, b + 1)
                    nc.vector.tensor_tensor(base[:], ps_b[:], over_tiles(bias[:]), ALU.add).then_inc(b_out, 1)

                dve.sem_inc(b_out, 1)
                for n in range(2):
                    dve.wait_ge(w_hi, n + 1)
                    nc.vector.tensor_tensor(w[n][1][:], wst[:], f32(w[n][0][:]), ALU.subtract).then_inc(w_lo, 1)
                dve.wait_ge(tab_in, 16 * 7)
                split_o(0)
                add_y(0)
                split_h(0)
                with dve.Fori(0, B - 1) as b:
                    split_o(b + 1)
                    add_y(b + 1)
                    base_out(b)
                    split_h(b + 1)
                    dve.wait_ge(b_step, 2 * b + 2)
                base_out(B - 1)

                v = nc.vector
                v.tensor_copy(emap[:], emap_i[:]).then_inc(g_step, 1)
                dve.wait_ge(g_step, 1)
                v.tensor_tensor(sel[:], emap[:].rearrange("p (o n) -> p o n", o=1).broadcast_to([P, E, NR]),
                                expert[:].rearrange("p (e n) -> p e n", e=E), ALU.is_equal).then_inc(g_step, 1)
                dve.wait_ge(g_step, 2)
                dve.wait_ge(r_out, 2 * B)
                v.tensor_tensor(logits[:], logits[:], rbias[:].rearrange("p (o n) -> p o n", o=1).broadcast_to([P, NT, NR]),
                                ALU.add).then_inc(g_step, 6)
                dve.wait_ge(g_step, 8)
                v.tensor_reduce(top[:], logits[:], AX, ALU.max).then_inc(g_step, 1)
                dve.wait_ge(g_step, 9)
                v.tensor_tensor(e[:], logits[:], top[:].rearrange("p (t o) -> p t o", o=1).broadcast_to([P, NT, NR]),
                                ALU.subtract).then_inc(g_step, 1)
                dve.wait_ge(g_exp, 1)
                v.tensor_reduce(total[:], e[:], AX, ALU.add).then_inc(g_step, 1)
                dve.wait_ge(g_step, 11)
                v.reciprocal(total[:], total[:]).then_inc(g_step, 1)
                dve.wait_ge(g_step, 12)
                v.tensor_tensor(e[:], e[:], total[:].rearrange("p (t o) -> p t o", o=1).broadcast_to([P, NT, NR]),
                                ALU.mult).then_inc(g_step, 1)
                dve.wait_ge(g_step, 13)
                n = 13
                for c in range(0, NT, QT):
                    tiles = slice(c, c + QT)
                    keep_best(nc, dve, g_step, n, e[:, tiles], cmp_a[:], cmp_b[:], rank[:, tiles], keepers[:, tiles],
                              earlier[:], LORA1_E)
                    v.tensor_tensor(keepers[:, tiles], keepers[:, tiles], e[:, tiles], ALU.mult).then_inc(g_step, 1)
                    dve.wait_ge(g_step, n + 7)
                    weights = keepers[:, tiles].rearrange("p t (o n) -> p t o n", o=1).broadcast_to([P, QT, E, NR])
                    mine = sel[:].rearrange("p (o e) n -> p o e n", o=1).broadcast_to([P, QT, E, NR])
                    v.tensor_tensor(mixed[:], weights, mine, ALU.mult).then_inc(g_step, 1)
                    dve.wait_ge(g_step, n + 8)
                    v.tensor_reduce(wexp[:, tiles], mixed[:], AX, ALU.add).then_inc(g_step, 1)
                    dve.wait_ge(g_step, n + 9)
                    n += 9
                v.tensor_scalar(wexp[:], wexp[:], LORA1_SCALE, None, ALU.mult).then_inc(g_step, 1)
                dve.wait_ge(g_step, n + 1)
                for i in range(E):
                    m = keep.mid1[:, :, i * R:(i + 1) * R]
                    v.tensor_tensor(m, m, wexp[:, :, i:i + 1].broadcast_to([P, NT, R]), ALU.mult).then_inc(g_step, 1)

            @block.tensor
            def _(pe):
                def turn_o(b):
                    pe.wait_ge(o_in, 2 * b + 2)
                    for t in range(TT):
                        for k in range(KT):
                            mm = nc.tensor.transpose(norm.ps[:, k, t * P:(t + 1) * P], o[:, t, k * P:(k + 1) * P],
                                                     keep.ident[:])
                    mm.then_inc(o_turned, 1)

                def output(b):
                    pe.wait_ge(o_lo, b + 1)
                    for t in range(TT):
                        passes = [(a, r, k) for a, r in split_passes(oh, w[0]) for k in range(KT)]
                        for j, (a, r, k) in enumerate(passes):
                            mm = nc.tensor.matmul(ps_y[:, t], a[:, k, t * P:(t + 1) * P], r[:, k],
                                                  start=(j == 0), stop=(j == len(passes) - 1))
                    mm.then_inc(y_done, 1)

                def mixture(b):
                    pe.wait_ge(h_lo, b + 1)
                    for t in range(TT):
                        passes = [(a, r, k) for a, r in split_passes(hs, w[1]) for k in range(KT)]
                        for j, (a, r, k) in enumerate(passes):
                            mm = nc.tensor.matmul(ps_b[:, t], a[:, k, t * P:(t + 1) * P], r[:, k],
                                                  start=(j == 0), stop=(j == len(passes) - 1))
                    mm.then_inc(b_done, 1)
                    for t in range(TT):
                        for k in range(KT):
                            mm = nc.tensor.matmul(ps_r[:, t], norm.ht[:, k, t * P:(t + 1) * P], rl[:, k],
                                                  start=(k == 0), stop=(k == KT - 1))
                    mm.then_inc(r_done, 1)

                norm.start(pe)
                pe.wait_ge(w_lo, 2)
                pe.wait_ge(tab_in, 16 * 7)
                turn_o(0)
                output(0)
                norm.transposes(pe, 0)
                with pe.Fori(0, B - 1) as b:
                    pe.wait_ge(norm.ready, KT * b + KT)
                    turn_o(b + 1)
                    output(b + 1)
                    mixture(b)
                    norm.transposes(pe, b + 1)
                    pe.wait_ge(b_out, b + 2)
                    pe.wait_ge(r_out, 2 * b + 2)
                mixture(B - 1)


def phase_finish(nc, io, keep, out):
    with ExitStack() as ctx:
        def sb(name, shape, dt=F32):
            return ctx.enter_context(nc.sbuf_tensor(name, shape, dt))

        def sem(name):
            return ctx.enter_context(nc.semaphore(name))

        ER = LORA1_E * LORA1_R
        gates = sb("h_gates", [P, B, D])
        b1 = sb("h_b1", [ER, D])
        bs = [sb(f"h_bs{i}", [ER, D], F32R) for i in range(2)]
        mid = sb("h_mid", [P, TT, ER])
        ms = [sb(f"h_ms{i}", [ER, S], F32R) for i in range(2)]
        gated = sb("h_gated", [P, TT, D])
        ps_m = ctx.enter_context(nc.psum_tensor("h_ps_m", [ER, S], F32))
        ps_l = ctx.enter_context(nc.psum_tensor("h_ps_l", [P, TT, D], F32))

        g_in = sem("h_g_in")
        b_in = sem("h_b_in")
        b_hi = sem("h_b_hi")
        b_lo = sem("h_b_lo")
        mid_in = sem("h_mid_in")
        m_done = sem("h_m_done")
        m_hi = sem("h_m_hi")
        m_lo = sem("h_m_lo")
        l_done = sem("h_l_done")
        l_gated = sem("h_l_gated")
        summed = sem("h_summed")
        stored = sem("h_stored")

        with nc.Block() as block:
            @block.sync
            def _(sp):
                sp.dma_start(b1[:], io["b1"]).then_inc(b_in, 16)
                for b in range(B):
                    sp.dma_start(gates[:, b], keep.gates[3, b:b + 1].partition_broadcast(P)).then_inc(g_in, 16)
                with sp.Fori(0, B) as b:
                    sp.wait_ge(summed, b + 2)
                    sp.dma_start(out[bass.ds(b, 1)].rearrange("o p t d -> p (o t) d"), element(keep.acc, b)).then_inc(stored, 16)
                sp.wait_ge(stored, 16 * B)

            @block.scalar
            def _(act):
                act.wait_ge(b_in, 16)
                nc.scalar.activation(bs[0][:], b1[:], ACT.Identity).then_inc(b_hi, 1)
                with act.Fori(0, B) as b:
                    nc.scalar.activation(mid[:], element(keep.mid1, b), ACT.Identity).then_inc(mid_in, 1)
                    act.wait_ge(m_done, b + 1)
                    nc.scalar.activation(ms[0][:], ps_m[:], ACT.Identity).then_inc(m_hi, 1)

            @block.vector
            def _(dve):
                dve.wait_ge(b_hi, 1)
                nc.vector.tensor_tensor(bs[1][:], b1[:], f32(bs[0][:]), ALU.subtract).then_inc(b_lo, 1)
                dve.wait_ge(g_in, 16 * B)
                with dve.Fori(0, B) as b:
                    dve.wait_ge(m_hi, b + 1)
                    nc.vector.tensor_tensor(ms[1][:], ps_m[:], f32(ms[0][:]), ALU.subtract).then_inc(m_lo, 1)
                    dve.wait_ge(l_done, b + 1)
                    dve.wait_ge(summed, b + 1)
                    g = gates[:, bass.ds(b, 1)].broadcast_to([P, TT, D])
                    nc.vector.tensor_tensor(gated[:], ps_l[:], g, ALU.mult).then_inc(l_gated, 1)

            @block.gpsimd
            def _(pool):
                pool.sem_inc(summed, 1)
                with pool.Fori(0, B) as b:
                    pool.wait_ge(l_gated, b + 1)
                    x = element(keep.acc, b)
                    nc.gpsimd.tensor_tensor(x, x, gated[:], ALU.add).then_inc(summed, 1)

            @block.tensor
            def _(pe):
                pe.wait_ge(b_lo, 1)
                with pe.Fori(0, B) as b:
                    pe.wait_ge(mid_in, b + 1)
                    for t in range(TT):
                        mm = nc.tensor.transpose(ps_m[:, t * P:(t + 1) * P], mid[:, t], keep.ident[:])
                    mm.then_inc(m_done, 1)
                    pe.wait_ge(m_lo, b + 1)
                    for t in range(TT):
                        for j, (a, r) in enumerate(split_passes(ms, bs)):
                            mm = nc.tensor.matmul(ps_l[:, t], a[:, t * P:(t + 1) * P], r[:], start=(j == 0), stop=(j == 2))
                    mm.then_inc(l_done, 1)
                    pe.wait_ge(l_gated, b + 1)


def build(nc, io, out):
    with ExitStack() as ctx:
        def sb(name, shape, dt=F32):
            return ctx.enter_context(nc.sbuf_tensor(name, shape, dt))

        def right(stack, name, shape):
            return stack.enter_context(nc.sbuf_tensor(name, shape, F32, side="right"))

        def scratch(name, shape, dt=F32):
            return nc.dram_tensor(name, shape, dt, kind="Internal").ap()

        k_parts = [scratch(f"k{i}_dram", [G0 * B, P, S]) for i in range(2)]
        v_parts = [scratch(f"v{i}_dram", [G0 * B, P, TT, HD0]) for i in range(2)]
        keep = Kept()
        keep.gates = scratch("gates", [4, B, D])
        keep.v1_dram = scratch("values1_dram", [P, 8 * B, TT, D // 8])
        keep.k, keep.v = k_parts, v_parts
        keep.k_by_element = [t.rearrange("(g b) p s -> b p g s", b=B) for t in k_parts]
        keep.v_by_element = [t.rearrange("(g b) p t c -> b p t g c", b=B) for t in v_parts]
        keep.mod = sb("mod", [P, 2, 4, KT, B])
        keep.ident, keep.eps = sb("ident", [P, P]), sb("eps", [P, 1])
        keep.ident_b, keep.mask_b = sb("ident_b", [P, P], BF16), sb("mask_b", [P, P], BF16)
        keep.qcos, keep.qsin = (sb(name, [P, S]) for name in ("qcos", "qsin"))
        mask = sb("mask", [P, P])
        table_in = ctx.enter_context(nc.semaphore("table_in"))
        eps_set = ctx.enter_context(nc.semaphore("eps_set"))
        with nc.Block() as block:
            @block.sync
            def _(sp):
                sp.dma_start(keep.ident[:], io["ident"]).then_inc(table_in, 16)
                sp.dma_start(mask[:], io["mask"]).then_inc(table_in, 16)
                sp.dma_start(keep.qcos[:], io["qcos"]).then_inc(table_in, 16)
                sp.dma_start(keep.qsin[:], io["qsin"]).then_inc(table_in, 16)

            @block.vector
            def _(dve):
                nc.vector.memset(keep.eps[:], EPS).then_inc(eps_set, 1)
                dve.wait_ge(table_in, 64)
                nc.vector.tensor_copy(keep.ident_b[:], keep.ident[:]).then_inc(eps_set, 1)
                nc.vector.tensor_copy(keep.mask_b[:], mask[:]).then_inc(eps_set, 1)


        with ExitStack() as tokens:
            keep.ht_hi, keep.ht_lo = (tokens.enter_context(nc.sbuf_tensor(name, [P, B, KT, S], F32R)) for name in ("ht_hi", "ht_lo"))
            with ExitStack() as split_weights:
                keep.wk_hi, keep.wk_lo, keep.wv_hi, keep.wv_lo = (
                    split_weights.enter_context(nc.sbuf_tensor(name, [P, KT, 2 * D], F32R))
                    for name in ("wk_hi", "wk_lo", "wv_hi", "wv_lo"))
                phase_setup(nc, io, keep)
                phase_keys(nc, io, keep)
            keep.acc = right(ctx, "x_stream", [P, NT, D])
            phase_attention0(nc, io, keep)
        keep.mid0 = right(ctx, "mid0", [P, NT, LORA0_E * LORA0_R])
        phase_router0(nc, io, keep)
        with ExitStack() as heads:
            keep.q1, keep.k1 = (heads.enter_context(nc.sbuf_tensor(n, [P, 8 * B, TT, D // 8], F32)) for n in ("queries1", "keys1"))
            phase_queries1(nc, io, keep)
            keep.o1 = right(ctx, "o1", [P, 8 * B, TT, D // 8])
            phase_attention1(nc, io, keep)
        keep.mid1 = right(ctx, "mid1", [P, NT, LORA1_E * LORA1_R])
        phase_router1(nc, io, keep)
        phase_finish(nc, io, keep, out)


def tables():
    q = np.arange(P)
    mask = np.where(q[None, :] > q[:, None], NEG, 0.0).astype(np.float32)
    inv = 1.0 / THETA ** (np.arange(0, HD0, 2, dtype=np.float32) / HD0)
    angle = np.outer(np.arange(S, dtype=np.float32), inv).T
    cos, sin = np.cos(angle), np.sin(angle)
    half = np.concatenate([cos, cos]), np.concatenate([sin, -sin])
    rotated = (np.arange(P) % HB0 < ROPE0)[:, None]
    inv1 = 1.0 / THETA ** (np.arange(0, HD1, 2, dtype=np.float32) / HD1)
    angle1 = np.outer(np.arange(S, dtype=np.float32), inv1)
    cos1 = np.concatenate([np.cos(angle1)] * 2, 1).reshape(TT, P, HD1).transpose(1, 0, 2)
    sin1 = np.concatenate([-np.sin(angle1), np.sin(angle1)], 1).reshape(TT, P, HD1).transpose(1, 0, 2)

    def earlier(n):
        return np.tile(np.tril(np.ones((n, n), np.float32), -1).reshape(1, -1), (P, 1))

    return {
        "cos1": cos1.astype(np.float32), "sin1": sin1.astype(np.float32),
        "earlier0": earlier(LORA0_E), "earlier1": earlier(NR),
        "expert": np.tile(np.repeat(np.arange(LORA1_E, dtype=np.float32), NR)[None], (P, 1)),
        "ident": np.eye(P, dtype=np.float32), "mask": mask,
        "qcos": half[0].astype(np.float32), "qsin": half[1].astype(np.float32),
        "kcos": np.where(rotated, half[0], 1.0).astype(np.float32),
        "ksin": np.where(rotated, half[1], 0.0).astype(np.float32),
    }


def by_partition(w):
    w = np.asarray(w)
    return np.ascontiguousarray(w.reshape(-1, P, w.shape[-1]).transpose(1, 0, 2))


def layouts(a):
    wq = np.asarray(a["L0_attn_Wq"]).T.reshape(KT, P, G0, 2, D // 2)
    wo = np.asarray(a["L0_attn_Wo"]).T.reshape(G0, HG, P, 2, D // 2)
    m = {
        "x": np.asarray(a["L0_attn_hidden_states"]),
        "c0": by_partition(np.asarray(a["L0_c"]).T), "c1": by_partition(np.asarray(a["L1_c"]).T),
        "wmod0": by_partition(a["L0_wmod"]), "wmod1": by_partition(a["L1_wmod"]),
        "wdk": by_partition(a["L0_attn_Wdk"]),
        "wupk": by_partition(np.asarray(a["L0_attn_Wupk"]).T),
        "wupv": by_partition(np.asarray(a["L0_attn_Wupv"]).T),
        "wkr": by_partition(np.asarray(a["L0_attn_Wkr"]).T),
        "wq_pieces": np.ascontiguousarray(wq.transpose(2, 0, 3, 1, 4)).reshape(G0 * B, P, D // 2),
        "wo_pieces": np.ascontiguousarray(wo.transpose(0, 1, 3, 2, 4)).reshape(G0 * B, P, D // 2),
    }
    order = np.arange(D).reshape(H1, HD1 // 2, 2).transpose(0, 2, 1).reshape(-1)
    m.update({
        "router0": by_partition(np.asarray(a["L0_ffn_router_w"]).T),
        "a0": by_partition(np.asarray(a["L0_ffn_A"]).reshape(-1, D).T),
        "b0": np.asarray(a["L0_ffn_B"]).transpose(0, 2, 1).reshape(-1, D),
        "wq1": by_partition(np.asarray(a["L1_attn_wq"])[:, order]),
        "wk1": by_partition(np.asarray(a["L1_attn_wk"])[:, order]),
        "wv1": by_partition(a["L1_attn_wv"]), "wo1": by_partition(a["L1_attn_wo"]),
        "base_w": by_partition(np.asarray(a["L1_ffn_base_W"]).T),
        "base_b": np.asarray(a["L1_ffn_base_b"]).reshape(1, -1),
        "router1": by_partition(np.asarray(a["L1_ffn_router_W"]).T),
        "router_b": np.asarray(a["L1_ffn_router_b"]).reshape(1, -1),
        "a1": by_partition(np.asarray(a["L1_ffn_A"]).reshape(-1, D).T),
        "b1": np.asarray(a["L1_ffn_B"]).transpose(0, 2, 1).reshape(-1, D),
        "expert_map": np.asarray(a["L1_ffn_expert_map"]).reshape(1, -1),
    })
    m.update(tables())
    return {k: np.ascontiguousarray(v) for k, v in m.items()}


def kernel(**inputs):
    import concourse.bacc as bacc
    from concourse.bass_utils import run_bass_kernel_spmd

    nc = bacc.Bacc("TRN2", target_bir_lowering=False, num_devices=1)
    arrays = layouts(inputs)
    io = {k: nc.dram_tensor(f"in_{k}", v.shape, mybir.dt.from_np(v.dtype), kind="ExternalInput").ap()
          for k, v in arrays.items()}
    io["x"] = io["x"].rearrange("b (t p) d -> b p t d", p=P)
    io["wmod"] = [io["wmod0"], io["wmod1"]]
    out = nc.dram_tensor("out_x", [B * S, D], F32, kind="ExternalOutput").ap()
    build(nc, io, out.rearrange("(b t p) d -> b p t d", p=P, t=TT))
    result = run_bass_kernel_spmd(nc, [{f"in_{k}": v for k, v in arrays.items()}], core_ids=[0])
    return result.results[0]["out_x"].reshape(B, S, D)
```

```python
from contextlib import ExitStack

import numpy as np

import concourse.bass as bass
from concourse import mybir

F32 = mybir.dt.float32
F32R = mybir.dt.float32r
BF16 = mybir.dt.bfloat16
I32 = mybir.dt.int32
ALU = mybir.AluOpType
ACT = mybir.ActivationFunctionType
AX = mybir.AxisListType.X

P = 128
B, S, D = 8, 256, 512
KT = D // P
TT = S // P
NT = B * TT
EPS = 1e-5

H0, G0, HD0 = 32, 8, 128
HG = H0 // G0
SCALE0 = HD0 ** -0.5
ROPE0 = 32
HB0 = HD0 // 2
LORA0_E, LORA0_R, LORA0_SCALE = 4, 16, 4.0
NEG = -1.0e30

H1 = 32
HD1 = D // H1
SCALE1 = HD1 ** -0.5
LORA1_E, LORA1_R, LORA1_SCALE = 8, 16, 2.0
NR = 2 * LORA1_E - 1

THETA = 10000.0
GATE_MIN = 0.25


def f32(ap):
    return ap.bitcast(F32)


def pair(table):
    n, w = table.shape
    return table.rearrange("p (o s) -> p o s", o=1).broadcast_to([n, 2, w])


class Kept:
    pass


def phase_setup(nc, io, keep):
    with ExitStack() as ctx:
        def sb(name, shape, dt=F32):
            return ctx.enter_context(nc.sbuf_tensor(name, shape, dt))

        def sem(name):
            return ctx.enter_context(nc.semaphore(name))

        cond = sb("cond", [P, 2, KT, B])
        cond_e = sb("cond_e", [P, 2, KT, B])
        cond_s = sb("cond_s", [P, 2, KT, B])
        NW = 3
        wmod = [nc.alloc_sbuf_tensor_at(f"wmod{i}", [P, KT, D], F32, offset=keep.tokens_at + i * KT * D * 4) for i in range(NW)]
        wdk = sb("wdk", [P, KT, D])
        wup = [sb(f"wup{i}", [P, KT, D]) for i in range(2)]
        wkr = sb("wkr", [P, KT, D])
        mod_raw = sb("mod_raw", [B, 12, D])
        gate_sign = sb("gate_sign", [B, 2, D])
        gate_mag = sb("gate_mag", [B, 2, D])
        ps_mod = [ctx.enter_context(nc.psum_tensor(f"ps_mod{i}", [P, D], F32)) for i in range(2)]
        ps_vec = ctx.enter_context(nc.psum_tensor("ps_vec", [P, 2, 4, KT, B], F32))
        ps_w = [ctx.enter_context(nc.psum_tensor(f"ps_w{i}", [P, D], F32)) for i in range(2)]

        cond_in = sem("cond_in")
        wmod_in = [sem(f"wmod_in{i}") for i in range(NW)]
        wup_in = [sem(f"wup_in{i}") for i in range(3)]
        silu_step = sem("silu_step")
        mod_done = sem("mod_done")
        mod_taken = sem("mod_taken")
        prod_done = sem("prod_done")
        prod_hi = sem("prod_hi")
        prod_lo = sem("prod_lo")
        kr_hi = sem("kr_hi")
        gate_step = sem("gate_step")
        gate_out_done = sem("gate_out_done")

        mods = [(l, v) for l in range(2) for v in (0, 1, 2, 3, 4, 5)]
        vectors = (0, 1, 3, 4)
        prods = [(m, h) for h in (None, 0, 1) for m in range(KT)]

        with nc.Block() as block:
            @block.sync
            def _(sp):
                sp.dma_start(cond[:, 0], io["c0"]).then_inc(cond_in, 16)
                sp.dma_start(cond[:, 1], io["c1"]).then_inc(cond_in, 16)
                sp.dma_start(wdk[:], io["wdk"]).then_inc(wup_in[0], 16)
                sp.dma_start(wup[0][:], io["wupk"]).then_inc(wup_in[0], 16)
                sp.dma_start(wkr[:], io["wkr"]).then_inc(cond_in, 16)
                sp.dma_start(wup[1][:], io["wupv"][:, :, 0:D]).then_inc(wup_in[1], 16)
                for n, (l, v) in enumerate(mods):
                    if n == 2:
                        sp.wait_ge(prod_done, KT)
                        sp.dma_start(wup[0][:], io["wupv"][:, :, D:2 * D]).then_inc(wup_in[2], 16)
                    if n >= NW:
                        sp.wait_ge(mod_done, n - NW + 1)
                    sp.dma_start(wmod[n % NW][:], io["wmod"][l][:, :, v * D:(v + 1) * D]).then_inc(wmod_in[n % NW], 16)
                sp.wait_ge(gate_step, 10)
                sp.dma_start(keep.gates.rearrange("n b d -> b n d"), mod_raw[:, 2:12:3]).then_inc(gate_out_done, 16)
                sp.wait_ge(gate_out_done, 16)

            @block.scalar
            def _(act):
                act.wait_ge(cond_in, 48)
                nc.scalar.activation(cond_e[:], cond[:], ACT.Exp, scale=-1.0).then_inc(silu_step, 1)
                for n, (m, h) in enumerate(prods):
                    act.wait_ge(prod_done, n + 1)
                    src = ps_w[n % 2][:]
                    if h is None:
                        dst = keep.wk_hi[:, m].rearrange("p (g q c) -> p g q c", g=G0, q=4)[:, :, 1:4:2, :]
                        src = src.rearrange("p (g q c) -> p g q c", g=G0, q=2)
                    else:
                        dst = keep.wv_hi[:, m, h * D:(h + 1) * D]
                    nc.scalar.activation(dst, src, ACT.Copy).then_inc(prod_hi, 1)
                for m in range(KT):
                    dst = keep.wk_hi[:, m].rearrange("p (g q c) -> p g q c", g=G0, q=4)[:, :, 0:4:2, :]
                    nc.scalar.activation(dst, wkr[:, m].rearrange("p (g q c) -> p g q c", g=G0, q=2),
                                         ACT.Copy).then_inc(kr_hi, 1)

            @block.tensor
            def _(pe):
                for n, (m, h) in enumerate(prods):
                    if m == 0:
                        pe.wait_ge(*((wup_in[0], 32) if h is None else (wup_in[1 + h], 16)))
                    if n >= 2:
                        pe.wait_ge(prod_lo, n - 1)
                        pe.wait_ge(prod_hi, n - 1)
                    rhs = wup[1 if h == 0 else 0]
                    for k in range(KT):
                        mm = nc.tensor.matmul(ps_w[n % 2][:], wdk[:, k, m * P:(m + 1) * P],
                                              rhs[:, k, :], start=(k == 0), stop=(k == KT - 1))
                    mm.then_inc(prod_done, 1)
                pe.wait_ge(silu_step, 4)
                for n, (l, v) in enumerate(mods):
                    pe.wait_ge(wmod_in[n % NW], 16 * (n // NW + 1))
                    if n >= 2:
                        pe.wait_ge(mod_taken, n - 1)
                    for k in range(KT):
                        mm = nc.tensor.matmul(ps_mod[n % 2][0:B], cond_s[:, l, k], wmod[n % NW][:, k],
                                              start=(k == 0), stop=(k == KT - 1))
                    mm.then_inc(mod_done, 1)
                pe.wait_ge(mod_taken, len(mods))
                for l in range(2):
                    for i, v in enumerate(vectors):
                        for k in range(KT):
                            mm = nc.tensor.transpose(ps_vec[:, l, i, k], mod_raw[:, 6 * l + v, k * P:(k + 1) * P],
                                                     keep.ident[0:B, 0:B])
                mm.then_inc(mod_done, 1)

            @block.vector
            def _(dve):
                def guard_gates(l):
                    g = mod_raw[:, 6 * l + 2:6 * l + 6:3]
                    n = 5 * l
                    dve.wait_ge(mod_taken, 6 * l + 6)
                    nc.vector.tensor_scalar(gate_sign[:], g, 0.0, 2.0, ALU.is_ge, ALU.mult).then_inc(gate_step, 1)
                    nc.vector.tensor_scalar(gate_mag[:], g, -1.0, None, ALU.mult).then_inc(gate_step, 1)
                    dve.wait_ge(gate_step, n + 2)
                    nc.vector.tensor_tensor(gate_mag[:], g, gate_mag[:], ALU.max).then_inc(gate_step, 1)
                    dve.wait_ge(gate_step, n + 3)
                    nc.vector.tensor_scalar(gate_mag[:], gate_mag[:], GATE_MIN, None, ALU.max).then_inc(gate_step, 1)
                    dve.wait_ge(gate_step, n + 4)
                    nc.vector.scalar_tensor_tensor(g, gate_sign[:], 1.0, gate_mag[:],
                                                   ALU.subtract, ALU.mult).then_inc(gate_step, 1)
                    dve.wait_ge(gate_step, n + 5)

                dve.wait_ge(silu_step, 1)
                nc.vector.tensor_scalar(cond_e[:], cond_e[:], 1.0, None, ALU.add).then_inc(silu_step, 1)
                dve.wait_ge(silu_step, 2)
                nc.vector.reciprocal(cond_s[:], cond_e[:]).then_inc(silu_step, 1)
                dve.wait_ge(silu_step, 3)
                nc.vector.tensor_tensor(cond_s[:], cond_s[:], cond[:], ALU.mult).then_inc(silu_step, 1)
                for n, (m, h) in enumerate(prods):
                    dve.wait_ge(prod_hi, n + 1)
                    src = ps_w[n % 2][:]
                    if h is None:
                        parts = [t[:, m].rearrange("p (g q c) -> p g q c", g=G0, q=4)[:, :, 1:4:2, :]
                                 for t in (keep.wk_hi, keep.wk_lo)]
                        src = src.rearrange("p (g q c) -> p g q c", g=G0, q=2)
                    else:
                        parts = [t[:, m, h * D:(h + 1) * D] for t in (keep.wv_hi, keep.wv_lo)]
                    nc.vector.tensor_tensor(parts[1], src, f32(parts[0]), ALU.subtract).then_inc(prod_lo, 1)
                for m in range(KT):
                    dve.wait_ge(kr_hi, m + 1)
                    parts = [t[:, m].rearrange("p (g q c) -> p g q c", g=G0, q=4)[:, :, 0:4:2, :]
                             for t in (keep.wk_hi, keep.wk_lo)]
                    nc.vector.tensor_tensor(parts[1], wkr[:, m].rearrange("p (g q c) -> p g q c", g=G0, q=2),
                                            f32(parts[0]), ALU.subtract)
                for n, (l, v) in enumerate(mods):
                    dve.wait_ge(mod_done, n + 1)
                    nc.vector.tensor_copy(mod_raw[:, n], ps_mod[n % 2][0:B]).then_inc(mod_taken, 1)
                    if v == 5:
                        guard_gates(l)
                dve.wait_ge(mod_done, len(mods) + 1)
                for i in range(4):
                    nc.vector.tensor_scalar(keep.mod[:, :, i], ps_vec[:, :, i], float(i % 2), None, ALU.add)


def phase_keys(nc, io, keep):
    with ExitStack() as ctx:
        def sb(name, shape, dt=F32):
            return ctx.enter_context(nc.sbuf_tensor(name, shape, dt))

        def sem(name):
            return ctx.enter_context(nc.semaphore(name))

        x = sb("x_in", [P, TT, D])
        stats = sb("ln_stats", [P, TT, 6])
        mv = sb("ln_mv", [P, TT, 2])
        std = sb("ln_std", [P, TT])
        rstd = sb("ln_rstd", [P, TT])
        xn = sb("xn", [P, TT, D])
        ht = sb("ht", [P, KT, S])
        hs = [sb(f"hs{i}", [P, KT, S], F32R) for i in range(2)]
        cos = sb("kcos", [P, S])
        sin = sb("ksin", [P, S])
        krot = [sb(f"k_rot{n}", [P, 2, S]) for n in range(2)]
        kswap = [sb(f"k_swap{n}", [P, 2, S]) for n in range(2)]
        kp = [[sb(f"k_part{i}{n}", [P, 2, S], F32R) for n in range(2)] for i in range(2)]
        vp = [sb(f"v_part{i}", [P, TT, 2 * D], F32R) for i in range(2)]
        ps_t = ctx.enter_context(nc.psum_tensor("ps_t", [P, KT, S], F32))
        ps_k = [ctx.enter_context(nc.psum_tensor(f"ps_k{i}", [P, 2, S], F32)) for i in range(2)]
        ps_v = [ctx.enter_context(nc.psum_tensor(f"ps_v{i}", [P, D], F32)) for i in range(2)]

        rot_in = sem("rot_in")
        x_in = sem("x_in_s")
        ln_step = sem("ln_step")
        ln_sqrt = sem("ln_sqrt")
        t_done = sem("t_done")
        ht_done = sem("ht_done")
        hi_done = sem("hi_done")
        lo_done = sem("lo_done")
        kept = sem("kept")
        v_done = sem("v_done")
        v_hi = sem("v_hi")
        v_lo = sem("v_lo")
        v_out = sem("v_out")
        k_done = sem("k_done")
        k_cos = sem("k_cos_s")
        k_rot = sem("k_rot_s")
        k_hi = sem("k_hi")
        k_lo = sem("k_lo")
        k_out = [sem(f"k_out{n}") for n in range(2)]

        NP = G0 // 2
        NV = TT * 2

        with nc.Block() as block:
            @block.sync
            def _(sp):
                for s in k_out:
                    sp.sem_inc(s, 32)
                sp.dma_start(x[:], io["x"][0]).then_inc(x_in, 16)
                sp.dma_start(cos[:], io["kcos"]).then_inc(rot_in, 16)
                sp.dma_start(sin[:], io["ksin"]).then_inc(rot_in, 16)

                def stores(b):
                    sp.wait_ge(lo_done, b + 1)
                    sp.wait_ge(hi_done, b + 1)
                    sp.dma_start(f32(keep.ht_hi[:, bass.ds(b, 1)]), f32(hs[0][:].rearrange("p (o k) s -> p o k s", o=1))).then_inc(kept, 16)
                    sp.dma_start(f32(keep.ht_lo[:, bass.ds(b, 1)]), f32(hs[1][:].rearrange("p (o k) s -> p o k s", o=1))).then_inc(kept, 16)

                def store_values(b):
                    sp.wait_ge(v_lo, NV * (b + 1))
                    for i in range(2):
                        for t in range(TT):
                            sp.dma_start(keep.v_by_element[i][bass.ds(b, 1), :, t].rearrange("o p g c -> p (o g) c"),
                                         f32(vp[i][:, t].rearrange("p (g c) -> p g c", g=G0))).then_inc(v_out, 16)

                def store_keys(b):
                    for g in range(NP):
                        sp.wait_ge(k_lo, NP * b + g + 3)
                        for i in range(2):
                            sp.dma_start(keep.k_by_element[i][bass.ds(b, 1), :, 2 * g:2 * g + 2].rearrange("o p g s -> p (o g) s"),
                                         f32(kp[i][g % 2][:])).then_inc(k_out[g % 2], 16)

                def load_x(b):
                    sp.wait_ge(ln_step, 7 * b)
                    sp.dma_start(x[:], io["x"][bass.ds(b, 1)].rearrange("o p t d -> p (o t) d")).then_inc(x_in, 16)

                load_x(1)
                stores(0)
                with sp.Fori(0, B - 2) as b:
                    store_values(b)
                    load_x(b + 2)
                    stores(b + 1)
                    store_keys(b)
                store_values(B - 2)
                stores(B - 1)
                store_keys(B - 2)
                store_values(B - 1)
                store_keys(B - 1)
                sp.wait_ge(kept, 32 * B)
                sp.wait_ge(v_out, 64 * B)
                for s in k_out:
                    sp.wait_ge(s, 32 * (NP // 2 * B) + 32)

            @block.vector
            def _(dve):
                def statistics(b):
                    n = 7 * b
                    dve.wait_ge(x_in, 16 * (b + 1))
                    for t in range(TT):
                        nc.vector.bn_stats(stats[:, t], x[:, t]).then_inc(ln_step, 1)
                    dve.wait_ge(ln_step, n + 2)
                    nc.vector.memset(rstd[:], 0.0)
                    for t in range(TT):
                        nc.vector.bn_aggr(mv[:, t], stats[:, t]).then_inc(ln_step, 1)

                def normalize(b):
                    n = 7 * b
                    dve.wait_ge(ln_sqrt, b + 1)
                    nc.vector.reciprocal(rstd[:], std[:]).then_inc(ln_step, 1)
                    dve.wait_ge(ln_step, n + 5)
                    for t in range(TT):
                        nc.vector.tensor_scalar(xn[:, t], x[:, t], mv[:, t, 0:1], rstd[:, t:t + 1],
                                                ALU.subtract, ALU.mult).then_inc(ln_step, 1)

                def split_h(b):
                    dve.wait_ge(hi_done, b + 1)
                    nc.vector.tensor_tensor(hs[1][:], ht[:], f32(hs[0][:]), ALU.subtract).then_inc(lo_done, 1)

                def rest_of_values(b, tiles):
                    for n in tiles:
                        dve.wait_ge(v_hi, NV * b + n + 1)
                        t, h = n // 2, n % 2
                        nc.vector.tensor_tensor(vp[1][:, t, h * D:(h + 1) * D], ps_v[n % 2][:],
                                                f32(vp[0][:, t, h * D:(h + 1) * D]), ALU.subtract).then_inc(v_lo, 1)

                def rotate(b, g):
                    dve.wait_ge(k_done, NP * b + g + 1)
                    dve.wait_ge(k_lo, NP * b + g + 1)
                    src, rot, swap = ps_k[g % 2], krot[g % 2], kswap[g % 2]
                    nc.vector.tensor_tensor(rot[:], src[:], pair(cos[:]), ALU.mult)
                    nc.vector.tensor_tensor(swap[0:HB0], src[HB0:P], pair(sin[HB0:P]), ALU.mult)
                    nc.vector.tensor_tensor(swap[HB0:P], src[0:HB0], pair(sin[0:HB0]), ALU.mult).then_inc(k_cos, 1)

                def rest_of_keys(b, g):
                    dve.wait_ge(k_hi, NP * b + g + 1)
                    nc.vector.tensor_tensor(kp[1][g % 2][:], krot[g % 2][:], f32(kp[0][g % 2][:]), ALU.subtract).then_inc(k_lo, 1)

                def keys(b):
                    for g in range(1, NP):
                        rotate(b, g)
                        rest_of_keys(b, g - 1)
                    rest_of_keys(b, NP - 1)

                dve.sem_inc(k_cos, 2)
                dve.sem_inc(k_lo, 2)
                statistics(0)
                normalize(0)
                split_h(0)
                dve.wait_ge(rot_in, 32)
                with dve.Fori(0, B - 1) as b:
                    rest_of_values(b, (0, 1))
                    statistics(b + 1)
                    rest_of_values(b, (2,))
                    dve.wait_ge(t_done, b + 1)
                    normalize(b + 1)
                    rest_of_values(b, (3,))
                    rotate(b, 0)
                    dve.wait_ge(kept, 32 * (b + 1))
                    dve.wait_ge(v_done, NV * (b + 1))
                    split_h(b + 1)
                    keys(b)
                rest_of_values(B - 1, range(NV))
                rotate(B - 1, 0)
                keys(B - 1)

            @block.scalar
            def _(act):
                def roots(b):
                    act.wait_ge(ln_step, 7 * b + 4)
                    nc.scalar.activation(std[:], mv[:, :, 1], ACT.Sqrt, bias=keep.eps[:, 0:1]).then_inc(ln_sqrt, 1)

                def modulate(b):
                    act.wait_ge(t_done, b + 1)
                    for k in range(KT):
                        nc.scalar.activation(ht[:, k], ps_t[:, k], ACT.Identity,
                                             bias=keep.mod[:, 0, 0, k, bass.ds(b, 1)],
                                             scale=keep.mod[:, 0, 1, k, bass.ds(b, 1)]).then_inc(ht_done, 1)
                    act.wait_ge(ht_done, KT * (b + 1))
                    nc.scalar.activation(hs[0][:], ht[:], ACT.Identity).then_inc(hi_done, 1)

                def values(b, tiles):
                    for n in tiles:
                        act.wait_ge(v_done, NV * b + n + 1)
                        t, h = n // 2, n % 2
                        nc.scalar.activation(vp[0][:, t, h * D:(h + 1) * D], ps_v[n % 2][:], ACT.Identity).then_inc(v_hi, 1)

                def keys(b):
                    for g in range(NP):
                        act.wait_ge(k_rot, NP * b + g + 1)
                        act.wait_ge(k_out[g % 2], 32 * (NP // 2 * b + g // 2) + 32)
                        nc.scalar.activation(kp[0][g % 2][:], krot[g % 2][:], ACT.Identity).then_inc(k_hi, 1)

                nc.scalar.preload_act_table(ACT.Sqrt)
                roots(0)
                modulate(0)
                with act.Fori(0, B - 1) as b:
                    values(b, (0, 1))
                    roots(b + 1)
                    values(b, (2, 3))
                    act.wait_ge(kept, 32 * (b + 1))
                    act.wait_ge(v_done, NV * (b + 1))
                    modulate(b + 1)
                    keys(b)
                    act.wait_ge(v_out, 64 * (b + 1))
                values(B - 1, range(NV))
                keys(B - 1)

            @block.gpsimd
            def _(pool):
                with pool.Fori(0, B) as b:
                    for g in range(NP):
                        pool.wait_ge(k_cos, NP * b + g + 3)
                        nc.gpsimd.tensor_tensor(krot[g % 2][:], krot[g % 2][:], kswap[g % 2][:], ALU.add).then_inc(k_rot, 1)

            @block.tensor
            def _(pe):
                def transposes(b):
                    pe.wait_ge(ln_step, 7 * b + 7)
                    for t in range(TT):
                        for k in range(KT):
                            mm = nc.tensor.transpose(ps_t[:, k, t * P:(t + 1) * P], xn[:, t, k * P:(k + 1) * P],
                                                     keep.ident[:])
                    mm.then_inc(t_done, 1)

                def values(b):
                    pe.wait_ge(lo_done, b + 1)
                    for n in range(NV):
                        t, h = n // 2, n % 2
                        if n >= 2:
                            pe.wait_ge(v_lo, NV * b + n - 1)
                        passes = [(hs[i], w, k) for i, w in ((0, keep.wv_hi), (1, keep.wv_hi), (0, keep.wv_lo)) for k in range(KT)]
                        for j, (a, w, k) in enumerate(passes):
                            mm = nc.tensor.matmul(ps_v[n % 2][:], a[:, k, t * P:(t + 1) * P], w[:, k, h * D:(h + 1) * D],
                                                  start=(j == 0), stop=(j == len(passes) - 1))
                        mm.then_inc(v_done, 1)

                def keys(b):
                    pe.wait_ge(kept, 32 * (b + 1))
                    for g in range(NP):
                        pe.wait_ge(k_cos, NP * b + g + 1)
                        for e in range(2):
                            passes = [(w, r, k) for w, r in ((keep.wk_hi, keep.ht_hi), (keep.wk_lo, keep.ht_hi), (keep.wk_hi, keep.ht_lo))
                                      for k in range(KT)]
                            for j, (w, r, k) in enumerate(passes):
                                mm = nc.tensor.matmul(ps_k[g % 2][:, e], w[:, k, (2 * g + e) * P:(2 * g + e + 1) * P],
                                                      r[:, bass.ds(b, 1), k].rearrange("p o s -> p (o s)"), start=(j == 0), stop=(j == len(passes) - 1))
                        mm.then_inc(k_done, 1)

                transposes(0)
                with pe.Fori(0, B - 1) as b:
                    values(b)
                    transposes(b + 1)
                    keys(b)
                    pe.wait_ge(v_lo, NV * (b + 1))
                values(B - 1)
                keys(B - 1)


def phase_attention0(nc, io, keep):
    U = G0 * B
    with ExitStack() as ctx:
        def sb(name, shape, dt=F32):
            return ctx.enter_context(nc.sbuf_tensor(name, shape, dt))

        def sem(name):
            return ctx.enter_context(nc.semaphore(name))

        shared_at = -(-nc.sbuf_base // 32) * 32
        pt = [sb(f"pt{i}", [P, 3, HG * P], F32R) for i in range(2)]
        W = KT * D
        WP = W // B
        WO_LATE = 2
        wq = [sb(f"wq{i}", [P, 2 * W], F32R) for i in range(2)]
        wo = [sb(f"wo{i}", [P, 2 * W], F32R) for i in range(2)]
        wq_new = sb("wq_new", [P, WP])
        wo_new = sb("wo_new", [P, WP])
        kk = [sb(f"kk{i}", [P, S], F32R) for i in range(2)]
        vv = [sb(f"vv{i}", [P, TT, HD0], F32R) for i in range(2)]
        qrot = [sb(f"q_rot{i}", [P, 2, S]) for i in range(2)]
        qswap = [sb(f"q_swap{i}", [P, 2, S]) for i in range(2)]
        q = [sb(f"q{i}", [P, HG, S], F32R) for i in range(2)]
        prob = nc.alloc_sbuf_tensor_at("prob", [P, 3 * HG * P], F32, offset=shared_at)
        row_max = sb("row_max", [P, 2, HG])
        neg_max = sb("neg_max", [P, 2, HG])
        row_sum = sb("row_sum", [P, 2, HG])
        inv_sum = sb("inv_sum", [P, 2, HG])
        ot = [sb(f"ot{i}", [P, TT, HG * P], F32R) for i in range(2)]
        ps_q = [ctx.enter_context(nc.psum_tensor(f"ps_q{i}", [P, 2, S], F32)) for i in range(2)]
        ps_s = ctx.enter_context(nc.psum_tensor("ps_s", [P, 3, D], F32))
        ps_o = [ctx.enter_context(nc.psum_tensor(f"ps_o{i}", [P, D], F32)) for i in range(2)]
        ps_y = [ps_o[0], ctx.enter_context(nc.psum_tensor("ps_y1", [P, D], F32))]
        s0 = ps_s[:, 0].rearrange("p (h k) -> p h k", h=HG)
        s1 = ps_s[:, 1:3].rearrange("p a (h k) -> p (a h) k", h=2)
        p0 = prob[:, 0:HG * P].rearrange("p (h k) -> p h k", h=HG)
        p1 = prob[:, HG * P:].rearrange("p (h k) -> p h k", h=HG)

        FIRST_WO = B - WO_LATE
        first_wq = (qrot[0], qrot[1], qswap[0], qswap[1])

        first_in = sem("first_in")
        first_wo_in = sem("first_wo_in")
        wq_in = sem("wq_in")
        wq_hi = sem("wq_hi")
        wq_lo = sem("wq_lo")
        wo_in = sem("wo_in")
        wo_hi = sem("wo_hi")
        wo_lo = sem("wo_lo")
        k_in = sem("k_in")
        v_in = sem("v_in")
        q_done = sem("q_done")
        q_mul = sem("q_mul")
        q_add = sem("q_add")
        q_hi = sem("q_hi")
        q_lo = sem("q_lo")
        s_done = sem("s_done")
        smax = sem("smax")
        p_exp = sem("p_exp")
        p_rcp = sem("p_rcp")
        p0_norm = sem("p0_norm")
        p1_norm = sem("p1_norm")
        t_done = sem("pt_done")
        t_hi = sem("t_hi")
        t_lo = sem("t_lo")
        o_done = sem("o_done")
        o_hi = sem("o_hi")
        o_lo = sem("o_lo")
        y_done = sem("y_done")
        y_acc = sem("y_acc")

        PARTS = ((1, U - B, True, True), (U - B, U - B + WO_LATE, False, True), (U - B + WO_LATE, U, False, False))

        with nc.Block() as block:
            @block.sync
            def _(sp):
                def load_wq(n):
                    sp.dma_start(wq_new[:], io["wq_pieces"][bass.ds(n, 1)].rearrange("o p c -> p (o c)")).then_inc(wq_in, 16)

                def load_wo(n):
                    sp.dma_start(wo_new[:], io["wo_pieces"][bass.ds(n, 1)].rearrange("o p c -> p (o c)")).then_inc(wo_in, 16)

                def load_keys(u):
                    for i in range(2):
                        sp.dma_start(f32(kk[i][:]), keep.k[i][bass.ds(u, 1)].rearrange("o p s -> p (o s)")).then_inc(k_in, 16)

                def load_values(u):
                    for i in range(2):
                        sp.dma_start(f32(vv[i][:]), keep.v[i][bass.ds(u, 1)].rearrange("o p t c -> p (o t) c")).then_inc(v_in, 16)

                def step(v, with_wq, with_wo):
                    if with_wq:
                        sp.wait_ge(wq_lo, v + B)
                        load_wq(v + B)
                    sp.wait_ge(s_done, v)
                    load_keys(v)
                    if with_wo:
                        sp.wait_ge(wo_lo, v + B - WO_LATE + B)
                        load_wo(v + B - WO_LATE)
                    sp.wait_ge(o_done, 2 * v)
                    load_values(v)

                for m, tile in enumerate(first_wq):
                    sp.dma_start(tile[:], io["wq_pieces"][2 * m:2 * m + 2].rearrange("o p c -> p o c")).then_inc(first_in, 16)
                load_keys(0)
                sp.dma_start(prob[:].rearrange("p (o c) -> p o c", c=WP), io["wo_pieces"][0:FIRST_WO].rearrange("o p c -> p o c")).then_inc(first_wo_in, 16)
                load_wq(B)
                load_wo(FIRST_WO)
                load_values(0)
                for first, last, with_wq, with_wo in PARTS:
                    with sp.Fori(first, last) as v:
                        step(v, with_wq, with_wo)

            def piece(w, n):
                return w[:, bass.ds((n % (2 * B)) * WP, WP)]

            def first_pieces(w, m):
                return w[:, 2 * m * WP:2 * (m + 1) * WP].rearrange("p (o c) -> p o c", o=2)

            @block.scalar
            def _(act):
                def split_wq(n):
                    act.wait_ge(wq_in, 16 * (n - B) + 16)
                    nc.scalar.activation(piece(wq[0], n), wq_new[:], ACT.Identity).then_inc(wq_hi, 1)

                def split_wo(n):
                    act.wait_ge(wo_in, 16 * (n - FIRST_WO) + 16)
                    nc.scalar.activation(piece(wo[0], n), wo_new[:], ACT.Identity).then_inc(wo_hi, 1)

                def exponentials(u):
                    act.wait_ge(smax, 3 * u + 3)
                    for t, (p, sc) in enumerate(((p0, s0), (p1, s1))):
                        for h in range(HG):
                            nc.scalar.activation(p[:, h], sc[:, h], ACT.Exp, bias=neg_max[:, t, h:h + 1], scale=SCALE0,
                                                 accum_out=row_sum[:, t, h:h + 1]).then_inc(p_exp, 1)

                def transposed(u):
                    for j in range(3):
                        act.wait_ge(t_done, 3 * u + (1 if j == 0 else 3))
                        nc.scalar.activation(pt[0][:, j], ps_s[:, j], ACT.Identity).then_inc(t_hi, 1)

                def queries(u):
                    for j in range(2):
                        act.wait_ge(q_add, 2 * u + j + 1)
                        nc.scalar.activation(q[0][:, 2 * j:2 * j + 2], qrot[j][:], ACT.Identity).then_inc(q_hi, 1)

                def output(u):
                    for j in range(TT):
                        act.wait_ge(o_done, 2 * u + j + 1)
                        nc.scalar.activation(ot[0][:, j], ps_o[j][:], ACT.Identity).then_inc(o_hi, 1)

                def step(v, with_wq, with_wo):
                    exponentials(v - 1)
                    if with_wq:
                        split_wq(v + B)
                    transposed(v - 1)
                    queries(v)
                    output(v - 1)
                    if with_wo:
                        split_wo(v + B - WO_LATE)

                act.wait_ge(first_in, 16 * len(first_wq))
                for m, tile in enumerate(first_wq):
                    nc.scalar.activation(first_pieces(wq[0], m), tile[:], ACT.Identity).then_inc(wq_hi, 2)
                nc.scalar.preload_act_table(ACT.Exp)
                act.wait_ge(first_wo_in, 16)
                nc.scalar.activation(wo[0][:, 0:FIRST_WO * WP], prob[:], ACT.Identity).then_inc(wo_hi, FIRST_WO)
                queries(0)
                split_wq(B)
                split_wo(FIRST_WO)
                act.wait_ge(wo_lo, B + FIRST_WO)
                for first, last, with_wq, with_wo in PARTS:
                    with act.Fori(first, last) as v:
                        step(v, with_wq, with_wo)
                exponentials(U - 1)
                transposed(U - 1)
                output(U - 1)

            @block.vector
            def _(dve):
                def rest_of_transposed(u):
                    for j in range(3):
                        dve.wait_ge(t_hi, 3 * u + j + 1)
                        nc.vector.tensor_tensor(pt[1][:, j], ps_s[:, j], f32(pt[0][:, j]), ALU.subtract).then_inc(t_lo, 1)

                def rest_of_output(u):
                    for j in range(TT):
                        dve.wait_ge(o_hi, 2 * u + j + 1)
                        nc.vector.tensor_tensor(ot[1][:, j], ps_o[j][:], f32(ot[0][:, j]), ALU.subtract).then_inc(o_lo, 1)

                def accumulate(u, j):
                    dve.wait_ge(y_done, 2 * u + j + 3)
                    a = keep.acc[:, bass.ds(((u + B) % B) * TT + j, 1)].rearrange("p o c -> p (o c)")
                    nc.vector.tensor_tensor(a, ps_y[j][:], a, ALU.add).then_inc(y_acc, 1)

                def rotate(u):
                    for j in range(2):
                        dve.wait_ge(q_done, 2 * u + j + 1)
                        src = ps_q[j]
                        nc.vector.tensor_tensor(qrot[j][:], src[:], pair(keep.qcos[:]), ALU.mult)
                        nc.vector.tensor_tensor(qswap[j][0:HB0], src[HB0:P], pair(keep.qsin[HB0:P]), ALU.mult)
                        nc.vector.tensor_tensor(qswap[j][HB0:P], src[0:HB0], pair(keep.qsin[0:HB0]), ALU.mult).then_inc(q_mul, 1)

                def maxima(u):
                    dve.wait_ge(s_done, u + 1)
                    nc.vector.tensor_reduce(row_max[:, 0], s0, AX, ALU.max).then_inc(smax, 1)
                    nc.vector.tensor_reduce(row_max[:, 1], s1, AX, ALU.max).then_inc(smax, 1)
                    dve.wait_ge(smax, 3 * u + 2)
                    nc.vector.tensor_scalar(neg_max[:], row_max[:], -SCALE0, None, ALU.mult).then_inc(smax, 1)

                def normalize(u):
                    dve.wait_ge(p_exp, 8 * u + 8)
                    nc.vector.reciprocal(inv_sum[:], row_sum[:]).then_inc(p_rcp, 1)
                    dve.wait_ge(p_rcp, u + 1)
                    inv = inv_sum[:, 1].rearrange("p (h o) -> p h o", o=1).broadcast_to([P, HG, S])
                    nc.vector.tensor_tensor(p1, p1, inv, ALU.mult).then_inc(p1_norm, 1)

                for i in range(2):
                    nc.vector.memset(f32(ot[i][:]), 0.0).then_inc(o_lo, 1)
                nc.vector.memset(keep.acc[:, 0:NT // 2], 0.0).then_inc(y_acc, 1)
                for m, tile in enumerate(first_wq):
                    dve.wait_ge(wq_hi, 2 * m + 2)
                    nc.vector.tensor_tensor(first_pieces(wq[1], m), tile[:], f32(first_pieces(wq[0], m)), ALU.subtract).then_inc(wq_lo, 2)
                dve.wait_ge(y_acc, 2)
                dve.wait_ge(wq_lo, B)
                rotate(0)
                with dve.Fori(1, U) as v:
                    maxima(v - 1)
                    accumulate(v - 2, 0)
                    normalize(v - 1)
                    rotate(v)
                    rest_of_transposed(v - 1)
                    accumulate(v - 2, 1)
                    rest_of_output(v - 1)
                maxima(U - 1)
                accumulate(U - 2, 0)
                normalize(U - 1)
                rest_of_transposed(U - 1)
                accumulate(U - 2, 1)
                rest_of_output(U - 1)
                for j in range(TT):
                    accumulate(U - 1, j)

            @block.gpsimd
            def _(pool):
                def split_wq(n):
                    pool.wait_ge(wq_hi, n + 1)
                    nc.gpsimd.tensor_tensor(piece(wq[1], n), wq_new[:], f32(piece(wq[0], n)), ALU.subtract).then_inc(wq_lo, 1)

                def split_wo(n):
                    pool.wait_ge(wo_hi, n + 1)
                    nc.gpsimd.tensor_tensor(piece(wo[1], n), wo_new[:], f32(piece(wo[0], n)), ALU.subtract).then_inc(wo_lo, 1)

                def normalize(u):
                    pool.wait_ge(p_rcp, u + 1)
                    inv = inv_sum[:, 0].rearrange("p (h o) -> p h o", o=1).broadcast_to([P, HG, P])
                    nc.gpsimd.tensor_tensor(p0, p0, inv, ALU.mult).then_inc(p0_norm, 1)

                def queries(u):
                    for j in range(2):
                        pool.wait_ge(q_mul, 2 * u + j + 1)
                        nc.gpsimd.tensor_tensor(qrot[j][:], qrot[j][:], qswap[j][:], ALU.add).then_inc(q_add, 1)
                    for j in range(2):
                        pool.wait_ge(q_hi, 2 * u + j + 1)
                        nc.gpsimd.tensor_tensor(q[1][:, 2 * j:2 * j + 2], qrot[j][:], f32(q[0][:, 2 * j:2 * j + 2]), ALU.subtract).then_inc(q_lo, 1)

                def step(v, with_wq, with_wo):
                    normalize(v - 1)
                    if with_wq:
                        split_wq(v + B)
                    queries(v)
                    if with_wo:
                        split_wo(v + B - WO_LATE)

                nc.gpsimd.memset(keep.acc[:, NT // 2:NT], 0.0).then_inc(y_acc, 1)
                for i in range(2):
                    nc.gpsimd.memset(f32(wo[i][:, W:2 * W]), 0.0).then_inc(wo_lo, B // 2)
                pool.wait_ge(wo_hi, FIRST_WO)
                nc.gpsimd.tensor_tensor(wo[1][:, 0:FIRST_WO * WP], prob[:], f32(wo[0][:, 0:FIRST_WO * WP]), ALU.subtract).then_inc(wo_lo, FIRST_WO)
                queries(0)
                split_wq(B)
                split_wo(FIRST_WO)
                for first, last, with_wq, with_wo in PARTS:
                    with pool.Fori(first, last) as v:
                        step(v, with_wq, with_wo)
                normalize(U - 1)

            @block.tensor
            def _(pe):
                def queries(par, u):
                    for j in range(2):
                        for e in range(2):
                            h = 2 * j + e
                            passes = [(w, r, k) for w, r in ((wq[0], keep.ht_hi), (wq[1], keep.ht_hi), (wq[0], keep.ht_lo)) for k in range(KT)]
                            for n, (w, r, k) in enumerate(passes):
                                c = par * W + k * D + h * HD0
                                mm = nc.tensor.matmul(ps_q[j][:, e], w[:, c:c + HD0],
                                                      r[:, bass.ds(u % B, 1), k].rearrange("p o s -> p (o s)"),
                                                      start=(n == 0), stop=(n == len(passes) - 1))
                        mm.then_inc(q_done, 1)

                def values(u):
                    pe.wait_ge(v_in, 32 * u + 32)
                    for j, blocks in ((0, ((0, 0),)), (1, ((0, 1), (1, 2)))):
                        pe.wait_ge(t_lo, 3 * u + 1 + 2 * j)
                        if j == 0:
                            pe.wait_ge(y_acc, 2 * u + 3)
                        passes = [(a, p, k, n) for a, p in split_passes(vv, pt) for k, n in blocks]
                        for n, (a, p, k, blk) in enumerate(passes):
                            mm = nc.tensor.matmul(ps_o[j][:], a[:, k], p[:, blk], start=(n == 0), stop=(n == len(passes) - 1))
                        mm.then_inc(o_done, 1)

                def scores(u):
                    put_masks(nc, keep, (s0, s1), range(TT))
                    pe.wait_ge(k_in, 32 * u + 32)
                    for h in range(HG):
                        if h % 2 == 0:
                            pe.wait_ge(q_lo, 2 * u + h // 2 + 1)
                        for t in range(TT):
                            out = s0[:, h] if t == 0 else s1[:, h]
                            keys = P * (t + 1)
                            for n, (a, r) in enumerate(split_passes(q, kk)):
                                mm = nc.tensor.matmul(out, a[:, h, t * P:(t + 1) * P], r[:, 0:keys],
                                                      start=False, stop=(n == 2), skip_group_check=True)
                    mm.then_inc(s_done, 1)

                def outputs(u, j):
                    pe.wait_ge(wo_lo, (u + 2 * B) // B * B)
                    pe.wait_ge(o_lo, 2 * u + j + 3)
                    pe.wait_ge(y_acc, 2 * u + j + 3)
                    at = ((u + 2 * B) // B % 2) * W
                    passes = [(o, w, h) for o, w in split_passes(ot, wo) for h in range(HG)]
                    for n, (o, w, h) in enumerate(passes):
                        mm = nc.tensor.matmul(ps_y[j][:], o[:, j, h * P:(h + 1) * P], w[:, bass.ds(at + h * D, D)],
                                              start=(n == 0), stop=(n == len(passes) - 1))
                    mm.then_inc(y_done, 1)

                def transposes(u):
                    for blk in range(3):
                        if blk == 0:
                            pe.wait_ge(p0_norm, u + 1)
                        if blk == 1:
                            pe.wait_ge(p1_norm, u + 1)
                        for h in range(HG):
                            src = (p0[:, h], p1[:, h, 0:P], p1[:, h, P:S])[blk]
                            mm = nc.tensor.transpose(ps_s[:, blk, h * P:(h + 1) * P], src, keep.ident[:])
                        mm.then_inc(t_done, 1)

                def step(v, par):
                    scores(v - 1)
                    outputs(v - 2, 0)
                    if par is not None:
                        pe.wait_ge(wq_lo, v // B * B + B)
                        queries(par, v)
                    transposes(v - 1)
                    outputs(v - 2, 1)
                    values(v - 1)

                pe.wait_ge(wq_lo, B)
                queries(0, 0)
                with pe.Fori(1, B) as v:
                    step(v, 0)
                with pe.Fori(B, 2 * B) as v:
                    step(v, 1)
                with pe.Fori(1, G0 // 2) as g2:
                    for par in range(2):
                        with pe.Fori(0, B) as b:
                            step(g2 * (2 * B) + par * B + b, par)
                step(U, None)
                for j in range(TT):
                    outputs(U - 1, j)


class NormedTokens:

    def __init__(self, nc, ctx, keep, layer, shift, name):
        def sb(n, shape, dt=F32):
            return ctx.enter_context(nc.sbuf_tensor(f"{name}_{n}", shape, dt))

        self.nc, self.keep, self.layer, self.shift = nc, keep, layer, shift
        self.stats = sb("stats", [P, TT, 6])
        self.mv = sb("mv", [P, TT, 2])
        self.std = sb("std", [P, TT])
        self.rstd = sb("rstd", [P, TT])
        self.xn = sb("xn", [P, TT, D])
        self.ht = sb("ht", [P, KT, S])
        self.ps = ctx.enter_context(nc.psum_tensor(f"{name}_ps_t", [P, KT, S], F32))
        self.step = ctx.enter_context(nc.semaphore(f"{name}_step"))
        self.rooted = ctx.enter_context(nc.semaphore(f"{name}_rooted"))
        self.turned = ctx.enter_context(nc.semaphore(f"{name}_turned"))
        self.ready = ctx.enter_context(nc.semaphore(f"{name}_ready"))

    def start(self, pe):
        pe.sem_inc(self.turned, 1)

    def normalize(self, dve, src, b):
        n, v = 7 * b, self.nc.vector
        v.memset(self.rstd[:], 0.0)
        for t in range(TT):
            v.bn_stats(self.stats[:, t], src[:, t]).then_inc(self.step, 1)
        dve.wait_ge(self.step, n + 2)
        v.memset(self.rstd[:], 0.0)
        for t in range(TT):
            v.bn_aggr(self.mv[:, t], self.stats[:, t]).then_inc(self.step, 1)
        dve.wait_ge(self.rooted, b + 1)
        v.reciprocal(self.rstd[:], self.std[:]).then_inc(self.step, 1)
        dve.wait_ge(self.step, n + 5)
        dve.wait_ge(self.turned, b + 1)
        for t in range(TT):
            v.tensor_scalar(self.xn[:, t], src[:, t], self.mv[:, t, 0:1], self.rstd[:, t:t + 1],
                            ALU.subtract, ALU.mult).then_inc(self.step, 1)

    def roots(self, act, b):
        act.wait_ge(self.step, 7 * b + 4)
        self.nc.scalar.activation(self.std[:], self.mv[:, :, 1], ACT.Sqrt,
                                  bias=self.keep.eps[:, 0:1]).then_inc(self.rooted, 1)

    def transposes(self, pe, b):
        pe.wait_ge(self.step, 7 * b + 7)
        for t in range(TT):
            for k in range(KT):
                mm = self.nc.tensor.transpose(self.ps[:, k, t * P:(t + 1) * P], self.xn[:, t, k * P:(k + 1) * P],
                                              self.keep.ident[:])
        mm.then_inc(self.turned, 1)

    def modulate(self, act, b):
        act.wait_ge(self.turned, b + 2)
        for k in range(KT):
            self.nc.scalar.activation(self.ht[:, k], self.ps[:, k], ACT.Identity,
                                      bias=self.keep.mod[:, self.layer, self.shift, k, bass.ds(b, 1)],
                                      scale=self.keep.mod[:, self.layer, self.shift + 1, k, bass.ds(b, 1)]).then_inc(self.ready, 1)


def split_passes(a, b):
    return ((a[0], b[0]), (a[1], b[0]), (a[0], b[1]))


def put_masks(nc, keep, scores, tiles):
    for t in tiles:
        heads = 2 if t else 4
        for h in range(0, 4, heads):
            mask = keep.mask_b[:].rearrange("p (o k) -> p o k", o=1).broadcast_to([P, heads, P])
            nc.tensor.matmul(scores[t][:, h:h + heads, t * P:(t + 1) * P], keep.ident_b[:], mask,
                             start=True, stop=False, skip_group_check=True)


def element(tensor, b):
    return tensor[:, bass.ds(b * TT, TT)]


def over_tiles(row):
    return row.rearrange("p (o d) -> p o d", o=1).broadcast_to([P, TT, row.shape[1]])


def keep_best(nc, dve, step, base, value, cmp_a, cmp_b, rank, keepers, earlier, count):
    _, t, n = value.shape
    as_m = value.rearrange("p t (o m) -> p t o m", o=1).broadcast_to([P, t, n, n])
    as_n = value.rearrange("p t (n o) -> p t n o", o=1).broadcast_to([P, t, n, n])
    first = earlier.rearrange("p (o n m) -> p o n m", o=1, n=n).broadcast_to([P, t, n, n])
    v = nc.vector
    v.tensor_tensor(cmp_a, as_m, as_n, ALU.is_gt).then_inc(step, 1)
    v.tensor_tensor(cmp_b, as_m, as_n, ALU.is_equal).then_inc(step, 1)
    dve.wait_ge(step, base + 2)
    v.tensor_tensor(cmp_b, cmp_b, first, ALU.mult).then_inc(step, 1)
    dve.wait_ge(step, base + 3)
    v.tensor_tensor(cmp_a, cmp_a, cmp_b, ALU.add).then_inc(step, 1)
    dve.wait_ge(step, base + 4)
    v.tensor_reduce(rank, cmp_a, AX, ALU.add).then_inc(step, 1)
    dve.wait_ge(step, base + 5)
    v.tensor_scalar(keepers, rank, count - 0.5, None, ALU.is_lt).then_inc(step, 1)
    dve.wait_ge(step, base + 6)


def phase_router0(nc, io, keep):
    with ExitStack() as ctx:
        def sb(name, shape, dt=F32):
            return ctx.enter_context(nc.sbuf_tensor(name, shape, dt))

        def sem(name):
            return ctx.enter_context(nc.semaphore(name))

        E, R = LORA0_E, LORA0_R
        x = [sb(f"d_x{n}", [P, TT, D]) for n in range(2)]
        gate = [sb(f"d_gate{n}", [P, D]) for n in range(2)]
        wst = [sb(f"d_wst{n}", [P, KT, D]) for n in range(2)]
        ra = sb("d_ra", [P, KT, E + E * R])
        norm = NormedTokens(nc, ctx, keep, 0, 2, "d")
        ps_r = ctx.enter_context(nc.psum_tensor("d_ps_r", [P, TT, E + E * R], F32))
        logits = sb("d_logits", [P, NT, E])
        earlier = sb("d_earlier", [P, E * E])
        cmp_a = sb("d_cmp_a", [P, NT, E, E])
        cmp_b = sb("d_cmp_b", [P, NT, E, E])
        rank = sb("d_rank", [P, NT, E])
        keepers = sb("d_keepers", [P, NT, E])
        top = sb("d_top", [P, NT])
        e = sb("d_e", [P, NT, E])
        total = sb("d_total", [P, NT])

        w_in = sem("d_w_in")
        x_in = [sem(f"d_x_in{n}") for n in range(2)]
        qkv_in = [sem(f"d_qkv_in{n}") for n in range(2)]
        qkv_hi = sem("d_qkv_hi")
        qkv_lo = sem("d_qkv_lo")
        x1_step = sem("d_x1_step")
        r_done = sem("d_r_done")
        r_out = sem("d_r_out")
        g_step = sem("d_g_step")
        g_exp = sem("d_g_exp")

        with nc.Block() as block:
            @block.sync
            def _(sp):
                sp.dma_start(ra[:, :, 0:E], io["router0"]).then_inc(w_in, 16)
                sp.dma_start(ra[:, :, E:], io["a0"]).then_inc(w_in, 16)
                sp.dma_start(earlier[:], io["earlier0"]).then_inc(w_in, 16)
                def load(b, slot):
                    sp.dma_start(x[slot][:], io["x"][bass.ds(b, 1)].rearrange("o p t d -> p (o t) d")).then_inc(x_in[slot], 16)
                    sp.dma_start(gate[slot][:], keep.gates[0, bass.ds(b, 1)].partition_broadcast(P)).then_inc(x_in[slot], 16)

                for slot in range(2):
                    load(slot, slot)
                sp.dma_start(wst[0][:], io["wq1"]).then_inc(qkv_in[0], 16)
                sp.dma_start(wst[1][:], io["wk1"]).then_inc(qkv_in[1], 16)
                def reload(n):
                    for slot in range(2):
                        sp.wait_ge(x1_step, 4 * n + 2 * slot - 2)
                        load(2 * n + slot, slot)

                reload(1)
                sp.wait_ge(qkv_lo, 1)
                sp.dma_start(wst[0][:], io["wv1"]).then_inc(qkv_in[0], 16)
                with sp.Fori(2, B // 2) as n:
                    reload(n)

            @block.gpsimd
            def _(pool):
                for n in range(3):
                    pool.wait_ge(qkv_in[n % 2], 16 * (n // 2 + 1))
                    nc.gpsimd.tensor_copy(keep.qkv_w[n][0][:], wst[n % 2][:]).then_inc(qkv_hi, 1)
                    pool.wait_ge(qkv_hi, n + 1)
                    nc.gpsimd.tensor_tensor(keep.qkv_w[n][1][:], wst[n % 2][:], f32(keep.qkv_w[n][0][:]), ALU.subtract).then_inc(qkv_lo, 1)

            @block.vector
            def _(dve):
                with dve.Fori(0, B // 2) as n:
                    for slot in range(2):
                        b = 2 * n + slot
                        x1 = element(keep.acc, b)
                        dve.wait_ge(x_in[slot], 32 * n + 32)
                        nc.vector.tensor_tensor(x1, x1, over_tiles(gate[slot][:]), ALU.mult).then_inc(x1_step, 1)
                        dve.wait_ge(x1_step, 2 * b + 1)
                        nc.vector.tensor_tensor(x1, x1, x[slot][:], ALU.add).then_inc(x1_step, 1)
                        dve.wait_ge(x1_step, 2 * b + 2)
                        norm.normalize(dve, x1, b)
                dve.wait_ge(w_in, 48)
                dve.wait_ge(r_out, 2 * B + 2)
                keep_best(nc, dve, g_step, 0, logits[:], cmp_a[:], cmp_b[:], rank[:], keepers[:], earlier[:], 2)
                nc.vector.tensor_reduce(top[:], logits[:], AX, ALU.max).then_inc(g_step, 1)
                dve.wait_ge(g_step, 7)
                nc.vector.tensor_tensor(e[:], logits[:], top[:].rearrange("p (t o) -> p t o", o=1).broadcast_to([P, NT, E]),
                                        ALU.subtract).then_inc(g_step, 1)
                dve.wait_ge(g_exp, 1)
                nc.vector.tensor_tensor(e[:], e[:], keepers[:], ALU.mult).then_inc(g_step, 1)
                dve.wait_ge(g_step, 9)
                nc.vector.tensor_reduce(total[:], e[:], AX, ALU.add).then_inc(g_step, 1)
                dve.wait_ge(g_step, 10)
                nc.vector.reciprocal(total[:], total[:]).then_inc(g_step, 1)
                dve.wait_ge(g_step, 11)
                nc.vector.tensor_scalar(total[:], total[:], LORA0_SCALE, None, ALU.mult).then_inc(g_step, 1)
                dve.wait_ge(g_step, 12)
                nc.vector.tensor_tensor(e[:], e[:], total[:].rearrange("p (t o) -> p t o", o=1).broadcast_to([P, NT, E]),
                                        ALU.mult).then_inc(g_step, 1)
                dve.wait_ge(g_step, 13)
                m = keep.mid0[:].rearrange("p t (e r) -> p t e r", e=E)
                nc.vector.tensor_tensor(m, m, e[:].rearrange("p t (e o) -> p t e o", o=1).broadcast_to([P, NT, E, R]),
                                        ALU.mult).then_inc(g_step, 1)

            @block.scalar
            def _(act):
                def copy_out(b):
                    act.wait_ge(r_done, b + 2)
                    nc.scalar.activation(element(logits, b), ps_r[:, :, 0:E], ACT.Identity).then_inc(r_out, 1)
                    nc.scalar.activation(element(keep.mid0, b), ps_r[:, :, E:], ACT.Identity).then_inc(r_out, 1)

                act.sem_inc(r_out, 2)
                nc.scalar.preload_act_table(ACT.Sqrt)
                norm.roots(act, 0)
                norm.modulate(act, 0)
                with act.Fori(0, B - 1) as b:
                    norm.roots(act, b + 1)
                    copy_out(b)
                    norm.modulate(act, b + 1)
                copy_out(B - 1)
                act.wait_ge(g_step, 8)
                nc.scalar.activation(e[:], e[:], ACT.Exp).then_inc(g_exp, 1)

            @block.tensor
            def _(pe):
                norm.start(pe)
                pe.sem_inc(r_done, 1)
                pe.wait_ge(w_in, 48)
                with pe.Fori(0, B) as b:
                    norm.transposes(pe, b)
                    pe.wait_ge(r_out, 2 * b + 2)
                    pe.wait_ge(norm.ready, KT * b + KT)
                    for t in range(TT):
                        for k in range(KT):
                            mm = nc.tensor.matmul(ps_r[:, t], norm.ht[:, k, t * P:(t + 1) * P], ra[:, k],
                                                  start=(k == 0), stop=(k == KT - 1))
                    mm.then_inc(r_done, 1)


def phase_queries1(nc, io, keep):
    with ExitStack() as ctx:
        def sb(name, shape, dt=F32):
            return ctx.enter_context(nc.sbuf_tensor(name, shape, dt))

        def sem(name):
            return ctx.enter_context(nc.semaphore(name))

        ER = LORA0_E * LORA0_R
        gate = sb("e_gate", [P, D])
        b0 = sb("e_b0", [2 * ER, TT, D])
        hs = [sb(f"e_hs{i}", [P, KT, S], F32R) for i in range(2)]
        vst = [sb(f"e_vst{i}", [P, 8, D // 8]) for i in range(2)]
        w = keep.qkv_w
        mid = sb("e_mid", [P, TT, ER])
        midt = sb("e_midt", [TT * ER, P])
        delta = sb("e_delta", [P, TT, D])
        norm = NormedTokens(nc, ctx, keep, 1, 0, "e")
        rcos = sb("e_rcos", [P, D])
        rswap = sb("e_rswap", [P, D])
        cos = sb("e_cos", [P, TT, HD1])
        sin = sb("e_sin", [P, TT, HD1])
        ps_m = ctx.enter_context(nc.psum_tensor("e_ps_m", [TT * ER, P], F32))
        ps_d = ctx.enter_context(nc.psum_tensor("e_ps_d", [P, TT, D], F32))
        ps_p = [ctx.enter_context(nc.psum_tensor(f"e_ps_p{i}", [P, D], F32)) for i in range(3)]

        b0_zero = sem("e_b0_zero")
        tab_in = sem("e_tab_in")
        gate_in = sem("e_gate_in")
        mid_ready = sem("e_mid_ready")
        m_done = sem("e_m_done")
        m_out = sem("e_m_out")
        d_done = sem("e_d_done")
        x2_step = sem("e_x2_step")
        h_hi = sem("e_h_hi")
        h_lo = sem("e_h_lo")
        p_done = sem("e_p_done")
        p_mul = sem("e_p_mul")
        p_out = sem("e_p_out")
        v_out = sem("e_v_out")
        v_stored = [sem(f"e_v_stored{t}") for t in range(TT)]

        with nc.Block() as block:
            @block.sync
            def _(sp):
                sp.wait_ge(b0_zero, 1)
                for t in range(TT):
                    sp.dma_start(b0[t * ER:(t + 1) * ER, t], io["b0"]).then_inc(tab_in, 16)
                sp.dma_start(cos[:], io["cos1"]).then_inc(tab_in, 16)
                sp.dma_start(sin[:], io["sin1"]).then_inc(tab_in, 16)
                sp.dma_start(gate[:], keep.gates[1, 0:1].partition_broadcast(P)).then_inc(gate_in, 16)

                def store_values(b):
                    for t in range(TT):
                        sp.wait_ge(v_out, TT * b + t + 2)
                        sp.dma_start(keep.v1_dram[:, bass.ds(b * 8, 8), t], vst[t][:]).then_inc(v_stored[t], 16)

                for s in v_stored:
                    sp.sem_inc(s, 16)
                with sp.Fori(1, B) as b:
                    sp.wait_ge(x2_step, 2 * b)
                    sp.dma_start(gate[:], keep.gates[1, bass.ds(b, 1)].partition_broadcast(P)).then_inc(gate_in, 16)
                    store_values(b - 1)
                store_values(B - 1)
                for s in v_stored:
                    sp.wait_ge(s, 16 * B + 16)

            @block.scalar
            def _(act):
                def lora_in(b):
                    nc.scalar.activation(mid[:], element(keep.mid0, b), ACT.Identity).then_inc(mid_ready, 1)
                    act.wait_ge(m_done, b + 1)
                    nc.scalar.activation(midt[:], ps_m[:], ACT.Identity).then_inc(m_out, 1)

                def values(b, t):
                    act.wait_ge(p_done, 6 * b + 3 * t + 3)
                    act.wait_ge(v_stored[t], 16 * b + 16)
                    nc.scalar.activation(vst[t][:], ps_p[2][:].rearrange("p (g c) -> p g c", g=8),
                                         ACT.Identity).then_inc(v_out, 1)

                def split_h(b, t):
                    act.wait_ge(norm.ready, KT * b + KT)
                    cols = slice(t * P, (t + 1) * P)
                    nc.scalar.activation(hs[0][:, :, cols], norm.ht[:, :, cols], ACT.Identity).then_inc(h_hi, 1)

                act.sem_inc(v_out, 1)
                lora_in(0)
                nc.scalar.preload_act_table(ACT.Sqrt)
                norm.roots(act, 0)
                norm.modulate(act, 0)
                split_h(0, 0)
                split_h(0, 1)
                with act.Fori(0, B - 1) as b:
                    lora_in(b + 1)
                    values(b, 0)
                    norm.roots(act, b + 1)
                    act.wait_ge(h_lo, TT * b + TT)
                    norm.modulate(act, b + 1)
                    act.wait_ge(p_done, 6 * b + 3)
                    split_h(b + 1, 0)
                    values(b, 1)
                    split_h(b + 1, 1)
                values(B - 1, 0)
                values(B - 1, 1)

            @block.vector
            def _(dve):
                nc.vector.memset(b0[:], 0.0).then_inc(b0_zero, 1)
                dve.wait_ge(tab_in, 64)

                def add_lora(b):
                    x2 = element(keep.acc, b)
                    dve.wait_ge(gate_in, 16 * b + 16)
                    dve.wait_ge(d_done, b + 1)
                    nc.vector.tensor_tensor(delta[:], ps_d[:], over_tiles(gate[:]), ALU.mult).then_inc(x2_step, 1)
                    dve.wait_ge(x2_step, 2 * b + 1)
                    nc.vector.tensor_tensor(x2, x2, delta[:], ALU.add).then_inc(x2_step, 1)

                def normalize(b):
                    dve.wait_ge(x2_step, 2 * b + 2)
                    norm.normalize(dve, element(keep.acc, b), b)

                def split_h(b, t):
                    dve.wait_ge(h_hi, TT * b + t + 1)
                    cols = slice(t * P, (t + 1) * P)
                    nc.vector.tensor_tensor(hs[1][:, :, cols], norm.ht[:, :, cols], f32(hs[0][:, :, cols]),
                                            ALU.subtract).then_inc(h_lo, 1)

                def rotate(b, t):
                    half = HD1 // 2
                    for n in range(2):
                        dve.wait_ge(p_done, 6 * b + 3 * t + n + 1)
                        dve.wait_ge(p_out, 4 * b + 2 * t + n + 1)
                        src = ps_p[n][:].rearrange("p (h c) -> p h c", h=H1)
                        c = cos[:, t].rearrange("p (o c) -> p o c", o=1).broadcast_to([P, H1, HD1])
                        sn = sin[:, t].rearrange("p (o c) -> p o c", o=1).broadcast_to([P, H1, HD1])
                        rs = rswap[:].rearrange("p (h c) -> p h c", h=H1)
                        nc.vector.tensor_tensor(rcos[:].rearrange("p (h c) -> p h c", h=H1), src, c, ALU.mult)
                        nc.vector.tensor_tensor(rs[:, :, 0:half], src[:, :, half:], sn[:, :, 0:half], ALU.mult)
                        nc.vector.tensor_tensor(rs[:, :, half:], src[:, :, 0:half], sn[:, :, half:], ALU.mult).then_inc(p_mul, 1)

                dve.sem_inc(p_mul, 2)
                add_lora(0)
                normalize(0)
                split_h(0, 0)
                split_h(0, 1)
                with dve.Fori(0, B - 1) as b:
                    add_lora(b + 1)
                    rotate(b, 0)
                    normalize(b + 1)
                    rotate(b, 1)
                    split_h(b + 1, 0)
                    split_h(b + 1, 1)
                rotate(B - 1, 0)
                rotate(B - 1, 1)

            @block.gpsimd
            def _(pool):
                pool.sem_inc(p_out, 1)
                with pool.Fori(0, B) as b:
                    for t in range(TT):
                        for n, dst in enumerate((keep.q1, keep.k1)):
                            pool.wait_ge(p_mul, 4 * b + 2 * t + n + 3)
                            nc.gpsimd.tensor_tensor(dst[:, bass.ds(b * 8, 8), t], rcos[:].rearrange("p (g c) -> p g c", g=8),
                                                    rswap[:].rearrange("p (g c) -> p g c", g=8), ALU.add).then_inc(p_out, 1)

            @block.tensor
            def _(pe):
                def lora_in(b):
                    pe.wait_ge(mid_ready, b + 1)
                    nc.tensor.transpose(ps_m[:], mid[:].rearrange("p t e -> p (t e)"), keep.ident[:]).then_inc(m_done, 1)

                def lora_out(b):
                    pe.wait_ge(m_out, b + 1)
                    for t in range(TT):
                        mm = nc.tensor.matmul(ps_d[:, t], midt[:], b0[:, t], start=True, stop=True)
                    mm.then_inc(d_done, 1)

                def project(b, t, n):
                    if n == 0:
                        pe.wait_ge(h_lo, TT * b + t + 1)
                    if n < 2:
                        pe.wait_ge(p_mul, 4 * b + 2 * t + n + 1)
                    else:
                        pe.wait_ge(v_out, 2 * b + t + 1)
                    passes = [(a, r, k) for a, r in split_passes(hs, w[n]) for k in range(KT)]
                    for j, (a, r, k) in enumerate(passes):
                        mm = nc.tensor.matmul(ps_p[n][:], a[:, k, t * P:(t + 1) * P], r[:, k],
                                              start=(j == 0), stop=(j == len(passes) - 1))
                    mm.then_inc(p_done, 1)

                norm.start(pe)
                pe.wait_ge(tab_in, 64)
                lora_in(0)
                lora_out(0)
                norm.transposes(pe, 0)
                with pe.Fori(0, B - 1) as b:
                    lora_in(b + 1)
                    project(b, 0, 0)
                    lora_out(b + 1)
                    project(b, 0, 1)
                    project(b, 0, 2)
                    project(b, 1, 0)
                    project(b, 1, 1)
                    norm.transposes(pe, b + 1)
                    project(b, 1, 2)
                for t in range(TT):
                    for n in range(3):
                        project(B - 1, t, n)


def phase_attention1(nc, io, keep):
    U = 8 * B
    HU = 4
    VW = 2 * HD1 + 2
    with ExitStack() as ctx:
        def sb(name, shape, dt=F32):
            return ctx.enter_context(nc.sbuf_tensor(name, shape, dt))

        def sem(name):
            return ctx.enter_context(nc.semaphore(name))

        stack = [sb(f"f_stack{n}", [P, TT * HU, 4, HD1]) for n in range(2)]
        kt = sb("f_kt", [P, 2, S], F32R)
        qt = [sb(f"f_qt{e}", [P, 2, S], F32R) for e in range(2)]
        vx = sb("f_vx", [P, TT, HU, HD1])
        vs = sb("f_vs", [P, TT, HU, VW], F32R)
        prob = sb("f_prob", [P, 3 * HU * P])
        row_max = sb("f_row_max", [P, 2, HU])
        neg_max = sb("f_neg_max", [P, 2, HU])
        inv_sum = sb("f_inv_sum", [P, TT * HU])
        pt = [sb(f"f_pt{i}", [P, 3, HU * P], F32R) for i in range(2)]
        osum = sb("f_osum", [P, TT * HU, HD1])
        ps_qk = [ctx.enter_context(nc.psum_tensor(f"f_ps_qk{n}", [P, 2, S], F32)) for n in range(2)]
        ps_s = ctx.enter_context(nc.psum_tensor("f_ps_s", [P, 3, D], F32))
        ps_t = [ctx.enter_context(nc.psum_tensor(f"f_ps_t{i}", [P, D], F32)) for i in range(2)]
        ps_o = ctx.enter_context(nc.psum_tensor("f_ps_o", [P, TT * HU, VW], F32))
        scores_of = (ps_s[:, 0].rearrange("p (h k) -> p h k", h=HU),
                     ps_s[:, 1:3].rearrange("p a (h k) -> p (a h) k", h=2))
        p0 = prob[:, 0:HU * P].rearrange("p (h k) -> p h k", h=HU)
        p1 = prob[:, HU * P:].rearrange("p (h k) -> p h k", h=HU)

        zeroed = sem("f_zeroed")
        v_in = sem("f_v_in")
        g_raw_in = sem("f_g_raw_in")
        st_hi = sem("f_st_hi")
        st_lo = sem("f_st_lo")
        vs_hi = sem("f_vs_hi")
        vs_lo = sem("f_vs_lo")
        qk_done = sem("f_qk_done")
        qk_out = sem("f_qk_out")
        s_done = sem("f_s_done")
        smax = sem("f_smax")
        sneg = sem("f_sneg")
        p_exp = sem("f_p_exp")
        t_done = sem("f_t_done")
        t_hi = sem("f_t_hi")
        t_lo = sem("f_t_lo")
        o_done = sem("f_o_done")
        o_step = sem("f_o_step")

        def steps(engine, step):
            step(0, 0, 2)
            step(1, 1, 2)
            with engine.Fori(2, U - 2) as v:
                step(v, 2, 2)
            step(U - 2, 2, 1)
            step(U - 1, 2, 0)

        def heads(src, u):
            x = src[:, bass.ds(u, 1)].rearrange("p o t (h r c) -> p (o t h) r c", h=HU, r=1)
            return x.broadcast_to([P, TT * HU, 2, HD1])

        with nc.Block() as block:
            @block.sync
            def _(sp):
                def load_values(u):
                    sp.dma_start(vx[:].rearrange("p t h c -> p t (h c)"),
                                 keep.v1_dram[:, bass.ds(u, 1)].rearrange("p o t c -> p (o t) c")).then_inc(v_in, 16)

                load_values(0)
                for tile, name in zip(keep.g_raw, ("wo1", "base_w")):
                    sp.dma_start(tile[:], io[name]).then_inc(g_raw_in, 16)
                sp.dma_start(keep.g_rl[:, :, 0:NR], io["router1"]).then_inc(g_raw_in, 16)
                sp.dma_start(keep.g_rl[:, :, NR:], io["a1"]).then_inc(g_raw_in, 16)
                with sp.Fori(1, U) as u:
                    sp.wait_ge(vs_lo, u)
                    load_values(u)
                sp.wait_ge(g_raw_in, 64)

            @block.vector
            def _(dve):
                def stacks(u, first=False):
                    if not first:
                        dve.wait_ge(qk_done, 2 * u)
                    for n, (src, hi) in enumerate(((keep.q1, slice(0, 4, 2)), (keep.k1, slice(0, 2)))):
                        nc.vector.tensor_copy(stack[n][:, :, hi].bitcast(F32R), heads(src, u)).then_inc(st_hi, 1)

                def rest_of_transposed(u, blocks):
                    for j in blocks:
                        dve.wait_ge(t_hi, 3 * u + j + 1)
                        nc.vector.tensor_tensor(pt[1][:, j], ps_t[j % 2][:], f32(pt[0][:, j]), ALU.subtract).then_inc(t_lo, 1)

                def maxima(u, t):
                    dve.wait_ge(s_done, 2 * u + t + 1)
                    nc.vector.tensor_reduce(row_max[:, t], scores_of[t], AX, ALU.max).then_inc(smax, 1)
                    dve.wait_ge(smax, 2 * u + t + 1)
                    nc.vector.tensor_scalar(neg_max[:, t], row_max[:, t], -SCALE1, None, ALU.mult).then_inc(sneg, 1)

                def output(u):
                    dve.wait_ge(o_done, u + 1)
                    parts = ps_o[:, :, 0:2 * HD1].rearrange("p n (r c) -> p n c r", r=2)
                    nc.vector.tensor_reduce(osum[:], parts, AX, ALU.add).then_inc(o_step, 1)
                    nc.vector.reciprocal(inv_sum[:], ps_o[:, :, 2 * HD1]).then_inc(o_step, 1)
                    dve.wait_ge(o_step, 3 * u + 2)
                    inv = inv_sum[:].rearrange("p (n o) -> p n o", o=1).broadcast_to([P, TT * HU, HD1])
                    dst = keep.o1[:, bass.ds(u, 1)].rearrange("p o t (h c) -> p (o t h) c", h=HU)
                    nc.vector.tensor_tensor(dst, osum[:], inv, ALU.mult).then_inc(o_step, 1)

                def step(v, before, after):
                    maxima(v, 1)
                    if before:
                        rest_of_transposed(v - 1, (1, 2))
                    if after:
                        maxima(v + 1, 0)
                    rest_of_transposed(v, (0,))
                    if after >= 2:
                        stacks(v + 2)
                    if before:
                        output(v - 1)

                for tile in qt:
                    nc.vector.memset(f32(tile[:]), 0.0).then_inc(zeroed, 1)
                nc.vector.memset(f32(vs[:]), 1.0).then_inc(zeroed, 1)
                stacks(0, first=True)
                maxima(0, 0)
                stacks(1)
                steps(dve, step)
                rest_of_transposed(U - 1, (1, 2))
                output(U - 1)

            @block.scalar
            def _(act):
                def queries_keys(u):
                    act.wait_ge(qk_done, 2 * u + 1)
                    for e in range(2):
                        rows = slice(e * P // 2, (e + 1) * P // 2)
                        nc.scalar.activation(qt[e][rows], ps_qk[0][rows], ACT.Identity).then_inc(qk_out, 1)
                    act.wait_ge(qk_done, 2 * u + 2)
                    nc.scalar.activation(kt[:], ps_qk[1][:], ACT.Identity).then_inc(qk_out, 1)

                def transposed(u, blocks):
                    for j in blocks:
                        act.wait_ge(t_done, 3 * u + j + 1)
                        nc.scalar.activation(pt[0][:, j], ps_t[j % 2][:], ACT.Identity).then_inc(t_hi, 1)

                def exponentials(u, t):
                    act.wait_ge(sneg, 2 * u + t + 1)
                    for h in range(HU):
                        nc.scalar.activation((p0, p1)[t][:, h], scores_of[t][:, h], ACT.Exp, bias=neg_max[:, t, h:h + 1],
                                             scale=SCALE1).then_inc(p_exp, 1)

                def values(u, before):
                    act.wait_ge(v_in, 16 * u + 16)
                    if before:
                        act.wait_ge(o_done, u)
                    nc.scalar.activation(vs[:, :, :, 0:HD1], vx[:], ACT.Identity).then_inc(vs_hi, 1)

                def step(v, before, after):
                    exponentials(v, 0)
                    if before:
                        values(v - 1, before >= 2)
                        transposed(v - 1, (1, 2))
                    if after:
                        queries_keys(v + 1)
                    exponentials(v, 1)
                    transposed(v, (0,))

                nc.scalar.preload_act_table(ACT.Exp)
                act.wait_ge(zeroed, 3)
                queries_keys(0)
                steps(act, step)
                values(U - 1, True)
                transposed(U - 1, (1, 2))

            @block.gpsimd
            def _(pool):
                def stacks(u):
                    pool.wait_ge(st_hi, 2 * u + 2)
                    for n, (src, lo) in enumerate(((keep.q1, slice(1, 4, 2)), (keep.k1, slice(2, 4)))):
                        h2 = stack[n][:, :, 0:1].broadcast_to([P, TT * HU, 2, HD1])
                        nc.gpsimd.tensor_tensor(stack[n][:, :, lo].bitcast(F32R), heads(src, u), h2, ALU.subtract).then_inc(st_lo, 1)

                def values(u):
                    pool.wait_ge(vs_hi, u + 1)
                    nc.gpsimd.tensor_tensor(vs[:, :, :, HD1:2 * HD1], vx[:], f32(vs[:, :, :, 0:HD1]), ALU.subtract).then_inc(vs_lo, 1)

                stacks(0)
                stacks(1)
                with pool.Fori(2, U) as u:
                    values(u - 2)
                    stacks(u)
                values(U - 2)
                values(U - 1)

            @block.tensor
            def _(pe):
                def queries_keys(u):
                    for n in range(2):
                        pe.wait_ge(st_lo, 2 * u + n + 1)
                        for i in range(2):
                            for t in range(TT):
                                a = stack[n][:, t * HU + 2 * i:t * HU + 2 * i + 2].rearrange("p h r c -> p (h r c)")
                                mm = nc.tensor.transpose(ps_qk[n][:, i, t * P:(t + 1) * P], a, keep.ident[:])
                        mm.then_inc(qk_done, 1)

                def transposes(u, j, before=True):
                    if j == 0 and before:
                        pe.wait_ge(t_lo, 3 * u)
                    if j == 2:
                        pe.wait_ge(t_lo, 3 * u + 1)
                    pe.wait_ge(p_exp, 8 * u + (4 if j == 0 else 8))
                    src, at = ((p0, 0), (p1, 0), (p1, P))[j]
                    for h in range(HU):
                        mm = nc.tensor.transpose(ps_t[j % 2][:, h * P:(h + 1) * P], src[:, h, at:at + P], keep.ident[:])
                    mm.then_inc(t_done, 1)

                def scores(u, t):
                    pe.wait_ge(qk_out, 3 * u + 3)
                    put_masks(nc, keep, scores_of, (t,))
                    for h in range(HU):
                        mm = nc.tensor.matmul(scores_of[t][:, h], qt[h % 2][:, h // 2, t * P:(t + 1) * P], kt[:, h // 2, 0:P * (t + 1)],
                                              start=False, stop=True, skip_group_check=True)
                    mm.then_inc(s_done, 1)

                def values(u, t, before):
                    if t == 0:
                        pe.wait_ge(vs_lo, u + 1)
                        if before:
                            pe.wait_ge(o_step, 3 * u)
                    pe.wait_ge(t_lo, 3 * u + 1 + 2 * t)
                    blocks = ((0, 1), (1, 2)) if t else ((0, 0),)
                    for h in range(HU):
                        passes = [(p, k, blk) for p in pt for k, blk in blocks]
                        for n, (p, k, blk) in enumerate(passes):
                            mm = nc.tensor.matmul(ps_o[:, t * HU + h], p[:, blk, h * P:(h + 1) * P], vs[:, k, h],
                                                  start=(n == 0), stop=(n == len(passes) - 1))
                    if t:
                        mm.then_inc(o_done, 1)

                def step(v, before, after):
                    if before:
                        transposes(v - 1, 1)
                    scores(v, 1)
                    if before:
                        transposes(v - 1, 2)
                    if after:
                        queries_keys(v + 1)
                    if before:
                        values(v - 1, 0, before >= 2)
                    transposes(v, 0, before > 0)
                    if after:
                        scores(v + 1, 0)
                    if before:
                        values(v - 1, 1, True)

                queries_keys(0)
                scores(0, 0)
                steps(pe, step)
                for j in (1, 2):
                    transposes(U - 1, j)
                for t in range(TT):
                    values(U - 1, t, True)


def phase_router1(nc, io, keep):
    with ExitStack() as ctx:
        def sb(name, shape, dt=F32):
            return ctx.enter_context(nc.sbuf_tensor(name, shape, dt))

        def sem(name):
            return ctx.enter_context(nc.semaphore(name))

        E, R = LORA1_E, LORA1_R
        ER = E * R
        gate = [sb(f"g_gate{i}", [P, D]) for i in range(2)]
        bias = sb("g_bias", [P, D])
        rl, raw = keep.g_rl, keep.g_raw
        w = [[sb(f"g_w{n}{i}", [P, KT, D], F32R) for i in range(2)] for n in range(2)]
        o = sb("g_o", [P, TT, D])
        oh = [sb(f"g_oh{i}", [P, KT, S], F32R) for i in range(2)]
        hs = [sb(f"g_hs{i}", [P, KT, S], F32R) for i in range(2)]
        y = sb("g_y", [P, TT, D])
        base = sb("g_base", [P, TT, D])
        norm = NormedTokens(nc, ctx, keep, 1, 2, "g")
        ps_y = ctx.enter_context(nc.psum_tensor("g_ps_y", [P, TT, D], F32))
        ps_b = ctx.enter_context(nc.psum_tensor("g_ps_b", [P, TT, D], F32))
        ps_r = ctx.enter_context(nc.psum_tensor("g_ps_r", [P, TT, NR + ER], F32))
        logits = sb("g_logits", [P, NT, NR])
        rbias = sb("g_rbias", [P, NR])
        emap_i = sb("g_emap_i", [P, NR], I32)
        emap = sb("g_emap", [P, NR])
        expert = sb("g_expert", [P, E * NR])
        sel = sb("g_sel", [P, E, NR])
        earlier = sb("g_earlier", [P, NR * NR])
        top = sb("g_top", [P, NT])
        e = sb("g_e", [P, NT, NR])
        rank = sb("g_rank", [P, NT, NR])
        keepers = sb("g_keepers", [P, NT, NR])
        total = sb("g_total", [P, NT])
        wexp = sb("g_wexp", [P, NT, E])
        cmp_a = sb("g_cmp_a", [P, TT, NR, NR])
        cmp_b = sb("g_cmp_b", [P, TT, NR, NR])
        mixed = sb("g_mixed", [P, NT, E, NR])

        tab_in = sem("g_tab_in")
        w_hi = sem("g_w_hi")
        w_lo = sem("g_w_lo")
        ga_in = sem("g_ga_in")
        gb_in = sem("g_gb_in")
        o_in = sem("g_o_in")
        o_turned = sem("g_o_turned")
        o_hi = sem("g_o_hi")
        o_lo = sem("g_o_lo")
        y_done = sem("g_y_done")
        x3_step = sem("g_x3_step")
        h_hi = sem("g_h_hi")
        h_lo = sem("g_h_lo")
        b_done = sem("g_b_done")
        r_done = sem("g_r_done")
        r_out = sem("g_r_out")
        b_out = sem("g_b_out")
        b_step = sem("g_b_step")
        rank_step = sem("g_rank_step")
        g_step = sem("g_g_step")
        g_exp = sem("g_g_exp")

        with nc.Block() as block:
            @block.sync
            def _(sp):
                sp.dma_start(bias[:], io["base_b"].partition_broadcast(P)).then_inc(tab_in, 16)
                sp.dma_start(rbias[:], io["router_b"].partition_broadcast(P)).then_inc(tab_in, 16)
                sp.dma_start(emap_i[:], io["expert_map"].partition_broadcast(P)).then_inc(tab_in, 16)
                sp.dma_start(expert[:], io["expert"]).then_inc(tab_in, 16)
                sp.dma_start(earlier[:], io["earlier1"]).then_inc(tab_in, 16)
                sp.dma_start(gate[0][:], keep.gates[2, 0:1].partition_broadcast(P)).then_inc(ga_in, 16)
                sp.dma_start(gate[1][:], keep.gates[3, 0:1].partition_broadcast(P)).then_inc(gb_in, 16)
                with sp.Fori(1, B) as b:
                    sp.wait_ge(x3_step, 2 * b)
                    sp.dma_start(gate[0][:], keep.gates[2, bass.ds(b, 1)].partition_broadcast(P)).then_inc(ga_in, 16)
                    sp.wait_ge(b_step, 2 * b + 1)
                    sp.dma_start(gate[1][:], keep.gates[3, bass.ds(b, 1)].partition_broadcast(P)).then_inc(gb_in, 16)

            @block.gpsimd
            def _(pool):
                def add_base(b):
                    pool.wait_ge(gb_in, 16 * b + 16)
                    pool.wait_ge(b_out, b + 2)
                    nc.gpsimd.tensor_tensor(base[:], base[:], over_tiles(gate[1][:]), ALU.mult).then_inc(b_step, 1)
                    pool.wait_ge(b_step, 2 * b + 2)
                    x3 = element(keep.acc, b)
                    nc.gpsimd.tensor_tensor(x3, x3, base[:], ALU.add).then_inc(b_step, 1)

                pool.sem_inc(b_step, 1)
                with pool.Fori(0, B) as b:
                    add_base(b)

            @block.scalar
            def _(act):
                def fetch(b):
                    for t in range(TT):
                        nc.scalar.activation(o[:, t].rearrange("p (g c) -> p g c", g=8),
                                             keep.o1[:, bass.ds(b * 8, 8), t], ACT.Identity).then_inc(o_in, 1)

                def split_o(b):
                    act.wait_ge(o_turned, b + 1)
                    nc.scalar.activation(oh[0][:], norm.ps[:], ACT.Identity).then_inc(o_hi, 1)

                def split_h(b):
                    act.wait_ge(norm.ready, KT * b + KT)
                    nc.scalar.activation(hs[0][:], norm.ht[:], ACT.Identity).then_inc(h_hi, 1)

                def router_out(b):
                    act.wait_ge(r_done, b + 1)
                    nc.scalar.activation(element(logits, b), ps_r[:, :, 0:NR], ACT.Identity).then_inc(r_out, 1)
                    nc.scalar.activation(element(keep.mid1, b), ps_r[:, :, NR:], ACT.Identity).then_inc(r_out, 1)

                fetch(0)
                for n in range(2):
                    nc.scalar.activation(w[n][0][:], raw[n][:], ACT.Identity).then_inc(w_hi, 1)
                def step(b, turned):
                    if turned:
                        fetch(b + 2)
                    if turned:
                        split_o(b + 2)
                    norm.roots(act, b + 1)
                    router_out(b)
                    act.wait_ge(h_lo, b + 1)
                    norm.modulate(act, b + 1)
                    split_h(b + 1)

                split_o(0)
                fetch(1)
                nc.scalar.preload_act_table(ACT.Sqrt)
                norm.roots(act, 0)
                norm.modulate(act, 0)
                split_h(0)
                split_o(1)
                with act.Fori(0, B - 2) as b:
                    step(b, True)
                step(B - 2, False)
                router_out(B - 1)
                act.wait_ge(g_step, 4)
                nc.scalar.activation(e[:], e[:], ACT.Exp).then_inc(g_exp, 1)

            @block.vector
            def _(dve):
                def split_o(b):
                    dve.wait_ge(o_hi, b + 1)
                    nc.vector.tensor_tensor(oh[1][:], norm.ps[:], f32(oh[0][:]), ALU.subtract).then_inc(o_lo, 1)

                def add_y(b):
                    x3 = element(keep.acc, b)
                    dve.wait_ge(ga_in, 16 * b + 16)
                    dve.wait_ge(y_done, b + 1)
                    nc.vector.tensor_tensor(y[:], ps_y[:], over_tiles(gate[0][:]), ALU.mult).then_inc(x3_step, 1)
                    dve.wait_ge(x3_step, 2 * b + 1)
                    nc.vector.tensor_tensor(x3, x3, y[:], ALU.add).then_inc(x3_step, 1)

                def normalize(b):
                    dve.wait_ge(x3_step, 2 * b + 2)
                    norm.normalize(dve, element(keep.acc, b), b)

                def split_h(b):
                    dve.wait_ge(h_hi, b + 1)
                    nc.vector.tensor_tensor(hs[1][:], norm.ht[:], f32(hs[0][:]), ALU.subtract).then_inc(h_lo, 1)

                def base_out(b):
                    dve.wait_ge(b_done, b + 1)
                    dve.wait_ge(b_step, 2 * b + 1)
                    nc.vector.tensor_tensor(base[:], ps_b[:], over_tiles(bias[:]), ALU.add).then_inc(b_out, 1)

                dve.sem_inc(b_out, 1)
                for n in range(2):
                    dve.wait_ge(w_hi, n + 1)
                    nc.vector.tensor_tensor(w[n][1][:], raw[n][:], f32(w[n][0][:]), ALU.subtract).then_inc(w_lo, 1)
                dve.wait_ge(tab_in, 16 * 5)
                def rank_experts(b):
                    dve.wait_ge(r_out, 2 * b + 2)
                    x = element(logits, b)
                    nc.vector.tensor_tensor(x, x, over_tiles(rbias[:]), ALU.add).then_inc(rank_step, 1)
                    dve.wait_ge(rank_step, 7 * b + 1)
                    keep_best(nc, dve, rank_step, 7 * b + 1, x, cmp_a[:], cmp_b[:], element(rank, b), element(keepers, b),
                              earlier[:], LORA1_E)

                def step(b, turned, ranked):
                    add_y(b + 1)
                    if turned:
                        split_o(b + 2)
                    normalize(b + 1)
                    base_out(b)
                    if ranked:
                        rank_experts(b - 1)
                    split_h(b + 1)

                split_o(0)
                add_y(0)
                normalize(0)
                split_h(0)
                split_o(1)
                step(0, True, False)
                with dve.Fori(1, B - 2) as b:
                    step(b, True, True)
                step(B - 2, False, True)
                rank_experts(B - 2)
                base_out(B - 1)
                rank_experts(B - 1)

                v = nc.vector
                v.tensor_copy(emap[:], emap_i[:]).then_inc(g_step, 1)
                dve.wait_ge(g_step, 1)
                v.tensor_tensor(sel[:], emap[:].rearrange("p (o n) -> p o n", o=1).broadcast_to([P, E, NR]),
                                expert[:].rearrange("p (e n) -> p e n", e=E), ALU.is_equal).then_inc(g_step, 1)
                v.tensor_reduce(top[:], logits[:], AX, ALU.max).then_inc(g_step, 1)
                dve.wait_ge(g_step, 3)
                v.tensor_tensor(e[:], logits[:], top[:].rearrange("p (t o) -> p t o", o=1).broadcast_to([P, NT, NR]),
                                ALU.subtract).then_inc(g_step, 1)
                dve.wait_ge(g_exp, 1)
                v.tensor_reduce(total[:], e[:], AX, ALU.add).then_inc(g_step, 1)
                dve.wait_ge(g_step, 5)
                v.tensor_tensor(e[:], e[:], keepers[:], ALU.mult).then_inc(g_step, 1)
                v.reciprocal(total[:], total[:]).then_inc(g_step, 1)
                dve.wait_ge(g_step, 7)
                v.scalar_tensor_tensor(e[:], e[:], LORA1_SCALE, total[:].rearrange("p (t o) -> p t o", o=1).broadcast_to([P, NT, NR]),
                                       ALU.mult, ALU.mult).then_inc(g_step, 1)
                dve.wait_ge(g_step, 8)
                v.tensor_tensor(mixed[:], e[:].rearrange("p t (o n) -> p t o n", o=1).broadcast_to([P, NT, E, NR]),
                                sel[:].rearrange("p (o e) n -> p o e n", o=1).broadcast_to([P, NT, E, NR]),
                                ALU.mult).then_inc(g_step, 1)
                dve.wait_ge(g_step, 9)
                v.tensor_reduce(wexp[:], mixed[:], AX, ALU.add).then_inc(g_step, 1)
                dve.wait_ge(g_step, 10)
                m = keep.mid1[:].rearrange("p t (e r) -> p t e r", e=E)
                v.tensor_tensor(m, m, wexp[:].rearrange("p t (e o) -> p t e o", o=1).broadcast_to([P, NT, E, R]),
                                ALU.mult).then_inc(g_step, 1)

            @block.tensor
            def _(pe):
                def turn_o(b):
                    pe.wait_ge(o_in, 2 * b + 2)
                    for t in range(TT):
                        for k in range(KT):
                            mm = nc.tensor.transpose(norm.ps[:, k, t * P:(t + 1) * P], o[:, t, k * P:(k + 1) * P],
                                                     keep.ident[:])
                    mm.then_inc(o_turned, 1)

                def output(b):
                    pe.wait_ge(o_lo, b + 1)
                    for t in range(TT):
                        passes = [(a, r, k) for a, r in split_passes(oh, w[0]) for k in range(KT)]
                        for j, (a, r, k) in enumerate(passes):
                            mm = nc.tensor.matmul(ps_y[:, t], a[:, k, t * P:(t + 1) * P], r[:, k],
                                                  start=(j == 0), stop=(j == len(passes) - 1))
                    mm.then_inc(y_done, 1)

                def base_tile(b, t):
                    if t == 0:
                        pe.wait_ge(h_lo, b + 1)
                        pe.wait_ge(b_out, b + 1)
                    passes = [(a, r, k) for a, r in split_passes(hs, w[1]) for k in range(KT)]
                    for j, (a, r, k) in enumerate(passes):
                        mm = nc.tensor.matmul(ps_b[:, t], a[:, k, t * P:(t + 1) * P], r[:, k],
                                              start=(j == 0), stop=(j == len(passes) - 1))
                    if t:
                        mm.then_inc(b_done, 1)

                def router(b):
                    for t in range(TT):
                        for k in range(KT):
                            mm = nc.tensor.matmul(ps_r[:, t], norm.ht[:, k, t * P:(t + 1) * P], rl[:, k],
                                                  start=(k == 0), stop=(k == KT - 1))
                    mm.then_inc(r_done, 1)

                def step(b, turned):
                    output(b + 1)
                    if turned:
                        pe.wait_ge(norm.ready, KT * b + KT)
                        turn_o(b + 2)
                    for t in range(TT):
                        base_tile(b, t)
                    router(b)
                    if turned:
                        pe.wait_ge(o_lo, b + 3)
                    norm.transposes(pe, b + 1)
                    pe.wait_ge(r_out, 2 * b + 2)

                norm.start(pe)
                turn_o(0)
                pe.wait_ge(w_lo, 1)
                output(0)
                norm.transposes(pe, 0)
                pe.wait_ge(norm.ready, KT)
                turn_o(1)
                pe.wait_ge(w_lo, 2)
                pe.wait_ge(tab_in, 16 * 5)
                with pe.Fori(0, B - 2) as b:
                    step(b, True)
                step(B - 2, False)
                for t in range(TT):
                    base_tile(B - 1, t)
                router(B - 1)


def phase_finish(nc, io, keep, out):
    with ExitStack() as ctx:
        def sb(name, shape, dt=F32):
            return ctx.enter_context(nc.sbuf_tensor(name, shape, dt))

        def sem(name):
            return ctx.enter_context(nc.semaphore(name))

        ER = LORA1_E * LORA1_R
        gates = sb("h_gates", [P, B, D])
        b1 = sb("h_b1", [ER, D])
        bs = [sb(f"h_bs{i}", [ER, D], F32R) for i in range(2)]
        mid = sb("h_mid", [P, TT, ER])
        ms = [sb(f"h_ms{i}", [ER, S], F32R) for i in range(2)]
        gated = [sb(f"h_gated{n}", [P, TT, D]) for n in range(2)]
        ps_m = [ctx.enter_context(nc.psum_tensor(f"h_ps_m{n}", [ER, S], F32)) for n in range(2)]
        ps_l = [ctx.enter_context(nc.psum_tensor(f"h_ps_l{n}", [P, TT, D], F32)) for n in range(2)]

        g_in = sem("h_g_in")
        b_in = sem("h_b_in")
        b_hi = sem("h_b_hi")
        b_lo = sem("h_b_lo")
        mid_in = sem("h_mid_in")
        m_done = sem("h_m_done")
        m_hi = sem("h_m_hi")
        m_lo = sem("h_m_lo")
        l_done = sem("h_l_done")
        l_gated = sem("h_l_gated")
        summed = sem("h_summed")
        stored = sem("h_stored")

        with nc.Block() as block:
            @block.sync
            def _(sp):
                sp.dma_start(b1[:], io["b1"]).then_inc(b_in, 16)
                for b in range(B):
                    sp.dma_start(gates[:, b], keep.gates[3, b:b + 1].partition_broadcast(P)).then_inc(g_in, 16)
                with sp.Fori(0, B) as b:
                    sp.wait_ge(summed, b + 3)
                    sp.dma_start(out[bass.ds(b, 1)].rearrange("o p t d -> p (o t) d"), element(keep.acc, b)).then_inc(stored, 16)
                sp.wait_ge(stored, 16 * B)

            @block.scalar
            def _(act):
                def fetch(b):
                    nc.scalar.activation(mid[:], element(keep.mid1, b), ACT.Identity).then_inc(mid_in, 1)

                def split(b, slot):
                    act.wait_ge(m_done, b + 1)
                    nc.scalar.activation(ms[0][:], ps_m[slot][:], ACT.Identity).then_inc(m_hi, 1)

                fetch(0)
                act.wait_ge(b_in, 16)
                nc.scalar.activation(bs[0][:], b1[:], ACT.Identity).then_inc(b_hi, 1)
                split(0, 0)
                fetch(1)

                def step(b, slot, more):
                    act.wait_ge(l_done, b + 1)
                    split(b + 1, 1 - slot)
                    if more:
                        fetch(b + 2)

                with act.Fori(0, B // 2 - 1) as n:
                    for slot in range(2):
                        step(2 * n + slot, slot, True)
                step(B - 2, 0, False)

            @block.vector
            def _(dve):
                def split(b, slot):
                    dve.wait_ge(m_hi, b + 1)
                    nc.vector.tensor_tensor(ms[1][:], ps_m[slot][:], f32(ms[0][:]), ALU.subtract).then_inc(m_lo, 1)

                def gate(b, slot):
                    dve.wait_ge(l_done, b + 1)
                    dve.wait_ge(summed, b + 1)
                    g = gates[:, bass.ds(b, 1)].broadcast_to([P, TT, D])
                    nc.vector.tensor_tensor(gated[slot][:], ps_l[slot][:], g, ALU.mult).then_inc(l_gated, 1)

                dve.sem_inc(l_gated, 2)
                dve.wait_ge(b_hi, 1)
                nc.vector.tensor_tensor(bs[1][:], b1[:], f32(bs[0][:]), ALU.subtract).then_inc(b_lo, 1)
                split(0, 0)
                dve.wait_ge(g_in, 16 * B)
                with dve.Fori(0, B // 2 - 1) as n:
                    for slot in range(2):
                        b = 2 * n + slot
                        split(b + 1, 1 - slot)
                        gate(b, slot)
                split(B - 1, 1)
                gate(B - 2, 0)
                gate(B - 1, 1)

            @block.gpsimd
            def _(pool):
                pool.sem_inc(summed, 2)
                with pool.Fori(0, B // 2) as n:
                    for slot in range(2):
                        b = 2 * n + slot
                        pool.wait_ge(l_gated, b + 3)
                        x = element(keep.acc, b)
                        nc.gpsimd.tensor_tensor(x, x, gated[slot][:], ALU.add).then_inc(summed, 1)

            @block.tensor
            def _(pe):
                def turn(b, slot):
                    pe.wait_ge(mid_in, b + 1)
                    for t in range(TT):
                        mm = nc.tensor.transpose(ps_m[slot][:, t * P:(t + 1) * P], mid[:, t], keep.ident[:])
                    mm.then_inc(m_done, 1)

                def lora(b, slot):
                    pe.wait_ge(m_lo, b + 1)
                    pe.wait_ge(l_gated, b + 1)
                    for t in range(TT):
                        for j, (a, r) in enumerate(split_passes(ms, bs)):
                            mm = nc.tensor.matmul(ps_l[slot][:, t], a[:, t * P:(t + 1) * P], r[:], start=(j == 0), stop=(j == 2))
                    mm.then_inc(l_done, 1)

                turn(0, 0)
                pe.wait_ge(b_lo, 1)
                with pe.Fori(0, B // 2 - 1) as n:
                    for slot in range(2):
                        b = 2 * n + slot
                        turn(b + 1, 1 - slot)
                        lora(b, slot)
                turn(B - 1, 1)
                lora(B - 2, 0)
                lora(B - 1, 1)


def build(nc, io, out):
    with ExitStack() as ctx:
        def sb(name, shape, dt=F32):
            return ctx.enter_context(nc.sbuf_tensor(name, shape, dt))

        def right(stack, name, shape):
            return stack.enter_context(nc.sbuf_tensor(name, shape, F32, side="right"))

        def scratch(name, shape, dt=F32):
            return nc.dram_tensor(name, shape, dt, kind="Internal").ap()

        k_parts = [scratch(f"k{i}_dram", [G0 * B, P, S]) for i in range(2)]
        v_parts = [scratch(f"v{i}_dram", [G0 * B, P, TT, HD0]) for i in range(2)]
        keep = Kept()
        keep.gates = scratch("gates", [4, B, D])
        keep.v1_dram = scratch("values1_dram", [P, 8 * B, TT, D // 8])
        keep.k, keep.v = k_parts, v_parts
        keep.k_by_element = [t.rearrange("(g b) p s -> b p g s", b=B) for t in k_parts]
        keep.v_by_element = [t.rearrange("(g b) p t c -> b p t g c", b=B) for t in v_parts]
        keep.mod = sb("mod", [P, 2, 4, KT, B])
        keep.ident, keep.eps = sb("ident", [P, P]), sb("eps", [P, 1])
        keep.ident_b, keep.mask_b = sb("ident_b", [P, P], BF16), sb("mask_b", [P, P], BF16)
        keep.qcos, keep.qsin = (sb(name, [P, S]) for name in ("qcos", "qsin"))
        mask = sb("mask", [P, P])
        table_in = ctx.enter_context(nc.semaphore("table_in"))
        with nc.Block() as block:
            @block.sync
            def _(sp):
                sp.dma_start(keep.ident[:], io["ident"]).then_inc(table_in, 16)
                sp.dma_start(mask[:], io["mask"]).then_inc(table_in, 16)
                sp.dma_start(keep.qcos[:], io["qcos"]).then_inc(table_in, 16)
                sp.dma_start(keep.qsin[:], io["qsin"]).then_inc(table_in, 16)

            @block.vector
            def _(dve):
                nc.vector.memset(keep.eps[:], EPS)
                dve.wait_ge(table_in, 64)
                nc.vector.tensor_copy(keep.ident_b[:], keep.ident[:])
                nc.vector.tensor_copy(keep.mask_b[:], mask[:])


        with ExitStack() as tokens:
            keep.tokens_at = -(-nc.sbuf_base // 32) * 32
            keep.ht_hi, keep.ht_lo = (tokens.enter_context(nc.sbuf_tensor(name, [P, B, KT, S], F32R)) for name in ("ht_hi", "ht_lo"))
            with ExitStack() as split_weights:
                keep.wk_hi, keep.wk_lo, keep.wv_hi, keep.wv_lo = (
                    split_weights.enter_context(nc.sbuf_tensor(name, [P, KT, 2 * D], F32R))
                    for name in ("wk_hi", "wk_lo", "wv_hi", "wv_lo"))
                phase_setup(nc, io, keep)
                phase_keys(nc, io, keep)
            keep.acc = right(ctx, "x_stream", [P, NT, D])
            phase_attention0(nc, io, keep)
        keep.mid0 = right(ctx, "mid0", [P, NT, LORA0_E * LORA0_R])
        with ExitStack() as heads:
            keep.q1, keep.k1 = (heads.enter_context(nc.sbuf_tensor(n, [P, 8 * B, TT, D // 8], F32)) for n in ("queries1", "keys1"))
            with ExitStack() as projections:
                keep.qkv_w = [[projections.enter_context(nc.sbuf_tensor(f"qkv_w{n}{i}", [P, KT, D], F32R)) for i in range(2)]
                              for n in range(3)]
                phase_router0(nc, io, keep)
                phase_queries1(nc, io, keep)
            keep.g_raw = [right(ctx, f"g_raw{n}", [P, KT, D]) for n in range(2)]
            keep.g_rl = right(ctx, "g_rl", [P, KT, NR + LORA1_E * LORA1_R])
            keep.o1 = right(ctx, "o1", [P, 8 * B, TT, D // 8])
            phase_attention1(nc, io, keep)
        keep.mid1 = right(ctx, "mid1", [P, NT, LORA1_E * LORA1_R])
        phase_router1(nc, io, keep)
        phase_finish(nc, io, keep, out)


def tables():
    q = np.arange(P)
    mask = np.where(q[None, :] > q[:, None], NEG, 0.0).astype(np.float32)
    inv = 1.0 / THETA ** (np.arange(0, HD0, 2, dtype=np.float32) / HD0)
    angle = np.outer(np.arange(S, dtype=np.float32), inv).T
    cos, sin = np.cos(angle), np.sin(angle)
    half = np.concatenate([cos, cos]), np.concatenate([sin, -sin])
    rotated = (np.arange(P) % HB0 < ROPE0)[:, None]
    inv1 = 1.0 / THETA ** (np.arange(0, HD1, 2, dtype=np.float32) / HD1)
    angle1 = np.outer(np.arange(S, dtype=np.float32), inv1)
    cos1 = np.concatenate([np.cos(angle1)] * 2, 1).reshape(TT, P, HD1).transpose(1, 0, 2)
    sin1 = np.concatenate([-np.sin(angle1), np.sin(angle1)], 1).reshape(TT, P, HD1).transpose(1, 0, 2)

    def earlier(n):
        return np.tile(np.tril(np.ones((n, n), np.float32), -1).reshape(1, -1), (P, 1))

    return {
        "cos1": cos1.astype(np.float32), "sin1": sin1.astype(np.float32),
        "earlier0": earlier(LORA0_E), "earlier1": earlier(NR),
        "expert": np.tile(np.repeat(np.arange(LORA1_E, dtype=np.float32), NR)[None], (P, 1)),
        "ident": np.eye(P, dtype=np.float32), "mask": mask,
        "qcos": half[0].astype(np.float32), "qsin": half[1].astype(np.float32),
        "kcos": np.where(rotated, half[0], 1.0).astype(np.float32),
        "ksin": np.where(rotated, half[1], 0.0).astype(np.float32),
    }


def by_partition(w):
    w = np.asarray(w)
    return np.ascontiguousarray(w.reshape(-1, P, w.shape[-1]).transpose(1, 0, 2))


def layouts(a):
    wq = np.asarray(a["L0_attn_Wq"]).T.reshape(KT, P, G0, 2, D // 2)
    wo = np.asarray(a["L0_attn_Wo"]).T.reshape(G0, HG, P, 2, D // 2)
    m = {
        "x": np.asarray(a["L0_attn_hidden_states"]),
        "c0": by_partition(np.asarray(a["L0_c"]).T), "c1": by_partition(np.asarray(a["L1_c"]).T),
        "wmod0": by_partition(a["L0_wmod"]), "wmod1": by_partition(a["L1_wmod"]),
        "wdk": by_partition(a["L0_attn_Wdk"]),
        "wupk": by_partition(np.asarray(a["L0_attn_Wupk"]).T),
        "wupv": by_partition(np.asarray(a["L0_attn_Wupv"]).T),
        "wkr": by_partition(np.asarray(a["L0_attn_Wkr"]).T),
        "wq_pieces": np.ascontiguousarray(wq.transpose(2, 0, 3, 1, 4)).reshape(G0 * B, P, D // 2),
        "wo_pieces": np.ascontiguousarray(wo.transpose(0, 1, 3, 2, 4)).reshape(G0 * B, P, D // 2),
    }
    order = np.arange(D).reshape(H1, HD1 // 2, 2).transpose(0, 2, 1).reshape(-1)
    m.update({
        "router0": by_partition(np.asarray(a["L0_ffn_router_w"]).T),
        "a0": by_partition(np.asarray(a["L0_ffn_A"]).reshape(-1, D).T),
        "b0": np.asarray(a["L0_ffn_B"]).transpose(0, 2, 1).reshape(-1, D),
        "wq1": by_partition(np.asarray(a["L1_attn_wq"])[:, order]),
        "wk1": by_partition(np.asarray(a["L1_attn_wk"])[:, order]),
        "wv1": by_partition(a["L1_attn_wv"]), "wo1": by_partition(a["L1_attn_wo"]),
        "base_w": by_partition(np.asarray(a["L1_ffn_base_W"]).T),
        "base_b": np.asarray(a["L1_ffn_base_b"]).reshape(1, -1),
        "router1": by_partition(np.asarray(a["L1_ffn_router_W"]).T),
        "router_b": np.asarray(a["L1_ffn_router_b"]).reshape(1, -1),
        "a1": by_partition(np.asarray(a["L1_ffn_A"]).reshape(-1, D).T),
        "b1": np.asarray(a["L1_ffn_B"]).transpose(0, 2, 1).reshape(-1, D),
        "expert_map": np.asarray(a["L1_ffn_expert_map"]).reshape(1, -1),
    })
    m.update(tables())
    return {k: np.ascontiguousarray(v) for k, v in m.items()}


def kernel(**inputs):
    import concourse.bacc as bacc
    from concourse.bass_utils import run_bass_kernel_spmd

    nc = bacc.Bacc("TRN2", target_bir_lowering=False, num_devices=1)
    arrays = layouts(inputs)
    io = {k: nc.dram_tensor(f"in_{k}", v.shape, mybir.dt.from_np(v.dtype), kind="ExternalInput").ap()
          for k, v in arrays.items()}
    io["x"] = io["x"].rearrange("b (t p) d -> b p t d", p=P)
    io["wmod"] = [io["wmod0"], io["wmod1"]]
    out = nc.dram_tensor("out_x", [B * S, D], F32, kind="ExternalOutput").ap()
    build(nc, io, out.rearrange("(b t p) d -> b p t d", p=P, t=TT))
    result = run_bass_kernel_spmd(nc, [{f"in_{k}": v for k, v in arrays.items()}], core_ids=[0])
    return result.results[0]["out_x"].reshape(B, S, D)
```
